# Optimizing a Trainium2 kernel written in Bass

```python
import numpy as np
import jax
import jax.numpy as jnp

def _softmax(x, axis=-1):
    return jax.nn.softmax(x, axis=axis)

def _gelu(x):
    return jax.nn.gelu(x, approximate=True)

def _silu(x):
    return jax.nn.silu(x)

def _sigmoid(x):
    return jax.nn.sigmoid(x)

def _layernorm(x, axis=-1, eps=1e-05):
    m = jnp.mean(x, axis=axis, keepdims=True)
    v = jnp.var(x, axis=axis, keepdims=True)
    return (x - m) / jnp.sqrt(v + eps)

def _scatter_add(tgt, idx, src, axis=0):
    return tgt.at[idx].add(src)

def _segment_sum(src, seg, n):
    return jax.ops.segment_sum(src, seg, n)
kernel_name = 'mk_gnn_ffn_d1_gnn_r32_bd2e38'

def setup_inputs(seed: int=0):
    np.random.seed(seed)
    _w = jnp.asarray

    def _rec_inputs():
        import jax
        import jax.numpy as jnp
        _gk = jax.random.key(seed)
        x = -0.0002117 + 1 * jax.random.normal(jax.random.fold_in(_gk, 1), (3125, 256), jnp.float32)
        _s = jax.random.randint(jax.random.fold_in(_gk, 2), (25000,), 0, 3125, jnp.int32)
        _d = jax.random.randint(jax.random.fold_in(_gk, 3), (25000,), 0, 3125, jnp.int32)
        _loop = jnp.arange(3125, dtype=jnp.int32)
        src = jnp.concatenate([_s, _d, _loop])
        dst = jnp.concatenate([_d, _s, _loop])
        _o = jnp.argsort(dst, stable=True)
        src = src[_o]
        dst = dst[_o]
        return (x, src, dst)
    x, src, dst = _rec_inputs()

    def _L0_gnn_setup():
        import jax, jax.numpy as jnp
        import numpy as np
        N_NODES = 3125
        N_EDGES = 100000
        D = 256
        key = jax.random.key(seed)
        ks = jax.random.split(key, 6)
        x = jax.random.normal(ks[0], (N_NODES, D), dtype=jnp.float32)
        edge_src = jax.random.randint(ks[1], (N_EDGES,), 0, N_NODES, dtype=jnp.int32)
        edge_dst = jax.random.randint(ks[2], (N_EDGES,), 0, N_NODES, dtype=jnp.int32)
        w = jnp.ones((1,), dtype=jnp.float32) * 3.0
        W1 = jax.random.normal(ks[3], (64, D), dtype=jnp.float32) * 0.05
        W2 = jax.random.normal(ks[4], (32, 64), dtype=jnp.float32) * 0.1
        W3 = jax.random.normal(ks[5], (D, 32), dtype=jnp.float32) * 0.1
        return {'x': x, 'edge_src': edge_src, 'edge_dst': edge_dst, 'w': w, 'W1': W1, 'W2': W2, 'W3': W3}
    _L0_gnn_all = _L0_gnn_setup()
    _L0_gnn_in = {k: v for k, v in _L0_gnn_all.items() if k in ('w', 'W1', 'W2', 'W3')}
    del _L0_gnn_all

    def _L0_ffn_setup():
        import jax, jax.numpy as jnp
        import numpy as np
        E = 8
        K = 2
        D = 256
        H = 512
        DOUT = 256
        EPS = 1e-05
        key = jax.random.key(seed)
        ks = jax.random.split(key, 9)
        s = 0.02
        return {'x': jax.random.normal(ks[0], (4, 256, D), jnp.float32), 'gamma': 1.0 + 0.05 * jax.random.normal(ks[1], (D,), jnp.float32), 'beta': 0.05 * jax.random.normal(ks[2], (D,), jnp.float32), 'Wr': 0.01 * jax.random.normal(ks[3], (D, E), jnp.float32), 'br': jnp.zeros((E,), jnp.float32), 'W1': s * jax.random.normal(ks[4], (E, D, H), jnp.float32), 'b1': s * jax.random.normal(ks[5], (E, H), jnp.float32), 'W2': s * jax.random.normal(ks[6], (E, H, DOUT), jnp.float32), 'b2': s * jax.random.normal(ks[7], (E, DOUT), jnp.float32)}
    _L0_ffn_all = _L0_ffn_setup()
    _L0_ffn_in = {k: v for k, v in _L0_ffn_all.items() if k in ('gamma', 'beta', 'Wr', 'br', 'W1', 'b1', 'W2', 'b2')}
    del _L0_ffn_all
    return {'x': x, 'src': src, 'dst': dst, 'L0_gnn_w': _L0_gnn_in['w'], 'L0_gnn_W1': _L0_gnn_in['W1'], 'L0_gnn_W2': _L0_gnn_in['W2'], 'L0_gnn_W3': _L0_gnn_in['W3'], 'L0_ffn_gamma': _L0_ffn_in['gamma'], 'L0_ffn_beta': _L0_ffn_in['beta'], 'L0_ffn_Wr': _L0_ffn_in['Wr'], 'L0_ffn_br': _L0_ffn_in['br'], 'L0_ffn_W1': _L0_ffn_in['W1'], 'L0_ffn_b1': _L0_ffn_in['b1'], 'L0_ffn_W2': _L0_ffn_in['W2'], 'L0_ffn_b2': _L0_ffn_in['b2']}

def reference(x, src, dst, L0_gnn_w, L0_gnn_W1, L0_gnn_W2, L0_gnn_W3, L0_ffn_gamma, L0_ffn_beta, L0_ffn_Wr, L0_ffn_br, L0_ffn_W1, L0_ffn_b1, L0_ffn_W2, L0_ffn_b2):
    import jax
    import jax.numpy as jnp

    def _L0_gnn_ref(x, edge_src, edge_dst, w, W1, W2, W3):
        import jax, jax.numpy as jnp
        import numpy as np
        N_NODES = 3125
        N_EDGES = 100000
        D = 256
        agg = jax.ops.segment_sum(x[edge_dst], edge_src, num_segments=N_NODES)
        y = agg + w * x
        h = jax.nn.relu(jnp.einsum('nd,hd->nh', y, W1))
        h = jax.nn.relu(jnp.einsum('nh,gh->ng', h, W2))
        h = jax.nn.relu(jnp.einsum('ng,og->no', h, W3))
        return h + x

    def _L0_ffn_ref(x, gamma, beta, Wr, br, W1, b1, W2, b2):
        import jax, jax.numpy as jnp
        import numpy as np
        E = 8
        K = 2
        D = 256
        H = 512
        DOUT = 256
        EPS = 1e-05
        mu = jnp.mean(x, axis=-1, keepdims=True)
        var = jnp.mean(jnp.square(x - mu), axis=-1, keepdims=True)
        xn = (x - mu) * jax.lax.rsqrt(var + EPS) * gamma + beta
        logits = jnp.einsum('bsd,de->bse', xn, Wr) + br
        top_vals, top_idx = jax.lax.top_k(logits, K)
        w = jax.nn.softmax(top_vals, axis=-1)
        w_full = jnp.einsum('bsk,bske->bse', w, jax.nn.one_hot(top_idx, E, dtype=w.dtype))
        y = jnp.zeros(x.shape[:-1] + (DOUT,), x.dtype)
        for e in range(E):
            h = jax.nn.gelu(jnp.einsum('bsd,dh->bsh', xn, W1[e]) + b1[e], approximate=False)
            y_e = jnp.einsum('bsh,hd->bsd', h, W2[e]) + b2[e]
            y = y + y_e * w_full[..., e, None]
        return y
    x = x + _L0_gnn_ref(_layernorm(x, axis=-1), src, dst, L0_gnn_w, L0_gnn_W1, L0_gnn_W2, L0_gnn_W3)
    x = x + _L0_ffn_ref(_layernorm(x, axis=-1)[None], L0_ffn_gamma, L0_ffn_beta, L0_ffn_Wr, L0_ffn_br, L0_ffn_W1, L0_ffn_b1, L0_ffn_W2, L0_ffn_b2)[0]
    return x

_drawn_inputs = setup_inputs


def setup_inputs(seed=0):
    import zlib

    import numpy as np

    out = dict(_drawn_inputs(seed))
    spreads = {'L0_ffn_br': (0.0, 0.312)}
    factors = {'L0_ffn_gamma': 8.0,
     'L0_ffn_beta': 8.0,
     'L0_ffn_Wr': 3.117,
     'L0_ffn_b1': 22.076,
     'L0_ffn_b2': 8.0}
    for name, (base, spread) in spreads.items():
        noise = np.random.default_rng([zlib.crc32(name.encode()), seed]).standard_normal(out[name].shape)
        drawn = base * np.exp(spread * noise) if base else spread * noise
        out[name] = jnp.asarray(drawn.astype(out[name].dtype))
    for name, factor in factors.items():
        out[name] = (out[name] * factor).astype(out[name].dtype)
    return out
```

```python
from contextlib import ExitStack

import concourse.bass as bass
from concourse import mybir
from concourse.alu_op_type import AluOpType as ALU

F32 = mybir.dt.float32
BF16 = mybir.dt.bfloat16
F16 = mybir.dt.float16
I32 = mybir.dt.int32
ACT = mybir.ActivationFunctionType
AX = mybir.AxisListType

P = 128
N = 3125
E = 53125
D = 256
T = 125
NT = N // T
G = 5
NG = NT // G
F1, F2 = 64, 32
EC = E // T
WD = 18
NQ = 7
NW = NT * NQ
NWX = 176
WG = (P, NWX - P)
STEPS = 3
CH = STEPS * P
WC = WD * NT
NX = 8
H = 512
KD, KH = D // P, H // P
NB = (2 * N + NX * (P - 1)) // P
EPS = 1e-5
MAGIC = 12582912.0
BIG = 3.0e38


def build(nc, x, src, dst, gnn_w, gW1, gW2, gW3, gamma, beta, Wr, br, W1, b1, W2, b2, out):
    ctx = ExitStack()
    with ctx:
        def sb(name, shape, dt, where=ctx):
            return where.enter_context(nc.sbuf_tensor(name, shape, dt))

        def sem(name):
            return ctx.enter_context(nc.semaphore(name))

        def ds(start, size):
            return bass.DynSlice(start, size)

        key_dram = nc.dram_tensor("edge_key", [E + CH], F32, kind="Internal").ap()
        lo_dram = nc.dram_tensor("edge_lo", [E + CH], F32, kind="Internal").ap()
        tok_dram = nc.dram_tensor("token_rows", [N, D], F32, kind="Internal").ap()
        pair_dram = nc.dram_tensor("pair_rows", [2 * N + NB * P, D], F32, kind="Internal").ap()

        res = sb("res", [T, NT, D], F32)
        z = sb("z", [T, NT, F1], F32)
        w1_sb = sb("w1_sb", [P, NX, KD, H], F32)
        w2_sb = sb("w2_sb", [P, NX, KH, D], F32)
        ident = sb("ident", [P, P], F32)
        ident16 = sb("ident16", [P, P], F16)
        iota = sb("iota", [P, WC], F16)
        part = sb("part", [P, 1], F32)
        later = sb("later", [P, P], BF16)
        ones16 = sb("ones16", [P, P], BF16)
        ones = sb("ones", [P, P], F32)
        eps = sb("eps", [P, 1], F32)
        zeros16 = sb("zeros16", [1, 512], BF16)
        gW1T = sb("gW1T", [P, KD, F1], F32)
        gW2T = sb("gW2T", [F1, F2], F32)
        gW3T = sb("gW3T", [F2, D], F32)
        wr_sb = sb("wr_sb", [P, KD, NX], F32)
        w_sb = sb("w_sb", [P, 1], F32)
        tile1 = sb("tile1", [T, NT], F32)
        ex_m8 = sb("ex_m8", [T, NT, NX], F32)
        logit = sb("logit", [T, NT, NX], F32)
        wgt = sb("wgt", [T, NT, 2], F32)
        rounds_f = sb("rounds_f", [1, 4], F32)
        rounds_i = sb("rounds_i", [1, 1], I32)

        psum = ctx.enter_context(nc.psum_tensor("psum", [P, 8, 512], F32))
        acc = psum[:, 0:4, :].rearrange("p b c -> p (b c)")

        L = {n: sem("load_" + n) for n in ("edges", "nextrow", "small", "bcast", "x", "experts", "rows")}
        c_pool, c_dve, c_pe = sem("const_pool"), sem("const_dve"), sem("const_pe")
        c_act = sem("const_act")
        link_dve, link_round, link_late = sem("link_dve"), sem("link_round"), sem("link_late")
        link_split, link_affine = sem("link_split"), sem("link_affine")
        key_stored, thr_ready = sem("key_stored"), sem("thr_ready")
        e_dve, e_pe, row_got = sem("e_dve"), sem("e_pe"), sem("row_got")
        idx_ready, got_key = sem("idx_ready"), sem("got_key")
        rounds_ready = sem("rounds_ready")
        xn_ready, var_ready, std_ready = sem("xn_ready"), sem("var_ready"), sem("std_ready")
        xnT_psum, xnT_sb, z_psum, z_sb = sem("xnT_psum"), sem("xnT_sb"), sem("z_psum"), sem("z_sb")
        res_ready, zsplit = sem("res_ready"), sem("zsplit")
        key_rel, keyT_psum, keyT_sb = sem("key_rel"), sem("keyT_psum"), sem("keyT_sb")
        onehots, win_psum, win_sb = sem("onehots"), sem("win_psum"), sem("win_sb")
        at_psum, at_dve, at_act, applied = sem("at_psum"), sem("at_dve"), sem("at_act"), sem("applied")
        y_ready, yT_psum, yT_sb = sem("y_ready"), sem("yT_psum"), sem("yT_sb")
        h2_psum, h2_sb, h3_psum = sem("h2_psum"), sem("h2_sb"), sem("h3_psum")
        var2, std2, tok_norm, tok_ready = sem("var2"), sem("std2"), sem("tok_norm"), sem("tok_ready")
        tok_stored, tokT_psum, tokT_sb = sem("tok_stored"), sem("tokT_psum"), sem("tokT_sb")
        logit_psum, logit_sb = sem("logit_psum"), sem("logit_sb")
        r_dve, r_pe, r_act = sem("r_dve"), sem("r_pe"), sem("r_act")
        pair_oh, pair_mm = sem("pair_oh"), sem("pair_mm")
        slots_ready, gcol_ready, scol_ready = sem("slots_ready"), sem("gcol_ready"), sem("scol_ready")
        xg_in = [sem(f"xg_in{i}") for i in range(4)]
        xgT_psum, xgT_sb, up_psum, up_sb = sem("xgT_psum"), sem("xgT_sb"), sem("up_psum"), sem("up_sb")
        gelu_sb, hT_psum, hT_sb = sem("gelu_sb"), sem("hT_psum"), sem("hT_sb")
        down_psum, down_sb = sem("down_psum"), sem("down_sb")
        scattered = [sem(f"scattered{i}") for i in range(4)]
        fin_in = [sem(f"fin_in{i}") for i in range(5)]
        fin_half, fin_done, out_stored = sem("fin_half"), sem("fin_done"), sem("out_stored")

        early = ExitStack()
        edge_i = sb("edge_i", [T, 2, EC], I32, early)
        next_i = sb("next_i", [T, 1], I32, early)
        edge_f = sb("edge_f", [T, 2, EC], F32, early)
        next_f = sb("next_f", [T, 1], F32, early)
        hi_f = sb("hi_f", [T, EC], F32, early)
        lo_f = sb("lo_f", [T, EC], F32, early)
        key_f = sb("key_f", [T, EC], F32, early)
        inv = sb("inv", [T, 3], F32, early)
        pad = sb("pad", [1, CH], F32, early)
        thr_row = sb("thr_row", [1, 26 * NQ], F32, early)
        thr = sb("thr", [P, 2], F32, early)
        cnt = sb("cnt", [P, 2, 4], F32, early)
        row_i = sb("row_i", [P, 2], I32, early)
        rows = sb("rows", [P, 2, EC], F32, early)
        junk = sb("junk", [P, EC], F32, early)
        flag = sb("flag", [P, 2], F32, early)
        start_f = sb("start_f", [P, 2], F32, early)
        start_i = sb("start_i", [P, 2], I32, early)
        start_row = sb("start_row", [1, NWX], F32, early)
        size_row = sb("size_row", [1, NW], F32, early)
        gath = sb("gath", [P, 2, 2, CH], F32, early)
        keyT = sb("keyT", [P, 2, STEPS, NWX], F32, early)
        xn = sb("xn", [T, G, D], F32, early)
        stats = sb("stats", [T, G, 6], F32, early)
        mv = sb("mv", [T, G, 2], F32, early)
        std = sb("std", [T, G], F32, early)
        rstd = sb("rstd", [T, G], F32, early)
        xnT = sb("xnT", [P, G, KD, T], F32, early)
        zres = sb("zres", [T, G, F1], F32, early)
        z3 = sb("z3", [T, NT, 3, F1], BF16, early)
        gW1_sb = sb("gW1_sb", [F1, D], F32, early)
        gW2_sb = sb("gW2_sb", [F2, F1], F32, early)
        gW3_sb = sb("gW3_sb", [P, 2, F2], F32, early)
        oh_col = sb("oh_col", [P, NQ, STEPS, WC], F16, early)
        oh_lo = sb("oh_lo", [P, NQ, STEPS, P], F16, early)
        cts = sb("cts", [P, 2, NT, T], F16, early)
        at = sb("at", [T, G, G * P], F16, early)
        early.close()

        lt = ExitStack()
        b1_sb = sb("b1_sb", [P, NX, H], F32, lt)
        b2_sb = sb("b2_sb", [P, NX, D], F32, lt)
        y1 = sb("y1", [T, G, F1], F32, lt)
        y1T = sb("y1T", [F1, G, T], F32, lt)
        h2T = sb("h2T", [F2, G, T], F32, lt)
        gam = sb("gam", [T, D], F32, lt)
        bet = sb("bet", [T, D], F32, lt)
        br_sb = sb("br_sb", [T, NX], F32, lt)
        stats2 = sb("stats2", [T, G, 6], F32, lt)
        mv2 = sb("mv2", [T, G, 2], F32, lt)
        std_2 = sb("std_2", [T, G], F32, lt)
        rstd2 = sb("rstd2", [T, G], F32, lt)
        tok = sb("tok", [T, G, D], F32, lt)
        tokT = sb("tokT", [P, G, KD, T], F32, lt)
        rt = [sb(f"rt{i}", [T, NT, NX], F32, lt) for i in range(4)]
        mask = sb("mask", [T, 2, NT, NX], F32, lt)
        sel = sb("sel", [T, NT, NX], BF16, lt)
        top = sb("top", [T, 4, NT], F32, lt)
        tot = sb("tot", [P, NX, NT], F32, lt)
        blk = sb("blk", [P, 4, NX], F32, lt)
        pos = sb("pos", [T, 2, NT], F32, lt)
        pblk = sb("pblk", [T, 2, NT], F32, lt)
        plane = sb("plane", [T, 2, NT], F32, lt)
        pairno = sb("pairno", [T, 2], F32, lt)
        oh_lane = sb("oh_lane", [T, 2 * G, P], BF16, lt)
        oh_blk = sb("oh_blk", [T, 2 * G, 2, NB], BF16, lt)
        slot = sb("slot", [P, 6, NB], F32, lt)
        thr2 = sb("thr2", [P, 1], F32, lt)
        gidx = sb("gidx", [P, NB], I32, lt)
        sidx = sb("sidx", [P, NB], I32, lt)
        gcol = sb("gcol", [P, 4], I32, lt)
        scol = sb("scol", [P, 4], I32, lt)
        ebt = sb("ebt", [1, NB, NX], F32, lt)
        ebf = sb("ebf", [1, NB], F32, lt)
        ebi = sb("ebi", [1, NB], I32, lt)
        xg = sb("xg", [P, 4, D], F32, lt)
        xgT = sb("xgT", [P, 2, KD, P], F32, lt)
        up = sb("up", [P, 2, H], F32, lt)
        hg = sb("hg", [P, 2, H], F32, lt)
        hT = sb("hT", [P, 2, KH, P], F32, lt)
        yb = sb("yb", [P, 4, D], F32, lt)
        fin = sb("fin", [T, 5, 2, D], F32, lt)
        lt.close()

        def chain(eng, s):
            st = {"base": 0, "n": 0}

            def done(ins):
                st["n"] += 1
                ins.then_inc(s, 1)

            def settle():
                eng.wait_ge(s, st["base"] + st["n"])

            def start(base):
                st["base"], st["n"] = base, 0

            return done, settle, start, st

        AT_DVE = (1, 3)
        AT_ACT = (0, 2, 4)
        SET = 5

        def at_count(r, kt, g):
            mine = AT_DVE if g in AT_DVE else AT_ACT
            return (at_dve if g in AT_DVE else at_act), (r * NT + kt) * len(mine) + mine.index(g) + 2

        x_t = x.rearrange("(t p) d -> p t d", p=T)
        out_t = out.rearrange("(t p) d -> p t d", p=T)
        tok_t = tok_dram.rearrange("(t p) d -> p t d", p=T)
        pair_t = pair_dram[0:2 * N, :].rearrange("(t p k) d -> p t k d", p=T, k=2)

        block = ctx.enter_context(nc.Block())

        @block.sync
        def _(sp):
            sp.dma_start(edge_i[:, 0, :], dst.rearrange("(p c) -> p c", c=EC)).then_inc(L["edges"], 16)
            sp.dma_start(edge_i[:, 1, :], src.rearrange("(p c) -> p c", c=EC)).then_inc(L["edges"], 16)
            sp.dma_start(next_i[0:T - 1, :], dst.rearrange("(p c) -> p c", c=EC)[1:T, 0:1],
                         allow_slow_non_contiguous=True).then_inc(L["nextrow"], 16)
            for p0, p1 in ((0, 112), (112, T)):
                sp.dma_start(res[p0:p1, :, :], x_t[p0:p1]).then_inc(L["x"], 16)
            sp.dma_start(gW1_sb[:], gW1).then_inc(L["small"], 16)
            sp.dma_start(gW2_sb[:], gW2).then_inc(L["small"], 16)
            sp.dma_start(gW3_sb[:], gW3.rearrange("(a p) f -> p a f", p=P)).then_inc(L["small"], 16)
            sp.dma_start(wr_sb[:], Wr.rearrange("(a p) e -> p a e", p=P)).then_inc(L["small"], 16)
            sp.dma_start(w_sb[:], gnn_w.rearrange("(a b) -> a b", a=1).broadcast_to([P, 1])).then_inc(L["small"], 16)
            sp.wait_ge(e_dve, 2)
            sp.dma_start(key_dram[0:E].rearrange("(p c) -> p c", c=EC), key_f[:]).then_inc(key_stored, 16)
            sp.dma_start(lo_dram[0:E].rearrange("(p c) -> p c", c=EC), lo_f[:]).then_inc(key_stored, 16)
            sp.dma_start(key_dram[E:E + CH].rearrange("(a c) -> a c", a=1), pad[:]).then_inc(key_stored, 16)
            sp.dma_start(lo_dram[E:E + CH].rearrange("(a c) -> a c", a=1), pad[:]).then_inc(key_stored, 16)
            sp.dma_start(w1_sb[:].rearrange("p e k h -> p (e k) h"),
                         W1.rearrange("e (k p) h -> p (e k) h", p=P)).then_inc(L["experts"], 16)
            sp.dma_start(w2_sb[:].rearrange("p e k h -> p (e k) h"),
                         W2.rearrange("e (k p) h -> p (e k) h", p=P)).then_inc(L["experts"], 16)
            sp.wait_ge(y_ready, 1)
            sp.dma_start(gam[:], gamma.rearrange("(a d) -> a d", a=1).broadcast_to([T, D])).then_inc(L["bcast"], 16)
            sp.dma_start(bet[:], beta.rearrange("(a d) -> a d", a=1).broadcast_to([T, D])).then_inc(L["bcast"], 16)
            sp.dma_start(br_sb[:], br.rearrange("(a d) -> a d", a=1).broadcast_to([T, NX])).then_inc(L["bcast"], 16)
            sp.dma_start(b1_sb[:], b1.rearrange("(a e) h -> a e h", a=1).broadcast_to([P, NX, H])).then_inc(L["experts"], 16)
            sp.dma_start(b2_sb[:], b2.rearrange("(a e) h -> a e h", a=1).broadcast_to([P, NX, D])).then_inc(L["experts"], 16)
            for g in range(NG):
                sp.wait_ge(tok_ready, g + 1)
                sp.dma_start(tok_t[:, ds(g * G, G), :], tok[:]).then_inc(tok_stored, 16)
            for i in range(4):
                sp.wait_ge(scattered[i], 16 * (NB // 4))

            def load_pairs(g, i):
                sp.dma_start(fin[:, i, :, :], pair_t[:, ds(g * G + i, 1), :, :]
                             .rearrange("p t k d -> p (t k) d")).then_inc(fin_in[i], 16)

            for i in range(G):
                load_pairs(0, i)
            with sp.Fori(1, NG) as g:
                for i in range(G):
                    sp.wait_ge(fin_done, g * G + i + 1 - G)
                    load_pairs(g, i)

        def tiles_in_pairs(eng, body):
            with eng.Fori(0, (NT - 1) // 2) as i:
                body(2 * i + 1, 1)
                body(2 * i + 2, 0)

        def all_blocks(eng, body, unrolled=8):
            for b in range(unrolled):
                body(b, b % 4)
            with eng.Fori(unrolled // 4, NB // 4 - 1) as i:
                for j in range(4):
                    body(4 * i + j, j)
            for b in range(NB - 4, NB):
                body(b, b % 4)

        def static(b):
            return isinstance(b, int)

        @block.gpsimd
        def _(pool):
            pool.iota(iota[:], pattern=[[1, WC]], base=0, channel_multiplier=0,
                      allow_small_or_imprecise_dtypes=True).then_inc(c_pool, 1)
            pool.iota(part[:], pattern=[[0, 1]], base=0, channel_multiplier=1,
                      allow_small_or_imprecise_dtypes=True).then_inc(c_pool, 1)
            pool.iota(thr_row[:], pattern=[[NT * T, 26], [NT * WD, NQ]], base=0, channel_multiplier=0,
                      allow_small_or_imprecise_dtypes=True).then_inc(c_pool, 1)
            pool.iota(tile1[:], pattern=[[1, NT]], base=1, channel_multiplier=0,
                      allow_small_or_imprecise_dtypes=True).then_inc(c_pool, 1)
            pool.iota(ex_m8[:], pattern=[[0, NT], [1, NX]], base=-NX, channel_multiplier=0,
                      allow_small_or_imprecise_dtypes=True).then_inc(c_pool, 1)
            pool.memset(pad[:], -1.0).then_inc(c_pool, 1)
            pool.memset(ones16[:], 1.0).then_inc(c_pool, 1)
            pool.memset(ones[:], 1.0).then_inc(c_pool, 1)
            pool.memset(eps[:], EPS).then_inc(c_pool, 1)
            pool.memset(zeros16[:], 0.0).then_inc(c_pool, 1)

            pool.wait_ge(e_dve, 4)
            pool.wait_ge(key_stored, 64)
            for g, w in enumerate(WG):
                pool.indirect_dma_start(out=rows[0:w, g, :], out_offset=None,
                                        in_=key_dram[0:E].rearrange("(r c) -> r c", c=EC),
                                        in_offset=bass.IndirectOffsetOnAxis(ap=row_i[0:w, g:g + 1], axis=0)
                                        ).then_inc(row_got, 16)

            def gather_edges():
                for a, table in enumerate((key_dram, lo_dram)):
                    for g, w in enumerate(WG):
                        pool.indirect_dma_start(out=gath[0:w, a, g, :], out_offset=None,
                                                in_=table.rearrange("(e a) -> e a", a=1),
                                                in_offset=bass.IndirectOffsetOnAxis(ap=start_i[0:w, g:g + 1], axis=0)
                                                ).then_inc(got_key, 16)

            pool.wait_ge(idx_ready, 1)
            gather_edges()
            done, settle, start, st = chain(pool, link_split)
            for g in range(NG):
                start(g * 3)
                pool.wait_ge(xn_ready, g * G + G)
                grp = res[:, ds(g * G, G), :]
                pool.tensor_tensor(grp, grp, xn[:], ALU.add).then_inc(res_ready, 1)
                pool.wait_ge(z_sb, g + 1)
                zg, z3g = z[:, ds(g * G, G), :], z3[:, ds(g * G, G), :, :]
                done(pool.tensor_copy(z3g[:, :, 0, :], zg))
                settle()
                done(pool.tensor_tensor(zres[:], zg, z3g[:, :, 0, :], ALU.subtract))
                settle()
                done(pool.tensor_copy(z3g[:, :, 1, :], zres[:]))
                settle()
                pool.tensor_tensor(z3g[:, :, 2, :], zres[:], z3g[:, :, 1, :], ALU.subtract).then_inc(zsplit, 1)
                assert st["n"] == 3
                pool.wait_ge(zsplit, g + 1)
            pool.wait_ge(rounds_ready, 1)
            n_rounds = pool.value_load(rounds_i[0:1, 0:1], min_val=1, max_val=-(-E // CH))
            with pool.Fori(0, n_rounds) as r:
                pool.wait_ge(idx_ready, r + 2)
                pool.wait_ge(keyT_psum, (r + 1) * STEPS)
                pool.nop(nofuse=True)
                gather_edges()

            pool.wait_ge(L["bcast"], 48)
            done, settle, start, st = chain(pool, link_affine)
            for g in range(NG):
                start(g)
                pool.wait_ge(tok_norm, g + 1)
                done(pool.tensor_tensor(tok[:], tok[:], gam[:].unsqueeze(1).broadcast_to([T, G, D]), ALU.mult))
                settle()
                pool.tensor_tensor(tok[:], tok[:], bet[:].unsqueeze(1).broadcast_to([T, G, D]),
                                   ALU.add).then_inc(tok_ready, 1)
                assert st["n"] == 1

            def gather_block(b, j):
                pool.tensor_copy(gcol[:, j:j + 1], gidx[:, ds(b, 1)]).then_inc(gcol_ready, 1)
                pool.wait_ge(gcol_ready, b + 1)
                pool.nop(nofuse=True)
                pool.indirect_dma_start(out=xg[:, j, :], out_offset=None, in_=tok_dram,
                                        in_offset=bass.IndirectOffsetOnAxis(ap=gcol[:, j:j + 1], axis=0)
                                        ).then_inc(xg_in[j], 16)

            def block(b, j):
                pool.tensor_copy(scol[:, j:j + 1], sidx[:, ds(b, 1)]).then_inc(scol_ready, 1)
                pool.wait_ge(scol_ready, b + 1)
                pool.wait_ge(down_sb, b + 1)
                pool.nop(nofuse=True)
                pool.indirect_dma_start(out=pair_dram, out_offset=bass.IndirectOffsetOnAxis(ap=scol[:, j:j + 1], axis=0),
                                        in_=yb[:, j, :], in_offset=None).then_inc(scattered[j], 16)
                if not (static(b) and b >= NB - 4):
                    pool.wait_ge(xgT_psum, b + 1)
                    gather_block(b + 4, j)

            pool.wait_ge(slots_ready, 1)
            pool.wait_ge(tok_stored, 16 * NG)
            for j in range(4):
                gather_block(j, j)
            all_blocks(pool, block)
            for j in range(4):
                pool.wait_ge(scattered[j], 16 * (NB // 4))

        @block.scalar
        def _(act):
            act.wait_ge(c_pe, 1)
            act.copy(gW1T[:].rearrange("p k f -> p (k f)"), psum[:, 7, 0:2 * F1]).then_inc(c_act, 1)
            act.copy(gW2T[:], psum[0:F1, 7, 2 * F1:2 * F1 + F2]).then_inc(c_act, 1)
            act.copy(gW3T[:], psum[0:F2, 7, 160:160 + D]).then_inc(c_act, 1)
            act.copy(rounds_f[0:1, 3:4], eps[0:1, :]).then_inc(at_act, 1)

            for g in range(NG):
                act.wait_ge(var_ready, g + 1)
                act.activation(std[:], mv[:, :, 1], ACT.Sqrt, bias=eps[0:T, :]).then_inc(std_ready, 1)
                for t in range(G):
                    act.wait_ge(xnT_psum, g * G + t + 1)
                    act.copy(xnT[:, t, :, :].rearrange("p k n -> p (k n)"), psum[:, t, 0:2 * T]).then_inc(xnT_sb, 1)
                act.wait_ge(z_psum, g + 1)
                act.copy(z[:, ds(g * G, G), :].rearrange("p t f -> p (t f)"), psum[0:T, 5, 0:G * F1]).then_inc(z_sb, 1)

            act.wait_ge(rounds_ready, 1)
            n_rounds = act.value_load(rounds_i[0:1, 0:1], min_val=1, max_val=-(-E // CH))
            with act.Fori(0, n_rounds) as r:
                def window(kt, par, q, first):
                    nd = WD if q < NQ - 1 else T - WD * (NQ - 1)
                    act.wait_ge(win_psum, r * NW + kt * NQ + q + 1)
                    if q == 0 and not first:
                        act.wait_ge(at_psum, r * NT * G + kt * G - 4)
                    act.copy(cts[:, par, :, WD * q:WD * q + nd],
                             psum[:, 4 + (par + q) % 2, 0:NT * nd].rearrange("p (d h) -> p h d", h=NT)).then_inc(win_sb, 1)

                def copy_at(kt, par, g):
                    act.wait_ge(at_psum, 1 + r * NT * G + kt * G + g + 1)
                    act.wait_ge(applied, SET + r * NT * G + (kt - 1) * G + g + 1)
                    act.copy(at[:, g, :], psum[0:T, 6 + (par + g) % 2, :].bitcast(F16)[:, 0:G * P]).then_inc(at_act, 1)

                for q in range(NQ):
                    window(0, 0, q, True)

                def tile(kt, par):
                    for q in range(NQ):
                        window(kt, par, q, False)
                        if q in AT_ACT:
                            copy_at(kt - 1, 1 - par, q)

                tiles_in_pairs(act, tile)
                for g in AT_ACT:
                    copy_at(NT - 1, 0, g)
                act.wait_ge(applied, SET + (r + 1) * NT * G)
                act.wait_ge(at_psum, 1 + (r + 1) * NT * G)

            for g in range(NG):
                for h, (t0, t1) in enumerate(((0, 3), (3, 5))):
                    act.wait_ge(yT_psum, g * 2 + h + 1)
                    act.activation(y1T[:, t0:t1, :].rearrange("p t n -> p (t n)"), psum[0:F1, 4 + h, 0:(t1 - t0) * T],
                                   ACT.Relu).then_inc(yT_sb, 1)
                for h, (t0, t1) in enumerate(((0, 3), (3, 5))):
                    act.wait_ge(h2_psum, g * 2 + h + 1)
                    act.activation(h2T[:, t0:t1, :].rearrange("p t n -> p (t n)"), psum[0:F2, 6 + h, 0:(t1 - t0) * T],
                                   ACT.Relu).then_inc(h2_sb, 1)
                for k in range(2):
                    act.wait_ge(var2, g * 2 + k + 1)
                    act.activation(std_2[:], mv2[:, :, 1], ACT.Sqrt, bias=eps[0:T, :]).then_inc(std2, 1)
                for t in range(G):
                    act.wait_ge(tokT_psum, g * G + t + 1)
                    act.copy(tokT[:, t, :, :].rearrange("p k n -> p (k n)"), psum[:, 6 + t % 2, 0:2 * T]).then_inc(tokT_sb, 1)

            act.wait_ge(r_dve, 1)
            act.activation(top[:, 3, :], top[:, 3, :], ACT.Exp).then_inc(r_act, 1)

            def copy_hT(b, j):
                act.wait_ge(hT_psum, b + 1)
                if not (static(b) and b < 2):
                    act.wait_ge(down_psum, b - 1)
                act.copy(hT[:, j % 2, :, :].rearrange("p k n -> p (k n)"), psum[:, 2 + j % 2, :]).then_inc(hT_sb, 1)

            def block(b, j):
                if not (static(b) and b < 1):
                    copy_hT(b - 1, (j - 1) % 4)
                act.wait_ge(up_sb, b + 1)
                if not (static(b) and b < 2):
                    act.wait_ge(hT_psum, b - 1)
                act.activation(hg[:, j % 2, :], up[:, j % 2, :], ACT.Gelu).then_inc(gelu_sb, 1)

            all_blocks(act, block)
            copy_hT(NB - 1, 3)

            with act.Fori(0, NG) as g:
                for i in range(G):
                    act.wait_ge(fin_done, g * G + i + 1)
                    act.dma_start(out_t[:, ds(g * G + i, 1), :], res[:, ds(g * G + i, 1), :]).then_inc(out_stored, 16)
            act.wait_ge(out_stored, 16 * NT)

        @block.tensor
        def _(pe):
            pe.wait_ge(c_pool, 10)
            pe.wait_ge(c_dve, 3)
            pe.wait_ge(L["small"], 80)
            for k in range(KD):
                pe.transpose(psum[:, 7, k * F1:(k + 1) * F1], gW1_sb[:, k * P:(k + 1) * P], ident[0:F1, 0:F1])
            pe.transpose(psum[0:F1, 7, 2 * F1:2 * F1 + F2], gW2_sb[:], ident[0:F2, 0:F2])
            for k in range(KD):
                last = pe.transpose(psum[0:F2, 7, 160 + k * P:160 + (k + 1) * P], gW3_sb[:, k, :], ident[:])
            last.then_inc(c_pe, 1)
            for g, w in enumerate(WG):
                last = pe.matmul(psum[0:w, 6, g:g + 1], thr_row[0:1, g * P:g * P + w], ones[0:1, 0:1],
                                 start=True, stop=True)
                last.then_inc((applied, at_psum)[g], 1)
            pe.wait_ge(e_dve, 3)
            pe.matmul(psum[:, 6, 2:3], ones[0:T, :], inv[:, 2:3], start=True, stop=True)
            pe.matmul(psum[:, 6, P:P + T], key_f[:, 0:1].broadcast_to([T, P]), ident[0:T, 0:T],
                      start=True, stop=True).then_inc(e_pe, 1)

            pe.wait_ge(c_act, 3)
            for g in range(NG):
                for t in range(G):
                    pe.wait_ge(xn_ready, g * G + t + 1)
                    for k in range(KD):
                        last = pe.transpose(psum[:, t, k * T:(k + 1) * T], xn[:, t, k * P:(k + 1) * P], ident[0:T, 0:T])
                    last.then_inc(xnT_psum, 1)
                for t in range(G):
                    pe.wait_ge(xnT_sb, g * G + t + 1)
                    for k in range(KD):
                        last = pe.matmul(psum[0:T, 5, t * F1:(t + 1) * F1], xnT[:, t, k, :], gW1T[:, k, :],
                                         start=(k == 0), stop=(k == KD - 1))
                last.then_inc(z_psum, 1)
                pe.wait_ge(z_sb, g + 1)
            for b in range(4):
                pe.matmul(psum[:, b, :], ones16[0:1, :], zeros16[:], start=True, stop=True).then_inc(applied, 1)
            pe.wait_ge(e_dve, 5)
            for g, w in enumerate(WG):
                last = pe.matmul(psum[0:1, 6, g * P:g * P + w], start_f[0:w, g:g + 1], ident[0:w, 0:w],
                                 start=True, stop=True)
            last.then_inc(e_pe, 1)

            pe.wait_ge(rounds_ready, 1)
            pe.wait_ge(zsplit, NG)
            n_rounds = pe.value_load(rounds_i[0:1, 0:1], min_val=1, max_val=-(-E // CH))
            with pe.Fori(0, n_rounds) as r:
                pe.wait_ge(key_rel, (r + 1) * 2)
                for j in range(STEPS):
                    for a in range(2):
                        for g, w in enumerate(WG):
                            c = a * NWX + g * P
                            last = pe.transpose(psum[:, 4 + j, c:c + w], gath[0:w, a, g, j * P:(j + 1) * P],
                                                ident[0:w, 0:w])
                    last.then_inc(keyT_psum, 1)
                pe.wait_ge(keyT_sb, (r + 1) * STEPS)

                def window(kt, par, q, early):
                    wc = NT * (WD if q < NQ - 1 else T - WD * (NQ - 1))
                    pe.wait_ge(onehots, r * NW + kt * NQ + q + 1)
                    if not early:
                        pe.wait_ge(win_sb, r * NW + kt * NQ + q - 1)
                    for j in range(STEPS):
                        last = pe.matmul(psum[:, 4 + (par + q) % 2, 0:wc], oh_lo[:, q, j, :], oh_col[:, q, j, 0:wc],
                                         start=(j == 0), stop=(j == STEPS - 1))
                    last.then_inc(win_psum, 1)

                def turn(kt, par, g, early):
                    if g == 0:
                        pe.wait_ge(win_sb, r * NW + (kt + 1) * NQ)
                    if not (early and g < 2):
                        pe.wait_ge(*at_count(r, kt if g >= 2 else kt - 1, (g - 2) % G))
                    bank = psum[0:T, 6 + (par + g) % 2, :].bitcast(F16)
                    for h in range(G):
                        last = pe.transpose(bank[:, h * P:(h + 1) * P], cts[:, par, g * G + h, :], ident16[:])
                    last.then_inc(at_psum, 1)

                def apply(kt, g):
                    pe.wait_ge(*at_count(r, kt, g))
                    for h in range(G):
                        c = (g * G + h) * F1
                        for i in range(3):
                            last = pe.matmul(acc[:, c:c + F1], at[:, g, h * P:(h + 1) * P],
                                             z3[:, ds(kt, 1), i, :].rearrange("p a f -> p (a f)"),
                                             start=False, stop=True, skip_group_check=True)
                    last.then_inc(applied, 1)

                for q in range(NQ):
                    window(0, 0, q, q < 2)

                def tile(kt, par):
                    for q in range(NQ):
                        window(kt, par, q, False)
                        if q < G:
                            turn(kt - 1, 1 - par, q, False)
                        if 1 <= q <= G:
                            apply(kt - 1, q - 1)

                tiles_in_pairs(pe, tile)
                for g in range(G + 1):
                    if g < G:
                        turn(NT - 1, 0, g, False)
                    if g >= 1:
                        apply(NT - 1, g - 1)

            for g in range(NG):
                halves = ((0, 3), (3, 5))
                pe.wait_ge(y_ready, g + 1)
                for h, (t0, t1) in enumerate(halves):
                    for t in range(t0, t1):
                        last = pe.transpose(psum[0:F1, 4 + h, (t - t0) * T:(t - t0 + 1) * T], y1[:, t, :], ident[0:T, 0:T])
                    last.then_inc(yT_psum, 1)
                for h, (t0, t1) in enumerate(halves):
                    pe.wait_ge(yT_sb, g * 2 + h + 1)
                    pe.matmul(psum[0:F2, 6 + h, 0:(t1 - t0) * T], gW2T[:], y1T[:, t0:t1, :].rearrange("p t n -> p (t n)"),
                              start=True, stop=True).then_inc(h2_psum, 1)
                for t in range(G):
                    pe.wait_ge(h2_sb, g * 2 + (1 if t < 3 else 2))
                    c = (t % 2) * D
                    pe.matmul(psum[0:T, 4 + t // 2, c:c + D], h2T[:, t, :], gW3T[:],
                              start=True, stop=True).then_inc(h3_psum, 1)
                pe.wait_ge(tok_ready, g + 1)
                for t in range(G):
                    if t >= 2:
                        pe.wait_ge(tokT_sb, g * G + t - 1)
                    for k in range(KD):
                        last = pe.transpose(psum[:, 6 + t % 2, k * T:(k + 1) * T], tok[:, t, k * P:(k + 1) * P], ident[0:T, 0:T])
                    last.then_inc(tokT_psum, 1)
                for t in range(G):
                    pe.wait_ge(tokT_sb, g * G + t + 1)
                    for k in range(KD):
                        last = pe.matmul(psum[0:T, 3, P + t * NX:P + (t + 1) * NX], tokT[:, t, k, :], wr_sb[:, k, :],
                                         start=(k == 0), stop=(k == KD - 1))
                last.then_inc(logit_psum, 1)
                pe.wait_ge(logit_sb, g + 1)

            pe.wait_ge(r_dve, 2)
            selv = sel[:].rearrange("p t e -> p (t e)")
            pe.matmul(psum[0:T, 4, 0:NT * NX], later[0:T, 0:T], selv, start=True, stop=True)
            pe.matmul(psum[:, 5, 0:NT * NX], ones16[0:T, :], selv, start=True, stop=True).then_inc(r_pe, 1)
            pe.matmul(psum[:, 6, 0:2 * NB], ones16[0:1, :], zeros16[:, 0:2 * NB], start=True, stop=True)
            with pe.Fori(0, NG) as g:
                for s_ in range(2 * G):
                    pe.wait_ge(pair_oh, g * 2 * G + s_ + 1)
                    pe.matmul(psum[:, 6, 0:2 * NB], oh_lane[:, s_, :], oh_blk[:, s_, :, :].rearrange("p a b -> p (a b)"),
                              start=False, stop=True, skip_group_check=True).then_inc(pair_mm, 1)

            pe.wait_ge(L["experts"], 64)
            pe.wait_ge(slots_ready, 1)

            def turn_x(b, j, i):
                pe.wait_ge(xg_in[j], 16 * (i + 1))
                if not (static(b) and b < 2):
                    pe.wait_ge(xgT_sb, b - 1)
                for k in range(KD):
                    last = pe.transpose(psum[:, 6 + j % 2, k * P:(k + 1) * P], xg[:, j, k * P:(k + 1) * P], ident[:])
                last.then_inc(xgT_psum, 1)

            def up_mm(b, j):
                e = pe.value_load(ebi[0:1, ds(b, 1)], min_val=0, max_val=NX - 1)
                pe.wait_ge(xgT_sb, b + 1)
                if not (static(b) and b < 2):
                    pe.wait_ge(up_sb, b - 1)
                for k in range(KD):
                    last = pe.matmul(psum[:, j % 2, :], xgT[:, j % 2, k, :], w1_sb[:, ds(e, 1), k, :].rearrange("p a h -> p (a h)"),
                                     start=(k == 0), stop=(k == KD - 1))
                last.then_inc(up_psum, 1)

            def turn_h(b, j):
                pe.wait_ge(gelu_sb, b + 1)
                if not (static(b) and b < 2):
                    pe.wait_ge(hT_sb, b - 1)
                for k in range(KH):
                    last = pe.transpose(psum[:, 2 + j % 2, k * P:(k + 1) * P], hg[:, j % 2, k * P:(k + 1) * P], ident[:])
                last.then_inc(hT_psum, 1)

            def down_mm(b, j):
                e = pe.value_load(ebi[0:1, ds(b, 1)], min_val=0, max_val=NX - 1)
                pe.wait_ge(hT_sb, b + 1)
                if not (static(b) and b < 2):
                    pe.wait_ge(down_sb, b - 1)
                for k in range(KH):
                    last = pe.matmul(psum[:, 4 + j % 2, 0:D], hT[:, j % 2, k, :], w2_sb[:, ds(e, 1), k, :].rearrange("p a h -> p (a h)"),
                                     start=(k == 0), stop=(k == KH - 1))
                last.then_inc(down_psum, 1)

            pe.wait_ge(logit_sb, NG)
            turn_x(0, 0, 0)

            def expert_step(b, j, i):
                if not (static(b) and b == NB - 1):
                    turn_x(b + 1, (j + 1) % 4, i if j < 3 else i + 1)
                up_mm(b, j)
                if not (static(b) and b < 1):
                    turn_h(b - 1, (j - 1) % 4)
                if not (static(b) and b < 2):
                    down_mm(b - 2, (j - 2) % 4)

            for b in range(8):
                expert_step(b, b % 4, b // 4)
            with pe.Fori(2, NB // 4 - 1) as i:
                for j in range(4):
                    expert_step(4 * i + j, j, i)
            for b in range(NB - 4, NB):
                expert_step(b, b % 4, b // 4)
            down_mm(NB - 2, 2)
            turn_h(NB - 1, 3)
            down_mm(NB - 1, 3)

        @block.vector
        def _(dve):
            done, settle, start, st = chain(dve, link_dve)

            def floor_of(out, in_, add, scale):
                done(dve.tensor_scalar(out, in_, add, scale, ALU.add, ALU.mult))
                settle()
                done(dve.tensor_scalar(out, out, 0.5, MAGIC, ALU.subtract, ALU.add))
                settle()
                done(dve.tensor_scalar(out, out, MAGIC, None, ALU.subtract))
                settle()

            dve.wait_ge(c_pool, 10)
            dve.tensor_scalar(ident[:], iota[:, 0:P], part[:], None, ALU.is_equal).then_inc(c_dve, 1)
            dve.tensor_scalar(ident16[:], iota[:, 0:P], part[:], None, ALU.is_equal).then_inc(c_dve, 1)
            dve.tensor_scalar(later[:], iota[:, 0:P], part[:], None, ALU.is_gt).then_inc(c_dve, 1)
            done(dve.memset(inv[:], 0.0))
            dve.memset(cnt[:], 0.0).then_inc(at_dve, 1)

            dve.wait_ge(L["edges"], 32)
            dve.wait_ge(L["nextrow"], 16)
            done(dve.tensor_copy(edge_f[:, 0, :], edge_i[:, 0, :]))
            done(dve.tensor_copy(edge_f[:, 1, :], edge_i[:, 1, :]))
            done(dve.tensor_copy(next_f[0:T - 1, :], next_i[0:T - 1, :]))
            settle()
            floor_of(hi_f[:], edge_f[:, 1, :], 0.5, 1.0 / T)
            dve.scalar_tensor_tensor(lo_f[:], hi_f[:], -float(T), edge_f[:, 1, :], ALU.mult, ALU.add).then_inc(e_dve, 1)
            dve.scalar_tensor_tensor(key_f[:], edge_f[:, 0, :], float(NT), hi_f[:], ALU.mult, ALU.add).then_inc(e_dve, 1)
            done(dve.tensor_tensor(junk[0:T, 0:EC - 1], edge_f[:, 0, 0:EC - 1], edge_f[:, 0, 1:EC], ALU.is_gt))
            done(dve.tensor_tensor(inv[0:T - 1, 1:2], edge_f[0:T - 1, 0, EC - 1:EC], next_f[0:T - 1, :], ALU.is_gt))
            settle()
            done(dve.tensor_reduce(inv[:, 0:1], junk[0:T, 0:EC - 1], AX.X, ALU.add))
            settle()
            dve.tensor_tensor(inv[:, 2:3], inv[:, 0:1], inv[:, 1:2], ALU.add).then_inc(e_dve, 1)
            dve.wait_ge(e_pe, 1)
            for g, w in enumerate(WG):
                done(dve.tensor_copy(thr[0:w, g:g + 1], psum[0:w, 6, g:g + 1]))
            done(dve.tensor_scalar(flag[:, 0:1], psum[:, 6, 2:3], 1.0, None, ALU.min))
            settle()
            done(dve.tensor_scalar(flag[:, 1:2], flag[:, 0:1], -1.0, 1.0, ALU.mult, ALU.add))
            for g, w in enumerate(WG):
                done(dve.tensor_scalar(rows[0:w, g, 0:T], psum[0:w, 6, P:P + T], thr[0:w, g:g + 1], None,
                                       ALU.is_lt, ALU.add, accum_out=cnt[0:w, g, 0:1]))
            settle()
            for g, w in enumerate(WG):
                done(dve.tensor_scalar(cnt[0:w, g, 1:2], cnt[0:w, g, 0:1], -1.0, 0.0, ALU.add, ALU.max))
            settle()
            for g, w in enumerate(WG):
                last = dve.tensor_copy(row_i[0:w, g:g + 1], cnt[0:w, g, 1:2])
            last.then_inc(e_dve, 1)
            dve.wait_ge(row_got, 32)
            for g, w in enumerate(WG):
                done(dve.tensor_scalar(junk[0:w, :], rows[0:w, g, :], thr[0:w, g:g + 1], None,
                                       ALU.is_lt, ALU.add, accum_out=cnt[0:w, g, 2:3]))
                settle()
                done(dve.scalar_tensor_tensor(cnt[0:w, g, 3:4], cnt[0:w, g, 1:2], float(EC), cnt[0:w, g, 2:3],
                                              ALU.mult, ALU.add))
                settle()
                last = dve.tensor_tensor(start_f[0:w, g:g + 1], cnt[0:w, g, 3:4], flag[0:w, 1:2], ALU.mult)
            last.then_inc(e_dve, 1)
            dve.wait_ge(e_dve, 5)
            for g, w in enumerate(WG):
                last = dve.tensor_copy(start_i[0:w, g:g + 1], start_f[0:w, g:g + 1])
            last.then_inc(idx_ready, 1)

            dve.wait_ge(L["x"], 32)
            before = st["n"]
            for g in range(NG):
                start(before + g * 2 * G)
                for t in range(G):
                    done(dve.bn_stats(stats[:, t, :], res[:, ds(g * G + t, 1), :].rearrange("p a d -> p (a d)")))
                settle()
                for t in range(G):
                    last = dve.bn_aggr(mv[:, t, :], stats[:, t, :])
                    if t < G - 1:
                        done(last)
                last.then_inc(var_ready, 1)
                dve.wait_ge(std_ready, g + 1)
                done(dve.reciprocal(rstd[:], std[:]))
                settle()
                for t in range(G):
                    dve.tensor_scalar(xn[:, t, :], res[:, ds(g * G + t, 1), :].rearrange("p a d -> p (a d)"),
                                      mv[:, t, 0:1], rstd[:, t:t + 1], ALU.subtract, ALU.mult).then_inc(xn_ready, 1)
                dve.wait_ge(xnT_psum, (g + 1) * G)
                dve.wait_ge(res_ready, g + 1)
                assert st["n"] == 2 * G, st["n"]
            start(before + NG * 2 * G)

            dve.wait_ge(e_pe, 2)
            done(dve.tensor_copy(start_row[:], psum[0:1, 6, 0:NWX]))
            settle()
            done(dve.tensor_tensor(size_row[:], start_row[:, 1:NWX], start_row[:, 0:NW], ALU.subtract))
            settle()
            done(dve.tensor_reduce(rounds_f[:, 0:1], size_row[:], AX.X, ALU.max))
            settle()
            done(dve.tensor_tensor(rounds_f[:, 1:2], rounds_f[:, 0:1], flag[0:1, 1:2], ALU.mult))
            settle()
            done(dve.scalar_tensor_tensor(rounds_f[:, 0:1], flag[0:1, 0:1], float(E), rounds_f[:, 1:2], ALU.mult, ALU.add))
            settle()
            floor_of(rounds_f[:, 2:3], rounds_f[:, 0:1], CH - 0.5, 1.0 / CH)
            done(dve.tensor_scalar(rounds_f[:, 1:2], rounds_f[:, 2:3], 1.0, None, ALU.max))
            settle()
            dve.tensor_copy(rounds_i[:], rounds_f[:, 1:2]).then_inc(rounds_ready, 1)
            dve.wait_ge(rounds_ready, 1)
            n_rounds = dve.value_load(rounds_i[0:1, 0:1], min_val=1, max_val=-(-E // CH))

            done, settle, start, st = chain(dve, link_round)
            with dve.Fori(0, n_rounds) as r:
                start(r * 3)
                dve.wait_ge(got_key, (r + 1) * 64)
                for g, w in enumerate(WG):
                    dve.tensor_scalar(gath[0:w, 0, g, :], gath[0:w, 0, g, :], thr[0:w, g:g + 1], None,
                                      ALU.subtract).then_inc(key_rel, 1)
                for g, w in enumerate(WG):
                    done(dve.tensor_scalar(start_f[0:w, g:g + 1], start_f[0:w, g:g + 1], float(CH), float(E),
                                           ALU.add, ALU.min))
                settle()
                for g, w in enumerate(WG):
                    last = dve.tensor_copy(start_i[0:w, g:g + 1], start_f[0:w, g:g + 1])
                    done(last) if g == 0 else last.then_inc(idx_ready, 1)
                for j in range(STEPS):
                    dve.wait_ge(keyT_psum, r * STEPS + j + 1)
                    dve.tensor_copy(keyT[:, :, j, :], psum[:, 4 + j, 0:2 * NWX].rearrange("p (a w) -> p a w", a=2)
                                    ).then_inc(keyT_sb, 1)
                dve.wait_ge(keyT_sb, (r + 1) * STEPS)

                def window(kt, q, first):
                    wc = NT * (WD if q < NQ - 1 else T - WD * (NQ - 1))
                    if not first:
                        dve.wait_ge(win_psum, r * NW + kt * NQ + q + 1 - NQ)
                    for j in range(STEPS):
                        dve.tensor_scalar(oh_col[:, q, j, 0:wc], iota[:, 0:wc],
                                          keyT[:, 0, j, ds(kt * NQ + q, 1)], None, ALU.is_equal)
                        last = dve.tensor_scalar(oh_lo[:, q, j, :], iota[:, 0:P],
                                                 keyT[:, 1, j, ds(kt * NQ + q, 1)], None, ALU.is_equal)
                    last.then_inc(onehots, 1)

                def copy_at(kt, par, g):
                    dve.wait_ge(at_psum, 1 + r * NT * G + kt * G + g + 1)
                    dve.wait_ge(applied, SET + r * NT * G + (kt - 1) * G + g + 1)
                    dve.tensor_copy(at[:, g, :], psum[0:T, 6 + (par + g) % 2, :].bitcast(F16)[:, 0:G * P]).then_inc(at_dve, 1)

                for q in range(NQ):
                    window(0, q, True)

                def tile(kt, par):
                    for q in range(NQ):
                        window(kt, q, False)
                        if q - 1 in AT_DVE:
                            copy_at(kt - 1, 1 - par, q - 1)

                tiles_in_pairs(dve, tile)
                for g in AT_DVE:
                    copy_at(NT - 1, 0, g)
                dve.wait_ge(win_psum, (r + 1) * NW)
                dve.wait_ge(applied, SET + (r + 1) * NT * G)
                assert st["n"] == 3, st["n"]

            dve.wait_ge(got_key, (n_rounds + 1) * 64)
            done, settle, start, st = chain(dve, link_late)
            PER_G = 7 * G - 1
            for g in range(NG):
                start(g * PER_G)
                dve.scalar_tensor_tensor(y1[:].rearrange("p t f -> p (t f)"),
                                         z[:, ds(g * G, G), :].rearrange("p t f -> p (t f)"), w_sb[0:T, :],
                                         acc[0:T, ds(g * G * F1, G * F1)], ALU.mult, ALU.add).then_inc(y_ready, 1)
                for t in range(G):
                    dve.wait_ge(h3_psum, g * G + min(t | 1, G - 1) + 1)
                    rt_ = res[:, ds(g * G + t, 1), :].rearrange("p a d -> p (a d)")
                    c = (t % 2) * D
                    done(dve.scalar_tensor_tensor(rt_, psum[0:T, 4 + t // 2, c:c + D], 0.0, rt_, ALU.max, ALU.add))
                settle()
                for k in range(2):
                    for t in range(G):
                        src_ = res[:, ds(g * G + t, 1), :].rearrange("p a d -> p (a d)") if k == 0 else tok[:, t, :]
                        done(dve.bn_stats(stats2[:, t, :], src_))
                    settle()
                    for t in range(G):
                        last = dve.bn_aggr(mv2[:, t, :], stats2[:, t, :])
                        if t < G - 1:
                            done(last)
                    last.then_inc(var2, 1)
                    dve.wait_ge(std2, g * 2 + k + 1)
                    done(dve.reciprocal(rstd2[:], std_2[:]))
                    settle()
                    for t in range(G):
                        src_ = res[:, ds(g * G + t, 1), :].rearrange("p a d -> p (a d)") if k == 0 else tok[:, t, :]
                        last = dve.tensor_scalar(tok[:, t, :], src_, mv2[:, t, 0:1], rstd2[:, t:t + 1],
                                                 ALU.subtract, ALU.mult)
                        if k == 0 or t < G - 1:
                            done(last)
                    if k == 0:
                        settle()
                last.then_inc(tok_norm, 1)
                if True:
                    dve.wait_ge(L["bcast"], 48)
                dve.wait_ge(logit_psum, g + 1)
                dve.tensor_tensor(logit[:, ds(g * G, G), :], psum[0:T, 3, P:P + G * NX].rearrange("p (t e) -> p t e", e=NX),
                                  br_sb[:].unsqueeze(1).broadcast_to([T, G, NX]), ALU.add).then_inc(logit_sb, 1)
                dve.wait_ge(tok_stored, (g + 1) * 16)
                assert st["n"] == PER_G, st["n"]
            start(NG * PER_G)
            dve.wait_ge(logit_sb, NG)

            def over_experts(v):
                return v.unsqueeze(2).broadcast_to([T, NT, NX])

            def largest(k, v, m, a):
                done(dve.tensor_reduce(m, v, AX.X, ALU.max))
                settle()
                done(dve.tensor_tensor(rt[0][:], v, over_experts(m), ALU.is_equal))
                settle()
                done(dve.tensor_tensor(rt[1][:], rt[0][:], ex_m8[:], ALU.mult))
                settle()
                done(dve.tensor_reduce(a, rt[1][:], AX.X, ALU.min))
                settle()
                done(dve.tensor_tensor(mask[:, k, :, :], ex_m8[:], over_experts(a), ALU.is_equal))
                settle()

            largest(0, logit[:], top[:, 0, :], top[:, 1, :])
            done(dve.scalar_tensor_tensor(rt[2][:].rearrange("p t e -> p (t e)"), mask[:, 0, :, :].rearrange("p t e -> p (t e)"),
                                          -BIG, logit[:].rearrange("p t e -> p (t e)"), ALU.mult, ALU.add))
            settle()
            largest(1, rt[2][:], top[:, 2, :], top[:, 1, :])
            dve.tensor_tensor(top[:, 3, :], top[:, 2, :], top[:, 0, :], ALU.subtract).then_inc(r_dve, 1)
            dve.tensor_tensor(sel[:], mask[:, 0, :, :], mask[:, 1, :, :], ALU.add).then_inc(r_dve, 1)
            dve.wait_ge(r_act, 1)
            done(dve.tensor_scalar(top[:, 0, :], top[:, 3, :], 1.0, None, ALU.add))
            settle()
            done(dve.reciprocal(wgt[:, :, 0], top[:, 0, :]))
            settle()
            done(dve.tensor_tensor(wgt[:, :, 1], wgt[:, :, 0], top[:, 3, :], ALU.mult))
            dve.wait_ge(r_pe, 1)
            total = psum[:, 5, 0:NT * NX].rearrange("p (t e) -> p t e", e=NX)
            for e in range(NX):
                done(dve.tensor_tensor_scan(tot[:, e, :], ones[:, 0:NT], total[:, :, e], 0.0, ALU.mult, ALU.add))
            settle()
            floor_of(blk[:, 0, :], tot[:, :, NT - 1], P - 0.5, 1.0 / P)
            done(dve.tensor_tensor_scan(blk[:, 1, :], ones[:, 0:NX], blk[:, 0, :], 0.0, ALU.mult, ALU.add))
            settle()
            done(dve.tensor_tensor(blk[:, 2, :], blk[:, 1, :], blk[:, 0, :], ALU.subtract))
            settle()
            done(dve.tensor_scalar(blk[:, 3, :], blk[:, 2, :], float(P), None, ALU.mult))
            done(dve.tensor_tensor(rt[3][:], psum[0:T, 4, 0:NT * NX].rearrange("p (t e) -> p t e", e=NX),
                                   tot[0:T, :, :].rearrange("p e t -> p t e"), ALU.add))
            settle()
            done(dve.tensor_tensor(rt[2][:], rt[3][:], total[0:T], ALU.subtract))
            settle()
            done(dve.tensor_tensor(rt[3][:], rt[2][:], blk[0:T, 3, :].unsqueeze(1).broadcast_to([T, NT, NX]), ALU.add))
            settle()
            for k in range(2):
                done(dve.tensor_tensor(rt[k][:], mask[:, k, :, :], rt[3][:], ALU.mult))
                settle()
                done(dve.tensor_reduce(pos[:, k, :], rt[k][:], AX.X, ALU.add))
                done(dve.tensor_scalar(pairno[:, k:k + 1], part[0:T, :], 2.0, float(k), ALU.mult, ALU.add))
            settle()
            floor_of(pblk[:], pos[:], 0.5, 1.0 / P)
            done(dve.scalar_tensor_tensor(plane[:].rearrange("p k t -> p (k t)"), pblk[:].rearrange("p k t -> p (k t)"),
                                          -float(P), pos[:].rearrange("p k t -> p (k t)"), ALU.mult, ALU.add))
            done(dve.tensor_tensor(ebt[:], iota[0:1, 0:NB].unsqueeze(2).broadcast_to([1, NB, NX]),
                                   blk[0:1, 1, :].unsqueeze(1).broadcast_to([1, NB, NX]), ALU.is_ge))
            settle()
            done(dve.tensor_reduce(ebf[:], ebt[:], AX.X, ALU.add))
            settle()
            done(dve.tensor_scalar(ebi[:], ebf[:], float(NX - 1), None, ALU.min))
            settle()
            with dve.Fori(0, NG) as g:
                for t in range(G):
                    for k in range(2):
                        s_, i = 2 * t + k, g * G + t
                        dve.tensor_scalar(oh_lane[:, s_, :], iota[0:T, 0:P], plane[:, k, ds(i, 1)], None, ALU.is_equal)
                        dve.tensor_scalar(oh_blk[:, s_, 0, :], iota[0:T, 0:NB], pblk[:, k, ds(i, 1)],
                                          tile1[:, ds(i, 1)], ALU.is_equal, ALU.mult)
                        dve.tensor_scalar(oh_blk[:, s_, 1, :], iota[0:T, 0:NB], pblk[:, k, ds(i, 1)],
                                          pairno[:, k:k + 1], ALU.is_equal, ALU.mult).then_inc(pair_oh, 1)
                dve.wait_ge(pair_mm, (g + 1) * 2 * G)
            done(dve.tensor_copy(slot[:, 0, :], psum[:, 6, 0:NB]))
            done(dve.tensor_copy(slot[:, 1, :], psum[:, 6, NB:2 * NB]))
            settle()
            floor_of(slot[:, 2, :], slot[:, 1, :], 0.5, 0.5)
            done(dve.scalar_tensor_tensor(slot[:, 3, :], slot[:, 0, :], float(T), slot[:, 2, :], ALU.mult, ALU.add))
            done(dve.scalar_tensor_tensor(slot[:, 4, :], slot[:, 0, :], float(2 * T), slot[:, 1, :], ALU.mult, ALU.add))
            settle()
            done(dve.tensor_scalar(gidx[:], slot[:, 3, :], -float(T), 0.0, ALU.add, ALU.max))
            done(dve.tensor_scalar(slot[:, 5, :], slot[:, 0, :], 0.0, None, ALU.is_equal))
            done(dve.tensor_scalar(thr2[:], part[:], float(2 * N + 2 * T), None, ALU.add))
            settle()
            done(dve.tensor_scalar(slot[:, 2, :], iota[:, 0:NB], float(P), thr2[:], ALU.mult, ALU.add))
            settle()
            done(dve.tensor_tensor(slot[:, 3, :], slot[:, 5, :], slot[:, 2, :], ALU.mult))
            settle()
            done(dve.scalar_tensor_tensor(sidx[:], slot[:, 4, :], -float(2 * T), slot[:, 3, :], ALU.add, ALU.add))
            settle()
            dve.engine_nop().then_inc(slots_ready, 1)

            dve.wait_ge(L["experts"], 64)

            def copy_x(b, j):
                dve.wait_ge(xgT_psum, b + 1)
                if not (static(b) and b < 2):
                    dve.wait_ge(up_psum, b - 1)
                dve.tensor_copy(xgT[:, j % 2, :, :].rearrange("p k n -> p (k n)"), psum[:, 6 + j % 2, 0:D]).then_inc(xgT_sb, 1)

            def add_b1(b, j):
                e = dve.value_load(ebi[0:1, ds(b, 1)], min_val=0, max_val=NX - 1)
                dve.wait_ge(up_psum, b + 1)
                if not (static(b) and b < 2):
                    dve.wait_ge(gelu_sb, b - 1)
                dve.tensor_tensor(up[:, j % 2, :], psum[:, j % 2, :], b1_sb[:, ds(e, 1), :].rearrange("p a h -> p (a h)"),
                                  ALU.add).then_inc(up_sb, 1)

            def add_b2(b, j, i):
                e = dve.value_load(ebi[0:1, ds(b, 1)], min_val=0, max_val=NX - 1)
                dve.wait_ge(down_psum, b + 1)
                if not (static(b) and b < 4):
                    dve.wait_ge(scattered[j], 16 * i)
                dve.tensor_tensor(yb[:, j, :], psum[:, 4 + j % 2, 0:D], b2_sb[:, ds(e, 1), :].rearrange("p a h -> p (a h)"),
                                  ALU.add).then_inc(down_sb, 1)

            def expert_step(b, j, i):
                if not (static(b) and b == NB - 1):
                    copy_x(b + 1, (j + 1) % 4)
                add_b1(b, j)
                if not (static(b) and b < 2):
                    add_b2(b - 2, (j - 2) % 4, i if j >= 2 else i - 1)

            copy_x(0, 0)
            for b in range(8):
                expert_step(b, b % 4, b // 4)
            with dve.Fori(2, NB // 4 - 1) as i:
                for j in range(4):
                    expert_step(4 * i + j, j, i)
            for b in range(NB - 4, NB):
                expert_step(b, b % 4, b // 4)
            add_b2(NB - 2, 2, NB // 4 - 1)
            add_b2(NB - 1, 3, NB // 4 - 1)

            with dve.Fori(0, NG) as g:
                for i in range(G):
                    t = g * G + i
                    r_ = res[:, ds(t, 1), :].rearrange("p a d -> p (a d)")
                    dve.wait_ge(fin_in[i], (g + 1) * 16)
                    dve.scalar_tensor_tensor(r_, fin[:, i, 0, :], wgt[:, ds(t, 1), 0], r_, ALU.mult, ALU.add).then_inc(fin_half, 1)
                    dve.wait_ge(fin_half, t + 1)
                    dve.scalar_tensor_tensor(r_, fin[:, i, 1, :], wgt[:, ds(t, 1), 1], r_, ALU.mult, ALU.add).then_inc(fin_done, 1)


_INS = ['x', 'src', 'dst', 'L0_gnn_w', 'L0_gnn_W1', 'L0_gnn_W2', 'L0_gnn_W3', 'L0_ffn_gamma', 'L0_ffn_beta',
        'L0_ffn_Wr', 'L0_ffn_br', 'L0_ffn_W1', 'L0_ffn_b1', 'L0_ffn_W2', 'L0_ffn_b2']
_OUTS = [((N, D), 'float32')]


def kernel(**inputs):
    import numpy as _np
    import concourse.bacc as _bacc
    from concourse import mybir as _mybir
    from concourse.bass_utils import run_bass_kernel_spmd as _run

    nc = _bacc.Bacc("TRN2", target_bir_lowering=False, num_devices=1)
    arrays, args = {}, []
    for name in _INS:
        a = _np.ascontiguousarray(inputs[name])
        arrays[f"in_{name}_dram"] = a
        args.append(nc.dram_tensor(f"in_{name}_dram", a.shape, _mybir.dt.from_np(a.dtype), kind="ExternalInput").ap())
    for i, (shape, dtype) in enumerate(_OUTS):
        dt = _mybir.dt.from_np(_np.dtype(dtype))
        args.append(nc.dram_tensor(f"out_{i}_dram", shape, dt, kind="ExternalOutput").ap())
    build(nc, *args)
    r = _run(nc, [arrays], core_ids=[0])
    return r.results[0]["out_0_dram"]
```

```python
from contextlib import ExitStack

import concourse.bass as bass
from concourse import mybir
from concourse.alu_op_type import AluOpType as ALU

F32 = mybir.dt.float32
BF16 = mybir.dt.bfloat16
F16 = mybir.dt.float16
I32 = mybir.dt.int32
ACT = mybir.ActivationFunctionType
AX = mybir.AxisListType

P = 128
N = 3125
E = 53125
D = 256
T = 125
NT = N // T
G = 5
NG = NT // G
F1, F2 = 64, 32
EC = E // T
WD = 5
NQ = T // WD
NW = NT * NQ
CH = P
WC = WD * NT
WB = 4
NC = -(-NQ // WB)
MAX_ROUNDS = -(-E // CH)
NX = 8
H = 512
KD, KH = D // P, H // P
NB = (2 * N + NX * (P - 1)) // P
EPS = 1e-5
MAGIC = 12582912.0
BIG = 3.0e38


def build(nc, x, src, dst, gnn_w, gW1, gW2, gW3, gamma, beta, Wr, br, W1, b1, W2, b2, out):
    ctx = ExitStack()
    with ctx:
        def sb(name, shape, dt, where=ctx):
            return where.enter_context(nc.sbuf_tensor(name, shape, dt))

        def sem(name):
            return ctx.enter_context(nc.semaphore(name))

        def ds(start, size):
            return bass.DynSlice(start, size)

        key_dram = nc.dram_tensor("edge_key", [E], F32, kind="Internal").ap()
        kl_dram = nc.dram_tensor("edge_key_lo", [E + CH, 2], F32, kind="Internal").ap()
        tok_dram = nc.dram_tensor("token_rows", [N, D], F32, kind="Internal").ap()
        pair_dram = nc.dram_tensor("pair_rows", [2 * N + NB * P, D], F32, kind="Internal").ap()

        res = sb("res", [T, NT, D], F32)
        z = sb("z", [T, NT, F1], F32)
        w1_sb = sb("w1_sb", [P, NX, KD, H], F32)
        w2_sb = sb("w2_sb", [P, NX, KH, D], F32)
        ident = sb("ident", [P, P], F32)
        ident16 = sb("ident16", [P, P], BF16)
        iota = sb("iota", [P, P], F32)
        count_up = sb("count_up", [P, P, NQ], BF16)
        part = sb("part", [P, 1], F32)
        later = sb("later", [P, P], BF16)
        ones16 = sb("ones16", [P, P], BF16)
        ones = sb("ones", [P, P], F32)
        eps = sb("eps", [P, 1], F32)
        zeros16 = sb("zeros16", [1, 512], BF16)
        gW1T = sb("gW1T", [P, KD, F1], F32)
        gW2T = sb("gW2T", [F1, F2], F32)
        gW3T = sb("gW3T", [F2, D], F32)
        wr_sb = sb("wr_sb", [P, KD, NX], F32)
        w_sb = sb("w_sb", [P, 1], F32)
        tile1 = sb("tile1", [T, NT], F32)
        ex_m8 = sb("ex_m8", [T, NT, NX], F32)
        logit = sb("logit", [T, NT, NX], F32)
        wgt = sb("wgt", [T, NT, 2], F32)
        thr = sb("thr", [T, NG], F32)
        rounds_f = sb("rounds_f", [1, 4], F32)
        rounds_i = sb("rounds_i", [1, 1], I32)

        psum = ctx.enter_context(nc.psum_tensor("psum", [P, 8, 512], F32))
        acc = psum[:, 0:4, :].rearrange("p b c -> p (b c)")

        L = {n: sem("load_" + n) for n in ("edges", "nextrow", "small", "few", "bcast", "experts")}
        x_in = [sem(f"load_x{g}") for g in range(NG)]
        c_pool, c_dve, c_pe = sem("const_pool"), sem("const_dve"), sem("const_pe")
        c_act, c_more = sem("const_act"), sem("const_more")
        link_dve, link_round, link_late = sem("link_dve"), sem("link_round"), sem("link_late")
        link_affine = sem("link_affine")
        key_stored, kl_stored = sem("key_stored"), sem("kl_stored")
        e_dve, e_pe, row_got = sem("e_dve"), sem("e_pe"), sem("row_got")
        idx_ready, got_key = sem("idx_ready"), sem("got_key")
        rounds_ready = sem("rounds_ready")
        xn_ready, var_ready, std_ready, zhi, zrest, zmid = (
            sem(n) for n in ("xn_ready", "var_ready", "std_ready", "zhi", "zrest", "zmid"))
        xnT_psum, xnT_sb, z_psum, z_sb = sem("xnT_psum"), sem("xnT_sb"), sem("z_psum"), sem("z_sb")
        res_ready, zsplit = sem("res_ready"), sem("zsplit")
        key_rel, keyT_psum, keyT_sb = sem("key_rel"), sem("keyT_psum"), sem("keyT_sb")
        onehots, win_psum, win_sb = sem("onehots"), sem("win_psum"), sem("win_sb")
        at_psum, at_dve, at_act, applied = sem("at_psum"), sem("at_dve"), sem("at_act"), sem("applied")
        y_ready, yT_psum, yT_sb = sem("y_ready"), sem("yT_psum"), sem("yT_sb")
        h2_psum, h2_sb, h3_psum = sem("h2_psum"), sem("h2_sb"), sem("h3_psum")
        var2, std2, tok_norm, tok_ready = [sem("var2a"), sem("var2b")], [sem("std2a"), sem("std2b")], sem("tok_norm"), sem("tok_ready")
        h3_used = sem("h3_used")
        tok_stored, tokT_psum, tokT_sb = [sem(f"tok_stored{i}") for i in range(3)], sem("tokT_psum"), sem("tokT_sb")
        logit_psum, logit_sb = sem("logit_psum"), sem("logit_sb")
        r_dve, r_pe, r_act = sem("r_dve"), sem("r_pe"), sem("r_act")
        pair_oh, pair_mm = sem("pair_oh"), sem("pair_mm")
        slots_ready, gcol_ready, scol_ready = sem("slots_ready"), sem("gcol_ready"), sem("scol_ready")
        xg_in = [sem(f"xg_in{i}") for i in range(4)]
        xgT_psum, xgT_sb, up_psum, up_sb = sem("xgT_psum"), sem("xgT_sb"), sem("up_psum"), sem("up_sb")
        gelu_sb, hT_psum, hT_sb = sem("gelu_sb"), sem("hT_psum"), sem("hT_sb")
        down_psum, down_sb = sem("down_psum"), sem("down_sb")
        scattered = [sem(f"scattered{i}") for i in range(4)]
        fin_in = [sem(f"fin_in{i}") for i in range(5)]
        fin_half, fin_done, out_stored = sem("fin_half"), sem("fin_done"), sem("out_stored")

        early = ExitStack()
        start_f = sb("start_f", [T, NG], F32, early)
        start_i = sb("start_i", [T, NG], I32, early)
        gath = sb("gath", [T, NG, CH, 2], F32, early)
        keyT = sb("keyT", [P, 2, NW], BF16, early)
        xn = sb("xn", [T, 2, G, D], F32, early)
        stats = sb("stats", [T, NT, 6], F32, early)
        mv = sb("mv", [T, NT, 2], F32, early)
        std = sb("std", [T, NT], F32, early)
        rstd = sb("rstd", [T, NT], F32, early)
        xnT = sb("xnT", [P, G, KD, T], F32, early)
        zres = sb("zres", [T, NT, F1], F32, early)
        z3 = sb("z3", [T, NT, 3, F1], BF16, early)
        gW1_sb = sb("gW1_sb", [F1, D], F32, early)
        gW2_sb = sb("gW2_sb", [F2, F1], F32, early)
        gW3_sb = sb("gW3_sb", [P, 2, F2], F32, early)
        at = sb("at", [T, G, G * P], BF16, early)
        prep = ExitStack()
        edge_i = sb("edge_i", [T, 2, EC], I32, prep)
        next_i = sb("next_i", [T, 1], I32, prep)
        edge_f = sb("edge_f", [T, 2, EC], F32, prep)
        next_f = sb("next_f", [T, 1], F32, prep)
        hi_f = sb("hi_f", [T, EC], F32, prep)
        key_f = sb("key_f", [T, EC], F32, prep)
        kl_f = sb("kl_f", [T, EC, 2], F32, prep)
        inv = sb("inv", [T, 3], F32, prep)
        pad = sb("pad", [1, 2 * CH], F32, prep)
        cnt = sb("cnt", [T, 4, NG], F32, prep)
        row_i = sb("row_i", [T, NG], I32, prep)
        rows = sb("rows", [T, NG, EC], F32, prep)
        junk = sb("junk", [T, EC], F32, prep)
        flag = sb("flag", [P, 2], F32, prep)
        start_row = sb("start_row", [1, NW + 1], F32, prep)
        size_row = sb("size_row", [1, NW], F32, prep)
        prep.close()
        oh_col = sb("oh_col", [P, 2, WC, NQ], BF16, early)
        oh_lo = sb("oh_lo", [P, 2, P, NQ], BF16, early)
        cts = sb("cts", [P, 2, NT, T], BF16, early)
        early.close()

        lt = ExitStack()
        b1_sb = sb("b1_sb", [P, NX, H], F32, lt)
        b2_sb = sb("b2_sb", [P, NX, D], F32, lt)
        gidx = sb("gidx", [P, NB], I32, lt)
        sidx = sb("sidx", [P, NB], I32, lt)
        ebi = sb("ebi", [1, NB], I32, lt)
        mlp = ExitStack()
        y1 = sb("y1", [T, 2, G, F1], F32, mlp)
        y1T = sb("y1T", [F1, G, T], F32, mlp)
        h2T = sb("h2T", [F2, G, T], F32, mlp)
        gam = sb("gam", [T, D], F32, mlp)
        bet = sb("bet", [T, D], F32, mlp)
        br_sb = sb("br_sb", [T, NX], F32, mlp)
        stats2 = sb("stats2", [T, 2, NT, 6], F32, mlp)
        mv2 = sb("mv2", [T, 2, NT, 2], F32, mlp)
        std_2 = sb("std_2", [T, 2, NT], F32, mlp)
        rstd2 = sb("rstd2", [T, 2, NT], F32, mlp)
        tok = sb("tok", [T, 3, G, D], F32, mlp)
        tokT = sb("tokT", [P, G, KD, T], F32, mlp)
        mlp.close()
        route = ExitStack()
        rt = [sb(f"rt{i}", [T, NT, NX], F32, route) for i in range(4)]
        mask = sb("mask", [T, 2, NT, NX], F32, route)
        sel = sb("sel", [T, NT, NX], BF16, route)
        top = sb("top", [T, 4, NT], F32, route)
        tot = sb("tot", [P, NX, NT], F32, route)
        blk = sb("blk", [P, 4, NX], F32, route)
        pos = sb("pos", [T, 2, NT], F32, route)
        pblk = sb("pblk", [T, 2, NT], F32, route)
        pblk16 = sb("pblk16", [T, 2, NT], BF16, route)
        plane16 = sb("plane16", [T, 2, NT], BF16, route)
        tile16 = sb("tile16", [T, NT], BF16, route)
        pairno16 = sb("pairno16", [T, 2, NT], BF16, route)
        oh_lane = sb("oh_lane", [T, 2, P, NT], BF16, route)
        oh_blk = sb("oh_blk", [T, 2, NB, NT], BF16, route)
        oh_val = sb("oh_val", [T, 2, 2, NB, NT], BF16, route)
        slot = sb("slot", [P, 6, NB], F32, route)
        lane_no = sb("lane_no", [P, 1], F32, route)
        ebt = sb("ebt", [1, NB, NX], F32, route)
        ebf = sb("ebf", [1, NB], F32, route)
        route.close()
        gcol = sb("gcol", [P, 4], I32, lt)
        scol = sb("scol", [P, 4], I32, lt)
        xg = sb("xg", [P, 4, D], F32, lt)
        xgT = sb("xgT", [P, 2, KD, P], F32, lt)
        up = sb("up", [P, 2, H], F32, lt)
        hg = sb("hg", [P, 2, H], F32, lt)
        hT = sb("hT", [P, 2, KH, P], F32, lt)
        yb = sb("yb", [P, 4, D], F32, lt)
        fin = sb("fin", [T, 5, 2, D], F32, lt)
        lt.close()

        def chain(eng, s):
            st = {"base": 0, "n": 0}

            def done(ins):
                st["n"] += 1
                ins.then_inc(s, 1)

            def settle():
                eng.wait_ge(s, st["base"] + st["n"])

            def start(base):
                st["base"], st["n"] = base, 0

            return done, settle, start, st

        def spread(eng, to, from_, s):
            for p0, p1 in ((0, 112), (112, T)):
                eng.dma_start(to[p0:p1], from_[p0:p1]).then_inc(s, 16)

        AT_DVE = (2, 4)
        AT_ACT = (0, 1, 3)
        LAG = 4
        SET = 5

        def at_count(r, kt, g):
            mine = AT_DVE if g in AT_DVE else AT_ACT
            return (at_dve if g in AT_DVE else at_act), (r * NT + kt) * len(mine) + mine.index(g) + 2

        x_t = x.rearrange("(t p) d -> p t d", p=T)
        out_t = out.rearrange("(t p) d -> p t d", p=T)
        tok_t = tok_dram.rearrange("(t p) d -> p t d", p=T)
        pair_t = pair_dram[0:2 * N, :].rearrange("(t p k) d -> p t k d", p=T, k=2)

        block = ctx.enter_context(nc.Block())

        @block.sync
        def _(sp):
            sp.dma_start(edge_i[:, 0, :], dst.rearrange("(p c) -> p c", c=EC)).then_inc(L["edges"], 16)
            sp.dma_start(edge_i[:, 1, :], src.rearrange("(p c) -> p c", c=EC)).then_inc(L["edges"], 16)
            sp.dma_start(next_i[0:T - 1, :], dst.rearrange("(p c) -> p c", c=EC)[1:T, 0:1],
                         allow_slow_non_contiguous=True).then_inc(L["nextrow"], 16)
            sp.dma_start(gW1_sb[:], gW1).then_inc(L["small"], 16)
            sp.dma_start(gW2_sb[:], gW2).then_inc(L["small"], 16)
            sp.dma_start(gW3_sb[:], gW3.rearrange("(a p) f -> p a f", p=P)).then_inc(L["small"], 16)
            for g in range(NG):
                spread(sp, res[:, g * G:(g + 1) * G, :], x_t[:, g * G:(g + 1) * G, :], x_in[g])
            sp.dma_start(wr_sb[:], Wr.rearrange("(a p) e -> p a e", p=P)).then_inc(L["few"], 16)
            sp.dma_start(w_sb[:], gnn_w.rearrange("(a b) -> a b", a=1).broadcast_to([P, 1])).then_inc(L["few"], 16)
            sp.wait_ge(e_dve, 1)
            sp.dma_start(key_dram.rearrange("(p c) -> p c", c=EC), key_f[:]).then_inc(key_stored, 16)
            sp.wait_ge(e_dve, 2)
            sp.dma_start(kl_dram[0:E, :].rearrange("(p c) k -> p (c k)", c=EC),
                         kl_f[:].rearrange("p c k -> p (c k)")).then_inc(kl_stored, 16)
            sp.dma_start(kl_dram[E:E + CH, :].rearrange("(a c) k -> a (c k)", a=1), pad[:]).then_inc(kl_stored, 16)
            sp.wait_ge(got_key, 16 * NG)
            sp.dma_start(w1_sb[:].rearrange("p e k h -> p (e k) h"),
                         W1.rearrange("e (k p) h -> p (e k) h", p=P)).then_inc(L["experts"], 16)
            sp.dma_start(w2_sb[:].rearrange("p e k h -> p (e k) h"),
                         W2.rearrange("e (k p) h -> p (e k) h", p=P)).then_inc(L["experts"], 16)
            sp.wait_ge(y_ready, 1)
            sp.dma_start(gam[:], gamma.rearrange("(a d) -> a d", a=1).broadcast_to([T, D])).then_inc(L["bcast"], 16)
            sp.dma_start(bet[:], beta.rearrange("(a d) -> a d", a=1).broadcast_to([T, D])).then_inc(L["bcast"], 16)
            sp.dma_start(br_sb[:], br.rearrange("(a d) -> a d", a=1).broadcast_to([T, NX])).then_inc(L["bcast"], 16)
            sp.dma_start(b1_sb[:], b1.rearrange("(a e) h -> a e h", a=1).broadcast_to([P, NX, H])).then_inc(L["experts"], 16)
            sp.dma_start(b2_sb[:], b2.rearrange("(a e) h -> a e h", a=1).broadcast_to([P, NX, D])).then_inc(L["experts"], 16)
            for g in range(NG):
                sp.wait_ge(tok_ready, g + 1)
                spread(sp, tok_t[:, g * G:(g + 1) * G, :], tok[:, g % 3, :, :], tok_stored[g % 3])
            for i in range(4):
                sp.wait_ge(scattered[i], 16 * (NB // 4))

            def load_pairs(g, i):
                spread(sp, fin[:, i, :, :], pair_t[:, ds(g * G + i, 1), :, :].rearrange("p t k d -> p (t k) d"), fin_in[i])

            for i in range(G):
                load_pairs(0, i)
            with sp.Fori(1, NG) as g:
                for i in range(G):
                    sp.wait_ge(fin_done, g * G + i + 1 - G)
                    load_pairs(g, i)

        def tiles_in_pairs(eng, body):
            with eng.Fori(0, (NT - 1) // 2) as i:
                body(2 * i + 1, 1)
                body(2 * i + 2, 0)

        def all_blocks(eng, body, unrolled=8):
            for b in range(unrolled):
                body(b, b % 4)
            with eng.Fori(unrolled // 4, NB // 4 - 1) as i:
                for j in range(4):
                    body(4 * i + j, j)
            for b in range(NB - 4, NB):
                body(b, b % 4)

        def static(b):
            return isinstance(b, int)

        @block.gpsimd
        def _(pool):
            pool.iota(iota[:], pattern=[[1, P]], base=0, channel_multiplier=0,
                      allow_small_or_imprecise_dtypes=True).then_inc(c_pool, 1)
            pool.iota(part[:], pattern=[[0, 1]], base=0, channel_multiplier=1,
                      allow_small_or_imprecise_dtypes=True).then_inc(c_pool, 1)
            pool.memset(ones[:], 1.0).then_inc(c_pool, 1)
            pool.memset(eps[:], EPS).then_inc(c_pool, 1)
            pool.iota(thr[:], pattern=[[NT * T * WD, NG]], base=0, channel_multiplier=NT * WD,
                      allow_small_or_imprecise_dtypes=True).then_inc(c_pool, 1)
            pool.memset(pad[:], -1.0).then_inc(c_pool, 1)
            pool.memset(start_row[:, NW:NW + 1], float(E)).then_inc(c_pool, 1)
            pool.memset(ones16[:], 1.0).then_inc(c_more, 1)
            pool.memset(zeros16[:], 0.0).then_inc(c_more, 1)
            pool.iota(tile1[:], pattern=[[1, NT]], base=1, channel_multiplier=0,
                      allow_small_or_imprecise_dtypes=True).then_inc(c_more, 1)
            pool.iota(ex_m8[:], pattern=[[0, NT], [1, NX]], base=-NX, channel_multiplier=0,
                      allow_small_or_imprecise_dtypes=True).then_inc(c_more, 1)
            pool.iota(count_up[:], pattern=[[1, P], [0, NQ]], base=0, channel_multiplier=0,
                      allow_small_or_imprecise_dtypes=True).then_inc(c_more, 1)

            pool.wait_ge(e_dve, 4)
            pool.wait_ge(key_stored, 16)
            for g in range(NG):
                pool.indirect_dma_start(out=rows[:, g, :], out_offset=None,
                                        in_=key_dram.rearrange("(r c) -> r c", c=EC),
                                        in_offset=bass.IndirectOffsetOnAxis(ap=row_i[:, g:g + 1], axis=0)
                                        ).then_inc(row_got, 16)

            def gather_edges():
                for g in range(NG):
                    pool.indirect_dma_start(out=gath[:, g, :, :].rearrange("p c k -> p (c k)"), out_offset=None,
                                            in_=kl_dram,
                                            in_offset=bass.IndirectOffsetOnAxis(ap=start_i[:, g:g + 1], axis=0)
                                            ).then_inc(got_key, 16)

            pool.wait_ge(idx_ready, 1)
            pool.wait_ge(kl_stored, 32)
            gather_edges()
            for g in range(NG):
                grp = slice(g * G, (g + 1) * G)
                pool.wait_ge(zhi, g + 1)
                pool.tensor_tensor(zres[:, grp, :], z[:, grp, :], z3[:, grp, 0, :], ALU.subtract).then_inc(zrest, 1)
                pool.tensor_tensor(res[:, grp, :], res[:, grp, :], xn[:, g % 2, :, :], ALU.add).then_inc(res_ready, 1)
                pool.wait_ge(zmid, g + 1)
                pool.tensor_tensor(z3[:, grp, 2, :], zres[:, grp, :], z3[:, grp, 1, :], ALU.subtract).then_inc(zsplit, 1)
            pool.wait_ge(rounds_ready, 1)
            n_rounds = pool.value_load(rounds_i[0:1, 0:1], min_val=1, max_val=MAX_ROUNDS)
            with pool.Fori(0, n_rounds) as r:
                pool.wait_ge(idx_ready, r + 2)
                pool.wait_ge(keyT_psum, (r + 1) * 4)
                pool.nop(nofuse=True)
                gather_edges()

            pool.wait_ge(L["bcast"], 48)
            done, settle, start, st = chain(pool, link_affine)
            for g in range(NG):
                start(g)
                pool.wait_ge(tok_norm, g + 1)
                t_ = tok[:, g % 3, :, :]
                done(pool.tensor_tensor(t_, t_, gam[:].unsqueeze(1).broadcast_to([T, G, D]), ALU.mult))
                settle()
                pool.tensor_tensor(t_, t_, bet[:].unsqueeze(1).broadcast_to([T, G, D]), ALU.add).then_inc(tok_ready, 1)
                assert st["n"] == 1

            def gather_block(b, j):
                pool.tensor_copy(gcol[:, j:j + 1], gidx[:, ds(b, 1)]).then_inc(gcol_ready, 1)
                pool.wait_ge(gcol_ready, b + 1)
                pool.nop(nofuse=True)
                pool.indirect_dma_start(out=xg[:, j, :], out_offset=None, in_=tok_dram,
                                        in_offset=bass.IndirectOffsetOnAxis(ap=gcol[:, j:j + 1], axis=0)
                                        ).then_inc(xg_in[j], 16)

            def gather_ahead(b, j):
                pool.wait_ge(xgT_psum, b + 1)
                gather_block(b + 4, j)

            def scatter_block(b, j):
                pool.wait_ge(down_sb, b + 1)
                pool.tensor_copy(scol[:, j:j + 1], sidx[:, ds(b, 1)]).then_inc(scol_ready, 1)
                pool.wait_ge(scol_ready, b + 1)
                pool.nop(nofuse=True)
                pool.indirect_dma_start(out=pair_dram, out_offset=bass.IndirectOffsetOnAxis(ap=scol[:, j:j + 1], axis=0),
                                        in_=yb[:, j, :], in_offset=None).then_inc(scattered[j], 16)

            def block(b, j):
                if not (static(b) and b >= NB - 4):
                    gather_ahead(b, j)
                if not (static(b) and b < 2):
                    scatter_block(b - 2, (j - 2) % 4)

            pool.wait_ge(slots_ready, 1)
            for i in range(3):
                pool.wait_ge(tok_stored[i], 32 * len(range(i, NG, 3)))
            for j in range(4):
                gather_block(j, j)
            all_blocks(pool, block)
            for b in (NB - 2, NB - 1):
                scatter_block(b, b % 4)
            for j in range(4):
                pool.wait_ge(scattered[j], 16 * (NB // 4))

        @block.scalar
        def _(act):
            act.wait_ge(c_pe, 1)
            act.copy(gW1T[:].rearrange("p k f -> p (k f)"), psum[:, 7, 0:2 * F1]).then_inc(c_act, 1)
            act.copy(gW2T[:], psum[0:F1, 7, 2 * F1:2 * F1 + F2]).then_inc(c_act, 1)
            act.copy(gW3T[:], psum[0:F2, 7, 160:160 + D]).then_inc(c_act, 1)
            act.copy(rounds_f[0:1, 3:4], eps[0:1, :]).then_inc(at_act, 1)

            def deviation(g):
                act.wait_ge(var_ready, g + 1)
                act.activation(std[:, g * G:(g + 1) * G], mv[:, g * G:(g + 1) * G, 1], ACT.Sqrt,
                               bias=eps[0:T, :]).then_inc(std_ready, 1)

            deviation(0)
            for g in range(NG):
                grp = slice(g * G, (g + 1) * G)
                if g + 1 < NG:
                    deviation(g + 1)
                for t in range(G):
                    act.wait_ge(xnT_psum, g * G + t + 1)
                    act.copy(xnT[:, t, :, :].rearrange("p k n -> p (k n)"), psum[:, t, 0:2 * T]).then_inc(xnT_sb, 1)
                act.wait_ge(z_psum, g + 1)
                zp = psum[0:T, 5 + g % 2, 0:G * F1].rearrange("p (t f) -> p t f", f=F1)
                act.copy(z[:, grp, :], zp).then_inc(z_sb, 1)
                act.copy(z3[:, grp, 0, :], zp).then_inc(zhi, 1)
                act.wait_ge(zrest, g + 1)
                act.copy(z3[:, grp, 1, :], zres[:, grp, :]).then_inc(zmid, 1)

            act.wait_ge(rounds_ready, 1)
            n_rounds = act.value_load(rounds_i[0:1, 0:1], min_val=1, max_val=MAX_ROUNDS)
            with act.Fori(0, n_rounds) as r:
                def window(kt, par, c, first):
                    nd = min(WB * WD, T - c * WB * WD)
                    act.wait_ge(win_psum, 1 + r * NT * NC + kt * NC + c + 1)
                    if c == 0 and not first:
                        act.wait_ge(at_psum, r * NT * G + kt * G - 4)
                    act.copy(cts[:, par, :, WB * WD * c:WB * WD * c + nd],
                             psum[:, 4 + (par + c) % 2, 0:NT * nd].rearrange("p (d h) -> p h d", h=NT)).then_inc(win_sb, 1)

                def copy_at(kt, par, g):
                    act.wait_ge(at_psum, 1 + r * NT * G + kt * G + g + 1)
                    act.wait_ge(applied, SET + r * NT * G + (kt - 1) * G + g + 1)
                    act.copy(at[:, g, :], psum[0:T, 6 + (par + g) % 2, :].bitcast(BF16)[:, 0:G * P]).then_inc(at_act, 1)

                for c in range(NC):
                    window(0, 0, c, True)

                def tile(kt, par):
                    for c in range(NC):
                        window(kt, par, c, False)
                        if c in AT_ACT:
                            copy_at(kt - 1, 1 - par, c)

                tiles_in_pairs(act, tile)
                for g in AT_ACT:
                    copy_at(NT - 1, 0, g)
                act.wait_ge(applied, SET + (r + 1) * NT * G)
                act.wait_ge(at_psum, 1 + (r + 1) * NT * G)

            def relus(g):
                for h, (t0, t1) in enumerate(((0, 3), (3, 5))):
                    act.wait_ge(yT_psum, g * 2 + h + 1)
                    act.activation(y1T[:, t0:t1, :].rearrange("p t n -> p (t n)"), psum[0:F1, 4 + h, 0:(t1 - t0) * T],
                                   ACT.Relu).then_inc(yT_sb, 1)
                for h, (t0, t1) in enumerate(((0, 3), (3, 5))):
                    act.wait_ge(h2_psum, g * 2 + h + 1)
                    act.activation(h2T[:, t0:t1, :].rearrange("p t n -> p (t n)"), psum[0:F2, 6 + h, 0:(t1 - t0) * T],
                                   ACT.Relu).then_inc(h2_sb, 1)

            def deviation2(g, k):
                act.wait_ge(var2[k], g + 1)
                act.activation(std_2[:, k, g * G:(g + 1) * G], mv2[:, k, g * G:(g + 1) * G, 1], ACT.Sqrt,
                               bias=eps[0:T, :]).then_inc(std2[k], 1)

            def copy_tokT(g):
                for t in range(G):
                    act.wait_ge(tokT_psum, g * G + t + 1)
                    act.copy(tokT[:, t, :, :].rearrange("p k n -> p (k n)"), psum[:, 7, 0:2 * T]).then_inc(tokT_sb, 1)

            for k in range(NG + LAG):
                if k < NG:
                    relus(k)
                if 0 <= k - 1 < NG:
                    deviation2(k - 1, 0)
                if 0 <= k - 2 < NG:
                    deviation2(k - 2, 1)
                if 0 <= k - LAG < NG:
                    copy_tokT(k - LAG)

            act.wait_ge(r_dve, 1)
            act.activation(top[:, 3, :], top[:, 3, :], ACT.Exp).then_inc(r_act, 1)

            def copy_hT(b, j):
                act.wait_ge(hT_psum, b + 1)
                if not (static(b) and b < 2):
                    act.wait_ge(down_psum, b - 1)
                act.copy(hT[:, j % 2, :, :].rearrange("p k n -> p (k n)"), psum[:, 2 + j % 2, :]).then_inc(hT_sb, 1)

            def block(b, j):
                if not (static(b) and b < 1):
                    copy_hT(b - 1, (j - 1) % 4)
                act.wait_ge(up_sb, b + 1)
                if not (static(b) and b < 2):
                    act.wait_ge(hT_psum, b - 1)
                act.activation(hg[:, j % 2, :], up[:, j % 2, :], ACT.Gelu).then_inc(gelu_sb, 1)

            all_blocks(act, block)
            copy_hT(NB - 1, 3)

            with act.Fori(0, NG) as g:
                for i in range(G):
                    act.wait_ge(fin_done, g * G + i + 1)
                    spread(act, out_t[:, ds(g * G + i, 1), :], res[:, ds(g * G + i, 1), :], out_stored)
            act.wait_ge(out_stored, 32 * NT)

        @block.tensor
        def _(pe):
            pe.wait_ge(c_pool, 7)
            pe.wait_ge(c_dve, 2)
            pe.wait_ge(L["small"], 48)
            for k in range(KD):
                pe.transpose(psum[:, 7, k * F1:(k + 1) * F1], gW1_sb[:, k * P:(k + 1) * P], ident[0:F1, 0:F1])
            pe.transpose(psum[0:F1, 7, 2 * F1:2 * F1 + F2], gW2_sb[:], ident[0:F2, 0:F2])
            for k in range(KD):
                last = pe.transpose(psum[0:F2, 7, 160 + k * P:160 + (k + 1) * P], gW3_sb[:, k, :], ident[:])
            last.then_inc(c_pe, 1)
            pe.wait_ge(e_dve, 3)
            pe.matmul(psum[:, 6, 0:1], ones[0:T, :], inv[:, 2:3], start=True, stop=True)
            pe.matmul(psum[0:T, 6, P:P + T], key_f[:, 0:1].broadcast_to([T, T]), ident[0:T, 0:T],
                      start=True, stop=True).then_inc(e_pe, 1)

            pe.wait_ge(c_act, 3)
            for g in range(NG):
                for t in range(G):
                    pe.wait_ge(xn_ready, g * G + t + 1)
                    for k in range(KD):
                        last = pe.transpose(psum[:, t, k * T:(k + 1) * T], xn[:, g % 2, t, k * P:(k + 1) * P], ident[0:T, 0:T])
                    last.then_inc(xnT_psum, 1)
                if g == 1:
                    pe.wait_ge(e_dve, 4)
                for t in range(G):
                    pe.wait_ge(xnT_sb, g * G + t + 1)
                    for k in range(KD):
                        last = pe.matmul(psum[0:T, 5 + g % 2, t * F1:(t + 1) * F1], xnT[:, t, k, :], gW1T[:, k, :],
                                         start=(k == 0), stop=(k == KD - 1))
                last.then_inc(z_psum, 1)
                if g >= 1:
                    pe.wait_ge(zhi, g)
            pe.wait_ge(zhi, NG)
            pe.wait_ge(c_more, 5)
            for b in range(4):
                pe.matmul(psum[:, b, :], ones16[0:1, :], zeros16[:], start=True, stop=True).then_inc(applied, 1)
            for s_ in (applied, at_psum, win_psum):
                pe.matmul(psum[:, 5, :], ones16[0:1, :], zeros16[:], start=True, stop=True).then_inc(s_, 1)
            pe.wait_ge(e_dve, 5)
            for g in range(NG):
                last = pe.matmul(psum[0:1, 6 + g // 4, (g % 4) * T:(g % 4 + 1) * T], start_f[:, g:g + 1],
                                 ident[0:T, 0:T], start=True, stop=True)
            last.then_inc(e_pe, 1)

            pe.wait_ge(rounds_ready, 1)
            pe.wait_ge(zsplit, NG)
            n_rounds = pe.value_load(rounds_i[0:1, 0:1], min_val=1, max_val=MAX_ROUNDS)
            with pe.Fori(0, n_rounds) as r:
                pe.wait_ge(key_rel, r + 1)
                pe.wait_ge(got_key, (r + 1) * 16 * NG)
                for a in range(2):
                    for g in range(NG):
                        last = pe.transpose(psum[:, 4 + 2 * a + g // 4, (g % 4) * T:(g % 4 + 1) * T], gath[:, g, :, a],
                                            ident[0:T, 0:T])
                        if g >= 3:
                            last.then_inc(keyT_psum, 1)
                pe.wait_ge(keyT_sb, (r + 1) * 4)

                def window(kt, par, c, early):
                    if c == 0:
                        pe.wait_ge(onehots, r * NT + kt + 1)
                    if not early:
                        pe.wait_ge(win_sb, r * NT * NC + kt * NC + c - 1)
                    for q in range(c * WB, min((c + 1) * WB, NQ)):
                        last = pe.matmul(psum[:, 4 + (par + c) % 2, (q % WB) * WC:(q % WB + 1) * WC],
                                         oh_lo[:, par, :, q], oh_col[:, par, :, q], start=True, stop=True)
                    last.then_inc(win_psum, 1)

                def turn(kt, par, g, early):
                    if g == 0:
                        pe.wait_ge(win_sb, r * NT * NC + (kt + 1) * NC)
                    if not (early and g < 2):
                        pe.wait_ge(*at_count(r, kt if g >= 2 else kt - 1, (g - 2) % G))
                    bank = psum[0:T, 6 + (par + g) % 2, :].bitcast(BF16)
                    for h in range(G):
                        last = pe.transpose(bank[:, h * P:(h + 1) * P], cts[:, par, g * G + h, :], ident16[:])
                    last.then_inc(at_psum, 1)

                def apply(kt, g):
                    pe.wait_ge(*at_count(r, kt, g))
                    for h in range(G):
                        c = (g * G + h) * F1
                        for i in range(3):
                            last = pe.matmul(acc[:, c:c + F1], at[:, g, h * P:(h + 1) * P],
                                             z3[:, ds(kt, 1), i, :].rearrange("p a f -> p (a f)"),
                                             start=False, stop=True, skip_group_check=True)
                    last.then_inc(applied, 1)

                for c in range(NC):
                    window(0, 0, c, c < 2)

                def tile(kt, par):
                    for c in range(NC):
                        window(kt, par, c, False)
                        if c < G:
                            turn(kt - 1, 1 - par, c, False)
                        if 1 <= c <= G:
                            apply(kt - 1, c - 1)

                tiles_in_pairs(pe, tile)
                for g in range(G + 1):
                    if g < G:
                        turn(NT - 1, 0, g, False)
                    if g >= 1:
                        apply(NT - 1, g - 1)

            pe.wait_ge(L["few"], 32)
            halves = ((0, 3), (3, 5))

            def mlp_group(g):
                pe.wait_ge(y_ready, g + 1)
                if g >= 1:
                    pe.wait_ge(h3_used, g)
                for h, (t0, t1) in enumerate(halves):
                    for t in range(t0, t1):
                        last = pe.transpose(psum[0:F1, 4 + h, (t - t0) * T:(t - t0 + 1) * T], y1[:, g % 2, t, :], ident[0:T, 0:T])
                    last.then_inc(yT_psum, 1)
                for h, (t0, t1) in enumerate(halves):
                    pe.wait_ge(yT_sb, g * 2 + h + 1)
                    pe.matmul(psum[0:F2, 6 + h, 0:(t1 - t0) * T], gW2T[:], y1T[:, t0:t1, :].rearrange("p t n -> p (t n)"),
                              start=True, stop=True).then_inc(h2_psum, 1)
                for t in range(G):
                    pe.wait_ge(h2_sb, g * 2 + (1 if t < 3 else 2))
                    c = (t % 2) * D
                    pe.matmul(psum[0:T, 4 + t // 2, c:c + D], h2T[:, t, :], gW3T[:],
                              start=True, stop=True).then_inc(h3_psum, 1)

            def router_group(g):
                pe.wait_ge(tok_ready, g + 1)
                for t in range(G):
                    if g * G + t >= 1:
                        pe.wait_ge(tokT_sb, g * G + t)
                    for k in range(KD):
                        last = pe.transpose(psum[:, 7, k * T:(k + 1) * T], tok[:, g % 3, t, k * P:(k + 1) * P], ident[0:T, 0:T])
                    last.then_inc(tokT_psum, 1)
                if g >= 1:
                    pe.wait_ge(logit_sb, g)
                for t in range(G):
                    pe.wait_ge(tokT_sb, g * G + t + 1)
                    for k in range(KD):
                        last = pe.matmul(psum[0:T, 3, P + t * NX:P + (t + 1) * NX], tokT[:, t, k, :], wr_sb[:, k, :],
                                         start=(k == 0), stop=(k == KD - 1))
                last.then_inc(logit_psum, 1)

            for k in range(NG + LAG):
                if k < NG:
                    mlp_group(k)
                if 0 <= k - LAG < NG:
                    router_group(k - LAG)

            pe.wait_ge(r_dve, 2)
            selv = sel[:].rearrange("p t e -> p (t e)")
            pe.matmul(psum[0:T, 4, 0:NT * NX], later[0:T, 0:T], selv, start=True, stop=True)
            pe.matmul(psum[:, 5, 0:NT * NX], ones16[0:T, :], selv, start=True, stop=True).then_inc(r_pe, 1)
            pe.matmul(psum[:, 6, 0:2 * NB], ones16[0:1, :], zeros16[:, 0:2 * NB], start=True, stop=True)
            pe.wait_ge(pair_oh, 2)
            with pe.Fori(0, NT) as t:
                for k in range(2):
                    pe.matmul(psum[:, 6, 0:2 * NB], oh_lane[:, k, :, ds(t, 1)].rearrange("p l a -> p (l a)"),
                              oh_val[:, k, :, :, ds(t, 1)].rearrange("p v b a -> p (v b a)"),
                              start=False, stop=True, skip_group_check=True).then_inc(pair_mm, 1)

            pe.wait_ge(L["experts"], 64)
            pe.wait_ge(slots_ready, 1)

            def turn_x(b, j, i):
                pe.wait_ge(xg_in[j], 16 * (i + 1))
                if not (static(b) and b < 2):
                    pe.wait_ge(xgT_sb, b - 1)
                for k in range(KD):
                    last = pe.transpose(psum[:, 6 + j % 2, k * P:(k + 1) * P], xg[:, j, k * P:(k + 1) * P], ident[:])
                last.then_inc(xgT_psum, 1)

            def up_mm(b, j):
                e = pe.value_load(ebi[0:1, ds(b, 1)], min_val=0, max_val=NX - 1)
                pe.wait_ge(xgT_sb, b + 1)
                if not (static(b) and b < 2):
                    pe.wait_ge(up_sb, b - 1)
                for k in range(KD):
                    last = pe.matmul(psum[:, j % 2, :], xgT[:, j % 2, k, :], w1_sb[:, ds(e, 1), k, :].rearrange("p a h -> p (a h)"),
                                     start=(k == 0), stop=(k == KD - 1))
                last.then_inc(up_psum, 1)

            def turn_h(b, j):
                pe.wait_ge(gelu_sb, b + 1)
                if not (static(b) and b < 2):
                    pe.wait_ge(hT_sb, b - 1)
                for k in range(KH):
                    last = pe.transpose(psum[:, 2 + j % 2, k * P:(k + 1) * P], hg[:, j % 2, k * P:(k + 1) * P], ident[:])
                last.then_inc(hT_psum, 1)

            def down_mm(b, j):
                e = pe.value_load(ebi[0:1, ds(b, 1)], min_val=0, max_val=NX - 1)
                pe.wait_ge(hT_sb, b + 1)
                if not (static(b) and b < 2):
                    pe.wait_ge(down_sb, b - 1)
                for k in range(KH):
                    last = pe.matmul(psum[:, 4 + j % 2, 0:D], hT[:, j % 2, k, :], w2_sb[:, ds(e, 1), k, :].rearrange("p a h -> p (a h)"),
                                     start=(k == 0), stop=(k == KH - 1))
                last.then_inc(down_psum, 1)

            pe.wait_ge(logit_sb, NG)
            turn_x(0, 0, 0)

            def expert_step(b, j, i):
                if not (static(b) and b == NB - 1):
                    turn_x(b + 1, (j + 1) % 4, i if j < 3 else i + 1)
                up_mm(b, j)
                if not (static(b) and b < 1):
                    turn_h(b - 1, (j - 1) % 4)
                if not (static(b) and b < 2):
                    down_mm(b - 2, (j - 2) % 4)

            for b in range(8):
                expert_step(b, b % 4, b // 4)
            with pe.Fori(2, NB // 4 - 1) as i:
                for j in range(4):
                    expert_step(4 * i + j, j, i)
            for b in range(NB - 4, NB):
                expert_step(b, b % 4, b // 4)
            down_mm(NB - 2, 2)
            turn_h(NB - 1, 3)
            down_mm(NB - 1, 3)

        @block.vector
        def _(dve):
            done, settle, start, st = chain(dve, link_dve)

            def floor_of(out, in_, add, scale):
                done(dve.tensor_scalar(out, in_, add, scale, ALU.add, ALU.mult))
                settle()
                done(dve.tensor_scalar(out, out, 0.5, MAGIC, ALU.subtract, ALU.add))
                settle()
                done(dve.tensor_scalar(out, out, MAGIC, None, ALU.subtract))
                settle()

            dve.wait_ge(c_pool, 7)
            dve.tensor_scalar(ident[:], iota[:], part[:], None, ALU.is_equal).then_inc(c_dve, 1)
            dve.tensor_scalar(ident16[:], iota[:], part[:], None, ALU.is_equal).then_inc(c_dve, 1)
            dve.tensor_scalar(later[:], iota[:], part[:], None, ALU.is_gt).then_inc(c_dve, 1)
            done(dve.memset(inv[:], 0.0))
            dve.memset(cnt[:], 0.0).then_inc(at_dve, 1)

            dve.wait_ge(L["edges"], 32)
            dve.wait_ge(L["nextrow"], 16)
            done(dve.tensor_copy(edge_f[:, 1, :], edge_i[:, 1, :]))
            done(dve.tensor_copy(edge_f[:, 0, :], edge_i[:, 0, :]))
            done(dve.tensor_copy(next_f[0:T - 1, :], next_i[0:T - 1, :]))
            settle()
            floor_of(hi_f[:], edge_f[:, 1, :], 0.5, 1.0 / T)
            dve.scalar_tensor_tensor(key_f[:], edge_f[:, 0, :], float(NT), hi_f[:], ALU.mult, ALU.add).then_inc(e_dve, 1)
            done(dve.tensor_tensor(junk[0:T, 0:EC - 1], edge_f[:, 0, 0:EC - 1], edge_f[:, 0, 1:EC], ALU.is_gt))
            done(dve.scalar_tensor_tensor(kl_f[:, :, 1], hi_f[:], -float(T), edge_f[:, 1, :], ALU.mult, ALU.add))
            done(dve.tensor_tensor(inv[0:T - 1, 1:2], edge_f[0:T - 1, 0, EC - 1:EC], next_f[0:T - 1, :], ALU.is_gt))
            settle()
            done(dve.tensor_reduce(inv[:, 0:1], junk[0:T, 0:EC - 1], AX.X, ALU.add))
            dve.wait_ge(e_dve, 1)
            dve.tensor_copy(kl_f[:, :, 0], key_f[:]).then_inc(e_dve, 1)
            settle()
            dve.tensor_tensor(inv[:, 2:3], inv[:, 0:1], inv[:, 1:2], ALU.add).then_inc(e_dve, 1)

            def moments(g):
                dve.wait_ge(x_in[g], 32)
                for t in range(g * G, (g + 1) * G):
                    done(dve.bn_stats(stats[:, t, :], res[:, t, :]))
                settle()
                for t in range(g * G, (g + 1) * G):
                    last = dve.bn_aggr(mv[:, t, :], stats[:, t, :])
                last.then_inc(var_ready, 1)

            def normalise(g):
                dve.wait_ge(std_ready, g + 1)
                if g >= 2:
                    dve.wait_ge(xnT_psum, (g - 1) * G)
                    dve.wait_ge(res_ready, g - 1)
                done(dve.reciprocal(rstd[:, g * G:(g + 1) * G], std[:, g * G:(g + 1) * G]))
                settle()
                for i, t in enumerate(range(g * G, (g + 1) * G)):
                    dve.tensor_scalar(xn[:, g % 2, i, :], res[:, t, :], mv[:, t, 0:1], rstd[:, t:t + 1],
                                      ALU.subtract, ALU.mult).then_inc(xn_ready, 1)

            dve.wait_ge(e_pe, 1)
            done(dve.tensor_scalar(flag[:, 0:1], psum[:, 6, 0:1], 1.0, None, ALU.min))
            settle()
            done(dve.tensor_scalar(flag[:, 1:2], flag[:, 0:1], -1.0, 1.0, ALU.mult, ALU.add))
            for g in range(NG):
                done(dve.tensor_scalar(rows[:, g, 0:T], psum[0:T, 6, P:P + T], thr[:, g:g + 1], None,
                                       ALU.is_lt, ALU.add, accum_out=cnt[:, 0, g:g + 1]))
            settle()
            done(dve.tensor_scalar(cnt[:, 1, :], cnt[:, 0, :], -1.0, 0.0, ALU.add, ALU.max))
            settle()
            dve.tensor_copy(row_i[:], cnt[:, 1, :]).then_inc(e_dve, 1)
            moments(0)
            moments(1)
            normalise(0)
            moments(2)
            dve.wait_ge(row_got, 16 * NG)
            for g in range(NG):
                done(dve.tensor_scalar(junk[:], rows[:, g, :], thr[:, g:g + 1], None,
                                       ALU.is_lt, ALU.add, accum_out=cnt[:, 2, g:g + 1]))
                settle()
            done(dve.scalar_tensor_tensor(cnt[:, 3, :], cnt[:, 1, :], float(EC), cnt[:, 2, :], ALU.mult, ALU.add))
            settle()
            dve.tensor_scalar(start_f[:], cnt[:, 3, :], flag[0:T, 1:2], None, ALU.mult).then_inc(e_dve, 1)
            dve.wait_ge(e_dve, 5)
            dve.tensor_copy(start_i[:], start_f[:]).then_inc(idx_ready, 1)
            normalise(1)
            for g in range(2, NG):
                if g + 1 < NG:
                    moments(g + 1)
                normalise(g)

            dve.wait_ge(e_pe, 2)
            done(dve.tensor_copy(start_row[:, 0:4 * T], psum[0:1, 6, 0:4 * T]))
            done(dve.tensor_copy(start_row[:, 4 * T:NW], psum[0:1, 7, 0:T]))
            settle()
            done(dve.tensor_tensor(size_row[:], start_row[:, 1:NW + 1], start_row[:, 0:NW], ALU.subtract))
            settle()
            done(dve.tensor_reduce(rounds_f[:, 0:1], size_row[:], AX.X, ALU.max))
            settle()
            done(dve.tensor_scalar(rounds_f[:, 1:2], rounds_f[:, 0:1], flag[0:1, 1:2], None, ALU.mult))
            settle()
            done(dve.scalar_tensor_tensor(rounds_f[:, 0:1], flag[0:1, 0:1], float(E), rounds_f[:, 1:2], ALU.mult, ALU.add))
            settle()
            floor_of(rounds_f[:, 2:3], rounds_f[:, 0:1], CH - 0.5, 1.0 / CH)
            done(dve.tensor_scalar(rounds_f[:, 1:2], rounds_f[:, 2:3], 1.0, None, ALU.max))
            settle()
            dve.tensor_copy(rounds_i[:], rounds_f[:, 1:2]).then_inc(rounds_ready, 1)
            dve.wait_ge(c_more, 5)
            dve.wait_ge(rounds_ready, 1)
            n_rounds = dve.value_load(rounds_i[0:1, 0:1], min_val=1, max_val=MAX_ROUNDS)

            done, settle, start, st = chain(dve, link_round)
            with dve.Fori(0, n_rounds) as r:
                start(r)
                dve.wait_ge(got_key, (r + 1) * 16 * NG)
                dve.tensor_tensor(gath[:, :, :, 0], gath[:, :, :, 0], thr[:].unsqueeze(2).broadcast_to([T, NG, CH]),
                                  ALU.subtract).then_inc(key_rel, 1)
                done(dve.tensor_scalar(start_f[:], start_f[:], float(CH), float(E), ALU.add, ALU.min))
                settle()
                dve.tensor_copy(start_i[:], start_f[:]).then_inc(idx_ready, 1)
                for a in range(2):
                    for i, (w0, w1) in enumerate(((0, 4 * T), (4 * T, NW))):
                        dve.wait_ge(keyT_psum, r * 4 + 2 * a + i + 1)
                        dve.tensor_copy(keyT[:, a, w0:w1], psum[:, 4 + 2 * a + i, 0:w1 - w0]).then_inc(keyT_sb, 1)
                dve.wait_ge(keyT_sb, (r + 1) * 4)

                def onehot_lo(kt, par):
                    dve.tensor_tensor(oh_lo[:, par, :, :], count_up[:],
                                      keyT[:, 1, ds(kt * NQ, NQ)].unsqueeze(1).broadcast_to([P, P, NQ]), ALU.is_equal)

                def onehot_col(kt, par):
                    dve.tensor_tensor(oh_col[:, par, :, :], count_up[:, 0:WC, :],
                                      keyT[:, 0, ds(kt * NQ, NQ)].unsqueeze(1).broadcast_to([P, WC, NQ]),
                                      ALU.is_equal).then_inc(onehots, 1)

                def copy_at(kt, par, g):
                    dve.wait_ge(at_psum, 1 + r * NT * G + kt * G + g + 1)
                    dve.wait_ge(applied, SET + r * NT * G + (kt - 1) * G + g + 1)
                    dve.tensor_copy(at[:, g, :], psum[0:T, 6 + (par + g) % 2, :].bitcast(BF16)[:, 0:G * P]).then_inc(at_dve, 1)

                for kt in range(2):
                    onehot_lo(kt, kt)
                    onehot_col(kt, kt)

                def tile(kt, par):
                    dve.wait_ge(win_psum, 1 + r * NT * NC + kt * NC)
                    onehot_lo(kt + 1, 1 - par)
                    copy_at(kt - 1, 1 - par, AT_DVE[0])
                    onehot_col(kt + 1, 1 - par)
                    copy_at(kt - 1, 1 - par, AT_DVE[1])

                with dve.Fori(0, (NT - 1) // 2 - 1) as i:
                    tile(2 * i + 1, 1)
                    tile(2 * i + 2, 0)
                tile(NT - 2, 1)
                for kt, par in ((NT - 2, 1), (NT - 1, 0)):
                    for g in AT_DVE:
                        copy_at(kt, par, g)
                dve.wait_ge(win_psum, 1 + (r + 1) * NT * NC)
                dve.wait_ge(applied, SET + (r + 1) * NT * G)
                assert st["n"] == 1, st["n"]

            dve.wait_ge(got_key, (n_rounds + 1) * 16 * NG)
            done, settle, start, st = chain(dve, link_late)
            dve.wait_ge(L["few"], 32)

            def y_group(g):
                if g >= 2:
                    dve.wait_ge(yT_psum, 2 * (g - 1))
                dve.scalar_tensor_tensor(y1[:, g % 2, :, :].rearrange("p t f -> p (t f)"),
                                         z[:, g * G:(g + 1) * G, :].rearrange("p t f -> p (t f)"), w_sb[0:T, :],
                                         acc[0:T, g * G * F1:(g + 1) * G * F1], ALU.mult, ALU.add).then_inc(y_ready, 1)

            def residual_group(g):
                for t in range(G):
                    dve.wait_ge(h3_psum, g * G + min(t | 1, G - 1) + 1)
                    c = (t % 2) * D
                    last = dve.scalar_tensor_tensor(res[:, g * G + t, :], psum[0:T, 4 + t // 2, c:c + D], 0.0,
                                                    res[:, g * G + t, :], ALU.max, ALU.add)
                last.then_inc(h3_used, 1)
                dve.wait_ge(h3_used, g + 1)

            def source(g, k, t):
                return res[:, g * G + t, :] if k == 0 else tok[:, g % 3, t, :]

            def moments2(g, k):
                for t in range(G):
                    done(dve.bn_stats(stats2[:, k, g * G + t, :], source(g, k, t)))
                settle()
                for t in range(G):
                    last = dve.bn_aggr(mv2[:, k, g * G + t, :], stats2[:, k, g * G + t, :])
                last.then_inc(var2[k], 1)

            def normalise2(g, k):
                dve.wait_ge(std2[k], g + 1)
                if k == 0 and g >= 3:
                    dve.wait_ge(tok_stored[g % 3], 32 * (g // 3))
                    dve.wait_ge(tokT_psum, (g - 2) * G)
                done(dve.reciprocal(rstd2[:, k, g * G:(g + 1) * G], std_2[:, k, g * G:(g + 1) * G]))
                settle()
                for t in range(G):
                    i = g * G + t
                    last = dve.tensor_scalar(tok[:, g % 3, t, :], source(g, k, t), mv2[:, k, i, 0:1], rstd2[:, k, i:i + 1],
                                             ALU.subtract, ALU.mult)
                    if k == 0:
                        done(last)
                if k == 0:
                    settle()
                else:
                    last.then_inc(tok_norm, 1)

            def logit_group(g):
                dve.wait_ge(logit_psum, g + 1)
                dve.tensor_tensor(logit[:, g * G:(g + 1) * G, :], psum[0:T, 3, P:P + G * NX].rearrange("p (t e) -> p t e", e=NX),
                                  br_sb[:].unsqueeze(1).broadcast_to([T, G, NX]), ALU.add).then_inc(logit_sb, 1)

            for k in range(NG + LAG):
                if k < NG:
                    y_group(k)
                if 0 <= k - 2 < NG:
                    normalise2(k - 2, 0)
                    moments2(k - 2, 1)
                if 0 <= k - 1 < NG:
                    residual_group(k - 1)
                    moments2(k - 1, 0)
                if 0 <= k - 3 < NG:
                    normalise2(k - 3, 1)
                if k == 2:
                    dve.wait_ge(L["bcast"], 48)
                if 0 <= k - LAG < NG:
                    logit_group(k - LAG)
            dve.wait_ge(logit_sb, NG)
            for i in range(3):
                dve.wait_ge(tok_stored[i], 32 * len(range(i, NG, 3)))

            def over_experts(v):
                return v.unsqueeze(2).broadcast_to([T, NT, NX])

            def largest(k, v, m, a):
                done(dve.tensor_reduce(m, v, AX.X, ALU.max))
                settle()
                done(dve.tensor_tensor(rt[0][:], v, over_experts(m), ALU.is_equal))
                settle()
                done(dve.tensor_tensor(rt[1][:], rt[0][:], ex_m8[:], ALU.mult))
                settle()
                done(dve.tensor_reduce(a, rt[1][:], AX.X, ALU.min))
                settle()
                done(dve.tensor_tensor(mask[:, k, :, :], ex_m8[:], over_experts(a), ALU.is_equal))
                settle()

            largest(0, logit[:], top[:, 0, :], top[:, 1, :])
            done(dve.scalar_tensor_tensor(rt[2][:].rearrange("p t e -> p (t e)"), mask[:, 0, :, :].rearrange("p t e -> p (t e)"),
                                          -BIG, logit[:].rearrange("p t e -> p (t e)"), ALU.mult, ALU.add))
            settle()
            largest(1, rt[2][:], top[:, 2, :], top[:, 1, :])
            dve.tensor_tensor(top[:, 3, :], top[:, 2, :], top[:, 0, :], ALU.subtract).then_inc(r_dve, 1)
            dve.tensor_tensor(sel[:], mask[:, 0, :, :], mask[:, 1, :, :], ALU.add).then_inc(r_dve, 1)
            dve.wait_ge(r_act, 1)
            done(dve.tensor_scalar(top[:, 0, :], top[:, 3, :], 1.0, None, ALU.add))
            settle()
            done(dve.reciprocal(wgt[:, :, 0], top[:, 0, :]))
            settle()
            done(dve.tensor_tensor(wgt[:, :, 1], wgt[:, :, 0], top[:, 3, :], ALU.mult))
            dve.wait_ge(r_pe, 1)
            total = psum[:, 5, 0:NT * NX].rearrange("p (t e) -> p t e", e=NX)
            for e in range(NX):
                done(dve.tensor_tensor_scan(tot[:, e, :], ones[:, 0:NT], total[:, :, e], 0.0, ALU.mult, ALU.add))
            settle()
            floor_of(blk[:, 0, :], tot[:, :, NT - 1], P - 0.5, 1.0 / P)
            done(dve.tensor_tensor_scan(blk[:, 1, :], ones[:, 0:NX], blk[:, 0, :], 0.0, ALU.mult, ALU.add))
            settle()
            done(dve.tensor_tensor(blk[:, 2, :], blk[:, 1, :], blk[:, 0, :], ALU.subtract))
            settle()
            done(dve.tensor_scalar(blk[:, 3, :], blk[:, 2, :], float(P), None, ALU.mult))
            done(dve.tensor_tensor(rt[3][:], psum[0:T, 4, 0:NT * NX].rearrange("p (t e) -> p t e", e=NX),
                                   tot[0:T, :, :].rearrange("p e t -> p t e"), ALU.add))
            settle()
            done(dve.tensor_tensor(rt[2][:], rt[3][:], total[0:T], ALU.subtract))
            settle()
            done(dve.tensor_tensor(rt[3][:], rt[2][:], blk[0:T, 3, :].unsqueeze(1).broadcast_to([T, NT, NX]), ALU.add))
            settle()
            for k in range(2):
                done(dve.tensor_tensor(rt[k][:], mask[:, k, :, :], rt[3][:], ALU.mult))
                settle()
                done(dve.tensor_reduce(pos[:, k, :], rt[k][:], AX.X, ALU.add))
                done(dve.tensor_scalar(lane_no[0:T, :] if k == 0 else top[:, 1, 0:1], part[0:T, :], 2.0, float(k), ALU.mult, ALU.add))
            settle()
            floor_of(pblk[:], pos[:], 0.5, 1.0 / P)
            done(dve.tensor_copy(pblk16[:], pblk[:]))
            done(dve.tensor_copy(tile16[:], tile1[:]))
            for k in range(2):
                done(dve.tensor_scalar(pairno16[:, k, :], ones[0:T, 0:NT], lane_no[0:T, :] if k == 0 else top[:, 1, 0:1], None,
                                       ALU.mult))
            done(dve.scalar_tensor_tensor(plane16[:].rearrange("p k t -> p (k t)"), pblk[:].rearrange("p k t -> p (k t)"),
                                          -float(P), pos[:].rearrange("p k t -> p (k t)"), ALU.mult, ALU.add))
            done(dve.tensor_tensor(ebt[:], iota[0:1, 0:NB].unsqueeze(2).broadcast_to([1, NB, NX]),
                                   blk[0:1, 1, :].unsqueeze(1).broadcast_to([1, NB, NX]), ALU.is_ge))
            settle()
            done(dve.tensor_reduce(ebf[:], ebt[:], AX.X, ALU.add))
            settle()
            done(dve.tensor_scalar(ebi[:], ebf[:], float(NX - 1), None, ALU.min))
            settle()
            for k in range(2):
                def over(v, n):
                    return v.unsqueeze(1).broadcast_to([T, n, NT])

                done(dve.tensor_tensor(oh_lane[:, k, :, :], count_up[0:T, :, :], over(plane16[:, k, :], P), ALU.is_equal))
                done(dve.tensor_tensor(oh_blk[:, k, :, :], count_up[0:T, 0:NB, :], over(pblk16[:, k, :], NB), ALU.is_equal))
                settle()
                done(dve.tensor_tensor(oh_val[:, k, 0, :, :], oh_blk[:, k, :, :], over(tile16[:], NB), ALU.mult))
                dve.tensor_tensor(oh_val[:, k, 1, :, :], oh_blk[:, k, :, :], over(pairno16[:, k, :], NB),
                                  ALU.mult).then_inc(pair_oh, 1)
            dve.wait_ge(pair_mm, 2 * NT)
            done(dve.tensor_copy(slot[:, 0, :], psum[:, 6, 0:NB]))
            done(dve.tensor_copy(slot[:, 1, :], psum[:, 6, NB:2 * NB]))
            settle()
            floor_of(slot[:, 2, :], slot[:, 1, :], 0.5, 0.5)
            done(dve.scalar_tensor_tensor(slot[:, 3, :], slot[:, 0, :], float(T), slot[:, 2, :], ALU.mult, ALU.add))
            done(dve.scalar_tensor_tensor(slot[:, 4, :], slot[:, 0, :], float(2 * T), slot[:, 1, :], ALU.mult, ALU.add))
            settle()
            done(dve.tensor_scalar(gidx[:], slot[:, 3, :], -float(T), 0.0, ALU.add, ALU.max))
            done(dve.tensor_scalar(slot[:, 5, :], slot[:, 0, :], 0.0, None, ALU.is_equal))
            done(dve.tensor_scalar(lane_no[:], part[:], float(2 * N + 2 * T), None, ALU.add))
            settle()
            done(dve.tensor_scalar(slot[:, 2, :], iota[:, 0:NB], float(P), lane_no[:], ALU.mult, ALU.add))
            settle()
            done(dve.tensor_tensor(slot[:, 3, :], slot[:, 5, :], slot[:, 2, :], ALU.mult))
            settle()
            done(dve.scalar_tensor_tensor(sidx[:], slot[:, 4, :], -float(2 * T), slot[:, 3, :], ALU.add, ALU.add))
            settle()
            dve.engine_nop().then_inc(slots_ready, 1)

            dve.wait_ge(L["experts"], 64)

            def copy_x(b, j):
                dve.wait_ge(xgT_psum, b + 1)
                if not (static(b) and b < 2):
                    dve.wait_ge(up_psum, b - 1)
                dve.tensor_copy(xgT[:, j % 2, :, :].rearrange("p k n -> p (k n)"), psum[:, 6 + j % 2, 0:D]).then_inc(xgT_sb, 1)

            def add_b1(b, j):
                e = dve.value_load(ebi[0:1, ds(b, 1)], min_val=0, max_val=NX - 1)
                dve.wait_ge(up_psum, b + 1)
                if not (static(b) and b < 2):
                    dve.wait_ge(gelu_sb, b - 1)
                dve.tensor_tensor(up[:, j % 2, :], psum[:, j % 2, :], b1_sb[:, ds(e, 1), :].rearrange("p a h -> p (a h)"),
                                  ALU.add).then_inc(up_sb, 1)

            def add_b2(b, j, i):
                e = dve.value_load(ebi[0:1, ds(b, 1)], min_val=0, max_val=NX - 1)
                dve.wait_ge(down_psum, b + 1)
                if not (static(b) and b < 4):
                    dve.wait_ge(scattered[j], 16 * i)
                dve.tensor_tensor(yb[:, j, :], psum[:, 4 + j % 2, 0:D], b2_sb[:, ds(e, 1), :].rearrange("p a h -> p (a h)"),
                                  ALU.add).then_inc(down_sb, 1)

            def expert_step(b, j, i):
                if not (static(b) and b == NB - 1):
                    copy_x(b + 1, (j + 1) % 4)
                add_b1(b, j)
                if not (static(b) and b < 2):
                    add_b2(b - 2, (j - 2) % 4, i if j >= 2 else i - 1)

            copy_x(0, 0)
            for b in range(8):
                expert_step(b, b % 4, b // 4)
            with dve.Fori(2, NB // 4 - 1) as i:
                for j in range(4):
                    expert_step(4 * i + j, j, i)
            for b in range(NB - 4, NB):
                expert_step(b, b % 4, b // 4)
            add_b2(NB - 2, 2, NB // 4 - 1)
            add_b2(NB - 1, 3, NB // 4 - 1)

            with dve.Fori(0, NG) as g:
                for i in range(G):
                    t = g * G + i
                    r_ = res[:, ds(t, 1), :].rearrange("p a d -> p (a d)")
                    dve.wait_ge(fin_in[i], (g + 1) * 32)
                    dve.scalar_tensor_tensor(r_, fin[:, i, 0, :], wgt[:, ds(t, 1), 0], r_, ALU.mult, ALU.add).then_inc(fin_half, 1)
                    dve.wait_ge(fin_half, t + 1)
                    dve.scalar_tensor_tensor(r_, fin[:, i, 1, :], wgt[:, ds(t, 1), 1], r_, ALU.mult, ALU.add).then_inc(fin_done, 1)


_INS = ['x', 'src', 'dst', 'L0_gnn_w', 'L0_gnn_W1', 'L0_gnn_W2', 'L0_gnn_W3', 'L0_ffn_gamma', 'L0_ffn_beta',
        'L0_ffn_Wr', 'L0_ffn_br', 'L0_ffn_W1', 'L0_ffn_b1', 'L0_ffn_W2', 'L0_ffn_b2']
_OUTS = [((N, D), 'float32')]


def kernel(**inputs):
    import numpy as _np
    import concourse.bacc as _bacc
    from concourse import mybir as _mybir
    from concourse.bass_utils import run_bass_kernel_spmd as _run

    nc = _bacc.Bacc("TRN2", target_bir_lowering=False, num_devices=1)
    arrays, args = {}, []
    for name in _INS:
        a = _np.ascontiguousarray(inputs[name])
        arrays[f"in_{name}_dram"] = a
        args.append(nc.dram_tensor(f"in_{name}_dram", a.shape, _mybir.dt.from_np(a.dtype), kind="ExternalInput").ap())
    for i, (shape, dtype) in enumerate(_OUTS):
        dt = _mybir.dt.from_np(_np.dtype(dtype))
        args.append(nc.dram_tensor(f"out_{i}_dram", shape, dt, kind="ExternalOutput").ap())
    build(nc, *args)
    r = _run(nc, [arrays], core_ids=[0])
    return r.results[0]["out_0_dram"]
```

```python
from contextlib import ExitStack

import concourse.bass as bass
from concourse import mybir
from concourse.alu_op_type import AluOpType as ALU

F32 = mybir.dt.float32
BF16 = mybir.dt.bfloat16
I32 = mybir.dt.int32
ACT = mybir.ActivationFunctionType
AX = mybir.AxisListType

P = 128
N = 3125
E = 53125
D = 256
T = 125
NT = N // T
G = 5
NG = NT // G
F1, F2 = 64, 32
EC = E // T
WD = 5
NQ = T // WD
NW = NT * NQ
CH = P
WC = WD * NT
WB = 4
NC = -(-NQ // WB)
MAX_ROUNDS = -(-E // CH)
NX = 8
H = 512
KD, KH = D // P, H // P
NB = (2 * N + NX * (P - 1)) // P
MIN_QUADS = -(-(-(-2 * N // P)) // 4)
MAX_QUADS = NB // 4
EPS = 1e-5
MAGIC = 12582912.0
BIG = 3.0e38


def build(nc, x, src, dst, gnn_w, gW1, gW2, gW3, gamma, beta, Wr, br, W1, b1, W2, b2, out):
    ctx = ExitStack()
    with ctx:
        def sb(name, shape, dt, where=ctx):
            return where.enter_context(nc.sbuf_tensor(name, shape, dt))

        def sem(name):
            return ctx.enter_context(nc.semaphore(name))

        def ds(start, size):
            return bass.DynSlice(start, size)

        key_dram = nc.dram_tensor("edge_key", [E], F32, kind="Internal").ap()
        kl_dram = nc.dram_tensor("edge_key_lo", [E + CH, 2], F32, kind="Internal").ap()
        tok_dram = nc.dram_tensor("token_rows", [N, D], F32, kind="Internal").ap()
        pair_dram = nc.dram_tensor("pair_rows", [2 * N + NB * P, D], F32, kind="Internal").ap()

        res = sb("res", [T, NT, D], F32)
        z = sb("z", [T, NT, F1], F32)
        w1_sb = sb("w1_sb", [P, NX, KD, H], F32)
        w2_sb = sb("w2_sb", [P, NX, KH, D], F32)
        ident = sb("ident", [P, P], F32)
        ident16 = sb("ident16", [P, P], BF16)
        iota = sb("iota", [P, P], F32)
        count_up = sb("count_up", [P, P, NQ], BF16)
        part = sb("part", [P, 1], F32)
        later = sb("later", [P, P], BF16)
        ones16 = sb("ones16", [P, P], BF16)
        ones = sb("ones", [P, P], F32)
        eps = sb("eps", [P, 1], F32)
        eps2 = sb("eps2", [P, 1], F32)
        zeros16 = sb("zeros16", [1, 512], BF16)
        b1_rows = sb("b1_rows", [NX * KH, P], F32)
        b1T = sb("b1T", [P, NX, KH], F32)
        gW1T = sb("gW1T", [P, KD, F1], F32)
        gW2T = sb("gW2T", [F1, F2], F32)
        gW3T = sb("gW3T", [P, D], F32)
        h2T = sb("h2T", [P, G, T], F32)
        wr_sb = sb("wr_sb", [P, KD, NX], F32)
        w_sb = sb("w_sb", [P, 1], F32)
        tile1 = sb("tile1", [T, NT], F32)
        ex_m8 = sb("ex_m8", [T, NT, NX], F32)
        logit = sb("logit", [T, NT, NX], F32)
        wgt = sb("wgt", [T, NT, 2], F32)
        thr = sb("thr", [T, NG], F32)
        rounds_f = sb("rounds_f", [1, 4], F32)
        rounds_i = sb("rounds_i", [1, 1], I32)

        psum = ctx.enter_context(nc.psum_tensor("psum", [P, 8, 512], F32))
        acc = psum[:, 0:4, :].rearrange("p b c -> p (b c)")

        L = {n: sem("load_" + n) for n in ("edges", "nextrow", "small", "few", "bcast", "experts")}
        x_in = [sem(f"load_x{g}") for g in range(NG)]
        c_pool, c_dve, c_pe = sem("const_pool"), sem("const_dve"), sem("const_pe")
        c_act, c_more = sem("const_act"), sem("const_more")
        link_dve, link_round, link_late = sem("link_dve"), sem("link_round"), sem("link_late")
        link_affine = sem("link_affine")
        key_stored, kl_stored = sem("key_stored"), sem("kl_stored")
        e_dve, e_pe, row_got = sem("e_dve"), sem("e_pe"), sem("row_got")
        idx_ready, got_key = sem("idx_ready"), sem("got_key")
        rounds_ready = sem("rounds_ready")
        xn_ready, var_ready, std_ready, zhi, zrest, zmid = (
            sem(n) for n in ("xn_ready", "var_ready", "std_ready", "zhi", "zrest", "zmid"))
        xnT_psum, xnT_sb, z_psum, z_sb = sem("xnT_psum"), sem("xnT_sb"), sem("z_psum"), sem("z_sb")
        res_ready, zsplit = sem("res_ready"), sem("zsplit")
        key_rel, keyT_psum, keyT_sb = sem("key_rel"), sem("keyT_psum"), sem("keyT_sb")
        onehots, win_psum, win_sb = sem("onehots"), sem("win_psum"), sem("win_sb")
        at_psum, at_dve, at_act, applied = sem("at_psum"), sem("at_dve"), sem("at_act"), sem("applied")
        y_ready, yT_psum, yT_sb = sem("y_ready"), sem("yT_psum"), sem("yT_sb")
        h2_psum, h2_sb, h3_psum = sem("h2_psum"), sem("h2_sb"), sem("h3_psum")
        tok_var, tok_std, tok_norm = sem("tok_var"), sem("tok_std"), sem("tok_norm")
        h3_used = sem("h3_used")
        tok_pool, tok_dve = sem("tok_ready_pool"), sem("tok_ready_dve")
        tok_stored, tokT_psum, tokT_sb = sem("tok_stored"), sem("tokT_psum"), sem("tokT_sb")
        logitT_psum, logitT_sb = sem("logitT_psum"), sem("logitT_sb")
        logit_psum, logit_sb = sem("logit_psum"), sem("logit_sb")
        r_dve, r_pe, r_act = sem("r_dve"), sem("r_pe"), sem("r_act")
        pair_oh, pair_mm = sem("pair_oh"), sem("pair_mm")
        slots_ready, gcol_ready, scol_ready = sem("slots_ready"), sem("gcol_ready"), sem("scol_ready")
        xg_in = [sem(f"xg_in{i}") for i in range(4)]
        xgT_psum, xgT_sb, up_psum, up_sb = sem("xgT_psum"), sem("xgT_sb"), sem("up_psum"), sem("up_sb")
        w1_copied, gelu_sb = sem("w1_copied"), sem("gelu_sb")
        down_psum, down_sb = sem("down_psum"), sem("down_sb")
        scattered = [sem(f"scattered{i}") for i in range(4)]
        fin_in = [sem(f"fin_in{g}") for g in range(NG)]
        fin_half, fin_done, out_stored = sem("fin_half"), sem("fin_done"), sem("out_stored")

        early = ExitStack()
        start_f = sb("start_f", [T, NG + 1], F32, early)
        start_i = sb("start_i", [T, NG], I32, early)
        gath = sb("gath", [T, NG, CH, 2], F32, early)
        keyT = sb("keyT", [P, 2, NW], BF16, early)
        xn = sb("xn", [T, 2, G, D], F32, early)
        stats = sb("stats", [T, NT, 6], F32, early)
        mv = sb("mv", [T, NT, 2], F32, early)
        std = sb("std", [T, NT], F32, early)
        rstd = sb("rstd", [T, NT], F32, early)
        xnT = sb("xnT", [P, G, KD, T], F32, early)
        zres = sb("zres", [T, NT, F1], F32, early)
        z3 = sb("z3", [T, NT, 3, F1], BF16, early)
        gW1_sb = sb("gW1_sb", [F1, D], F32, early)
        gW2_sb = sb("gW2_sb", [F2, F1], F32, early)
        gW3_sb = sb("gW3_sb", [P, 2, F2], F32, early)
        at = sb("at", [T, G, G * P], BF16, early)
        prep = ExitStack()
        edge_i = sb("edge_i", [T, 2, EC], I32, prep)
        next_i = sb("next_i", [T, 1], I32, prep)
        edge_f = sb("edge_f", [T, 2, EC], F32, prep)
        next_f = sb("next_f", [T, 1], F32, prep)
        hi_f = sb("hi_f", [T, EC], F32, prep)
        key_f = sb("key_f", [T, EC], F32, prep)
        kl_f = sb("kl_f", [T, EC, 2], F32, prep)
        inv = sb("inv", [T, 3], F32, prep)
        pad = sb("pad", [1, 2 * CH], F32, prep)
        cnt = sb("cnt", [T, 4, NG], F32, prep)
        row_i = sb("row_i", [T, NG], I32, prep)
        rows = sb("rows", [T, NG, EC], F32, prep)
        junk = sb("junk", [T, EC], F32, prep)
        flag = sb("flag", [P, 2], F32, prep)
        start_row = sb("start_row", [NG, T + 1], F32, prep)
        size_row = sb("size_row", [NG, T], F32, prep)
        largest_size = sb("largest_size", [NG, 1], F32, prep)
        prep.close()
        oh_col = sb("oh_col", [P, 2, WC, NQ], BF16, early)
        oh_lo = sb("oh_lo", [P, 2, P, NQ], BF16, early)
        cts = sb("cts", [P, 2, NT, T], BF16, early)
        early.close()

        lt = ExitStack()
        b2_sb = sb("b2_sb", [P, NX, D], F32, lt)
        gidx = sb("gidx", [P, NB], I32, lt)
        sidx = sb("sidx", [P, NB], I32, lt)
        ebi = sb("ebi", [1, NB], I32, lt)
        quads_i = sb("quads_i", [1, 1], I32, lt)
        tok = sb("tok", [T, NT, D], F32, lt)
        mlp = ExitStack()
        y1 = sb("y1", [T, NT, F1], F32, mlp)
        y1T = sb("y1T", [F1, G, T], F32, mlp)
        gam = sb("gam", [T, D], F32, mlp)
        bet = sb("bet", [T, D], F32, mlp)
        br_sb = sb("br_sb", [T, NX], F32, mlp)
        stats2 = sb("stats2", [T, NT, 6], F32, mlp)
        mv2 = sb("mv2", [T, NT, 2], F32, mlp)
        std_2 = sb("std_2", [T, NT], F32, mlp)
        rstd2 = sb("rstd2", [T, NT], F32, mlp)
        tokT = sb("tokT", [P, KD, G, T], F32, mlp)
        logitT = sb("logitT", [NX, G, T], F32, mlp)
        mlp.close()
        route = ExitStack()
        rt = [sb(f"rt{i}", [T, NT, NX], F32, route) for i in range(4)]
        mask = sb("mask", [T, 2, NT, NX], F32, route)
        sel = sb("sel", [T, NT, NX], BF16, route)
        top = sb("top", [T, 4, NT], F32, route)
        tot = sb("tot", [P, NX, NT], F32, route)
        blk = sb("blk", [P, 4, NX], F32, route)
        pos = sb("pos", [T, 2, NT], F32, route)
        pblk = sb("pblk", [T, 2, NT], F32, route)
        pblk16 = sb("pblk16", [T, 2, NT], BF16, route)
        plane16 = sb("plane16", [T, 2, NT], BF16, route)
        tile16 = sb("tile16", [T, NT], BF16, route)
        pairno16 = sb("pairno16", [T, 2, NT], BF16, route)
        oh_lane = sb("oh_lane", [T, 2, P, NT], BF16, route)
        oh_blk = sb("oh_blk", [T, 2, NB, NT], BF16, route)
        oh_val = sb("oh_val", [T, 2, 2, NB, NT], BF16, route)
        slot = sb("slot", [P, 6, NB], F32, route)
        pair_no = sb("pair_no", [T, 2], F32, route)
        spare_row = sb("spare_row", [P, 1], F32, route)
        quads_f = sb("quads_f", [1, 1], F32, route)
        ebt = sb("ebt", [1, NB, NX], F32, route)
        ebf = sb("ebf", [1, NB], F32, route)
        route.close()
        gcol = sb("gcol", [P, 4], I32, lt)
        scol = sb("scol", [P, 4], I32, lt)
        xg = sb("xg", [P, 4, D], F32, lt)
        xgT = sb("xgT", [P, 2, KD, P], F32, lt)
        w1_now = sb("w1_now", [P, 2, KD, H], F32, lt)
        up = sb("up", [P, 2, KH, P], F32, lt)
        hT = sb("hT", [P, 2, KH, P], F32, lt)
        yb = sb("yb", [P, 4, D], F32, lt)
        lt.close()

        def chain(eng, s):
            st = {"base": 0, "n": 0}

            def done(ins):
                st["n"] += 1
                ins.then_inc(s, 1)

            def settle():
                eng.wait_ge(s, st["base"] + st["n"])

            def start(base):
                st["base"], st["n"] = base, 0

            return done, settle, start, st

        def spread(eng, to, from_, s):
            for p0, p1 in ((0, 112), (112, T)):
                eng.dma_start(to[p0:p1], from_[p0:p1]).then_inc(s, 16)

        AT_DVE = (0, 2, 4)
        AT_ACT = (1, 3)
        LAG = 4
        H3 = (6, 7, 0)
        TURN = (1, 2)
        AFFINE_POOL = 3
        halves = ((0, 3), (3, 5))
        SET = 5

        def at_count(r, kt, g):
            mine = AT_DVE if g in AT_DVE else AT_ACT
            return (at_dve if g in AT_DVE else at_act), (r * NT + kt) * len(mine) + mine.index(g) + 2

        def tok_ready(g):
            return (tok_pool, g + 1) if g < AFFINE_POOL else (tok_dve, g + 1 - AFFINE_POOL)

        def fin(g):
            n = G * 2 * D
            flat = (w1_sb if g < 3 else w2_sb)[0:T].rearrange("p e k h -> p (e k h)")
            return flat[:, (g % 3) * n:(g % 3 + 1) * n].rearrange("p (t d) -> p t d", t=G)

        x_t = x.rearrange("(t p) d -> p t d", p=T)
        out_t = out.rearrange("(t p) d -> p t d", p=T)
        tok_t = tok_dram.rearrange("(t p) d -> p t d", p=T)
        pair_t = pair_dram[0:2 * N, :].rearrange("(t p k) d -> p t k d", p=T, k=2)

        block = ctx.enter_context(nc.Block())

        def tiles_in_pairs(eng, body):
            with eng.Fori(0, (NT - 1) // 2) as i:
                body(2 * i + 1, 1)
                body(2 * i + 2, 0)

        def middle_quads(eng):
            return eng.value_load(quads_i[0:1, 0:1], min_val=MIN_QUADS - 3, max_val=MAX_QUADS - 3)

        def all_blocks(eng, middle, body):
            for b in range(8):
                body(b, b % 4, b // 4, False)
            with eng.Fori(2, middle + 2) as i:
                for j in range(4):
                    body(4 * i + j, j, i, False)
            for j in range(4):
                body(4 * (middle + 2) + j, j, middle + 2, True)

        def static(b):
            return isinstance(b, int)

        @block.sync
        def _(sp):
            sp.dma_start(edge_i[:, 0, :], dst.rearrange("(p c) -> p c", c=EC)).then_inc(L["edges"], 16)
            sp.dma_start(edge_i[:, 1, :], src.rearrange("(p c) -> p c", c=EC)).then_inc(L["edges"], 16)
            sp.dma_start(next_i[0:T - 1, :], dst.rearrange("(p c) -> p c", c=EC)[1:T, 0:1],
                         allow_slow_non_contiguous=True).then_inc(L["nextrow"], 16)
            sp.dma_start(gW1_sb[:], gW1).then_inc(L["small"], 16)
            sp.dma_start(gW2_sb[:], gW2).then_inc(L["small"], 16)
            sp.dma_start(gW3_sb[:], gW3.rearrange("(a p) f -> p a f", p=P)).then_inc(L["small"], 16)
            sp.dma_start(b1_rows[:], b1.rearrange("e (c p) -> (e c) p", p=P)).then_inc(L["small"], 16)
            for g in range(NG):
                spread(sp, res[:, g * G:(g + 1) * G, :], x_t[:, g * G:(g + 1) * G, :], x_in[g])
            sp.dma_start(wr_sb[:], Wr.rearrange("(a p) e -> p a e", p=P)).then_inc(L["few"], 16)
            sp.dma_start(w_sb[:], gnn_w.rearrange("(a b) -> a b", a=1).broadcast_to([P, 1])).then_inc(L["few"], 16)
            sp.wait_ge(e_dve, 1)
            sp.dma_start(key_dram.rearrange("(p c) -> p c", c=EC), key_f[:]).then_inc(key_stored, 16)
            sp.wait_ge(e_dve, 2)
            sp.dma_start(kl_dram[0:E, :].rearrange("(p c) k -> p (c k)", c=EC),
                         kl_f[:].rearrange("p c k -> p (c k)")).then_inc(kl_stored, 16)
            sp.dma_start(kl_dram[E:E + CH, :].rearrange("(a c) k -> a (c k)", a=1), pad[:]).then_inc(kl_stored, 16)
            sp.wait_ge(got_key, 16 * NG)
            sp.dma_start(w1_sb[:].rearrange("p e k h -> p (e k) h"),
                         W1.rearrange("e (k p) h -> p (e k) h", p=P)).then_inc(L["experts"], 16)
            sp.dma_start(w2_sb[:].rearrange("p e k h -> p (e k) h"),
                         W2.rearrange("e (k p) h -> p (e k) h", p=P)).then_inc(L["experts"], 16)
            sp.wait_ge(res_ready, NG)
            sp.wait_ge(y_ready, 1)
            sp.dma_start(gam[:], gamma.rearrange("(a d) -> a d", a=1).broadcast_to([T, D])).then_inc(L["bcast"], 16)
            sp.dma_start(bet[:], beta.rearrange("(a d) -> a d", a=1).broadcast_to([T, D])).then_inc(L["bcast"], 16)
            sp.dma_start(br_sb[:], br.rearrange("(a d) -> a d", a=1).broadcast_to([T, NX])).then_inc(L["bcast"], 16)
            sp.dma_start(b2_sb[:], b2.rearrange("(a e) h -> a e h", a=1).broadcast_to([P, NX, D])).then_inc(L["experts"], 16)
            for g in range(NG):
                sp.wait_ge(*tok_ready(g))
                spread(sp, tok_t[:, g * G:(g + 1) * G, :], tok[:, g * G:(g + 1) * G, :], tok_stored)
            sp.wait_ge(slots_ready, 1)
            middle = middle_quads(sp)
            for i in range(4):
                sp.wait_ge(scattered[i], 16 * (middle + 3))

            for g in range(NG):
                spread(sp, fin(g), pair_t[:, g * G:(g + 1) * G, :, :].rearrange("p t k d -> p t (k d)"), fin_in[g])

        @block.gpsimd
        def _(pool):
            pool.iota(iota[:], pattern=[[1, P]], base=0, channel_multiplier=0,
                      allow_small_or_imprecise_dtypes=True).then_inc(c_pool, 1)
            pool.iota(part[:], pattern=[[0, 1]], base=0, channel_multiplier=1,
                      allow_small_or_imprecise_dtypes=True).then_inc(c_pool, 1)
            pool.memset(ones[:], 1.0).then_inc(c_pool, 1)
            pool.memset(eps[:], EPS).then_inc(c_pool, 1)
            pool.memset(eps2[:], EPS * EPS).then_inc(c_pool, 1)
            pool.iota(thr[:], pattern=[[NT * T * WD, NG]], base=0, channel_multiplier=NT * WD,
                      allow_small_or_imprecise_dtypes=True).then_inc(c_pool, 1)
            pool.memset(pad[:], -1.0).then_inc(c_pool, 1)
            pool.memset(start_f[:, NG:NG + 1], float(E)).then_inc(c_pool, 1)
            pool.memset(gW3T[:], 0.0).then_inc(c_more, 1)
            pool.memset(h2T[:].rearrange("p t n -> p (t n)"), 0.0).then_inc(c_more, 1)
            pool.memset(ones16[:], 1.0).then_inc(c_more, 1)
            pool.memset(zeros16[:], 0.0).then_inc(c_more, 1)
            pool.iota(tile1[:], pattern=[[1, NT]], base=1, channel_multiplier=0,
                      allow_small_or_imprecise_dtypes=True).then_inc(c_more, 1)
            pool.iota(ex_m8[:], pattern=[[0, NT], [1, NX]], base=-NX, channel_multiplier=0,
                      allow_small_or_imprecise_dtypes=True).then_inc(c_more, 1)
            pool.iota(count_up[:], pattern=[[1, P], [0, NQ]], base=0, channel_multiplier=0,
                      allow_small_or_imprecise_dtypes=True).then_inc(c_more, 1)

            pool.wait_ge(e_dve, 4)
            pool.wait_ge(key_stored, 16)
            for g in range(NG):
                pool.indirect_dma_start(out=rows[:, g, :], out_offset=None,
                                        in_=key_dram.rearrange("(r c) -> r c", c=EC),
                                        in_offset=bass.IndirectOffsetOnAxis(ap=row_i[:, g:g + 1], axis=0)
                                        ).then_inc(row_got, 16)

            def gather_edges():
                for g in range(NG):
                    pool.indirect_dma_start(out=gath[:, g, :, :].rearrange("p c k -> p (c k)"), out_offset=None,
                                            in_=kl_dram,
                                            in_offset=bass.IndirectOffsetOnAxis(ap=start_i[:, g:g + 1], axis=0)
                                            ).then_inc(got_key, 16)

            def add_normalised(g):
                grp = slice(g * G, (g + 1) * G)
                pool.wait_ge(xn_ready, (g + 1) * G)
                pool.tensor_tensor(res[:, grp, :], res[:, grp, :], xn[:, g % 2, :, :], ALU.add).then_inc(res_ready, 1)

            add_normalised(0)
            pool.wait_ge(idx_ready, 1)
            pool.wait_ge(kl_stored, 32)
            gather_edges()
            for g in range(1, NG):
                add_normalised(g)
            pool.wait_ge(rounds_ready, 1)
            n_rounds = pool.value_load(rounds_i[0:1, 0:1], min_val=1, max_val=MAX_ROUNDS)
            with pool.Fori(0, n_rounds) as r:
                pool.wait_ge(idx_ready, r + 2)
                pool.wait_ge(keyT_psum, (r + 1) * 4)
                pool.nop(nofuse=True)
                gather_edges()

            pool.wait_ge(L["bcast"], 48)
            done, settle, start, st = chain(pool, link_affine)
            for g in range(AFFINE_POOL):
                t_ = tok[:, g * G:(g + 1) * G, :]
                pool.wait_ge(tok_norm, g + 1)
                done(pool.tensor_tensor(t_, t_, gam[:].unsqueeze(1).broadcast_to([T, G, D]), ALU.mult))
                settle()
                pool.tensor_tensor(t_, t_, bet[:].unsqueeze(1).broadcast_to([T, G, D]), ALU.add).then_inc(tok_pool, 1)

            def gather_block(b, j):
                pool.tensor_copy(gcol[:, j:j + 1], gidx[:, ds(b, 1)]).then_inc(gcol_ready, 1)
                pool.wait_ge(gcol_ready, b + 1)
                pool.nop(nofuse=True)
                pool.indirect_dma_start(out=xg[:, j, :], out_offset=None, in_=tok_dram,
                                        in_offset=bass.IndirectOffsetOnAxis(ap=gcol[:, j:j + 1], axis=0)
                                        ).then_inc(xg_in[j], 16)

            def gather_ahead(b, j):
                pool.wait_ge(xgT_psum, b + 1)
                gather_block(b + 4, j)

            def scatter_block(b, j):
                pool.wait_ge(down_sb, b + 1)
                pool.tensor_copy(scol[:, j:j + 1], sidx[:, ds(b, 1)]).then_inc(scol_ready, 1)
                pool.wait_ge(scol_ready, b + 1)
                pool.nop(nofuse=True)
                pool.indirect_dma_start(out=pair_dram, out_offset=bass.IndirectOffsetOnAxis(ap=scol[:, j:j + 1], axis=0),
                                        in_=yb[:, j, :], in_offset=None).then_inc(scattered[j], 16)

            def block(b, j, i, last):
                if not last:
                    gather_ahead(b, j)
                if not (static(b) and b < 2):
                    scatter_block(b - 2, (j - 2) % 4)

            pool.wait_ge(slots_ready, 1)
            pool.wait_ge(tok_stored, 32 * NG)
            for j in range(4):
                gather_block(j, j)
            middle = middle_quads(pool)
            all_blocks(pool, middle, block)
            for j in (2, 3):
                scatter_block(4 * (middle + 2) + j, j)
            for j in range(4):
                pool.wait_ge(scattered[j], 16 * (middle + 3))

        @block.scalar
        def _(act):
            act.wait_ge(c_pe, 1)
            act.copy(gW1T[:].rearrange("p k f -> p (k f)"), psum[:, 7, 0:2 * F1]).then_inc(c_act, 1)
            act.copy(gW2T[:], psum[0:F1, 7, 2 * F1:2 * F1 + F2]).then_inc(c_act, 1)
            act.wait_ge(c_more, 2)
            act.copy(gW3T[0:F2, :], psum[0:F2, 7, 160:160 + D]).then_inc(c_act, 1)
            act.copy(b1T[:].rearrange("p e c -> p (e c)"), psum[:, 7, 416:416 + NX * KH]).then_inc(c_act, 1)
            act.copy(rounds_f[0:1, 3:4], eps[0:1, :]).then_inc(at_act, 1)

            def deviation(g):
                act.wait_ge(var_ready, g + 1)
                act.activation(std[:, g * G:(g + 1) * G], mv[:, g * G:(g + 1) * G, 1], ACT.Sqrt,
                               bias=eps[0:T, :]).then_inc(std_ready, 1)

            def copy_mid(g):
                act.wait_ge(zrest, g + 1)
                act.copy(z3[:, g * G:(g + 1) * G, 1, :], zres[:, g * G:(g + 1) * G, :]).then_inc(zmid, 1)

            deviation(0)
            for g in range(NG):
                grp = slice(g * G, (g + 1) * G)
                if g + 1 < NG:
                    deviation(g + 1)
                for t in range(G):
                    act.wait_ge(xnT_psum, g * G + t + 1)
                    act.copy(xnT[:, t, :, :].rearrange("p k n -> p (k n)"), psum[:, t, 0:2 * T]).then_inc(xnT_sb, 1)
                act.wait_ge(z_psum, g + 1)
                zp = psum[0:T, 5 + g % 2, 0:G * F1].rearrange("p (t f) -> p t f", f=F1)
                act.copy(z[:, grp, :], zp).then_inc(z_sb, 1)
                act.copy(z3[:, grp, 0, :], zp).then_inc(zhi, 1)
                if g >= 1:
                    copy_mid(g - 1)
            copy_mid(NG - 1)

            act.wait_ge(rounds_ready, 1)
            n_rounds = act.value_load(rounds_i[0:1, 0:1], min_val=1, max_val=MAX_ROUNDS)
            with act.Fori(0, n_rounds) as r:
                def window(kt, par, c, first):
                    nd = min(WB * WD, T - c * WB * WD)
                    act.wait_ge(win_psum, 1 + r * NT * NC + kt * NC + c + 1)
                    if c == 0 and not first:
                        act.wait_ge(at_psum, r * NT * G + kt * G - 4)
                    act.copy(cts[:, par, :, WB * WD * c:WB * WD * c + nd],
                             psum[:, 4 + (par + c) % 2, 0:NT * nd].rearrange("p (d h) -> p h d", h=NT)).then_inc(win_sb, 1)

                def copy_at(kt, par, g):
                    act.wait_ge(at_psum, 1 + r * NT * G + kt * G + g + 1)
                    act.wait_ge(applied, SET + r * NT * G + (kt - 1) * G + g + 1)
                    act.copy(at[:, g, :], psum[0:T, 6 + (par + g) % 2, :].bitcast(BF16)[:, 0:G * P]).then_inc(at_act, 1)

                for c in range(NC):
                    window(0, 0, c, True)

                def tile(kt, par):
                    for c in range(NC):
                        if c - 1 in AT_ACT:
                            copy_at(kt - 1, 1 - par, c - 1)
                        window(kt, par, c, False)

                tiles_in_pairs(act, tile)
                for g in AT_ACT:
                    copy_at(NT - 1, 0, g)
                act.wait_ge(applied, SET + (r + 1) * NT * G)
                act.wait_ge(at_psum, 1 + (r + 1) * NT * G)


            def relu_y(g):
                for h, (t0, t1) in enumerate(halves):
                    act.wait_ge(yT_psum, g * 2 + h + 1)
                    act.activation(y1T[:, t0:t1, :].rearrange("p t n -> p (t n)"), psum[0:F1, 4 + h, 0:(t1 - t0) * T],
                                   ACT.Relu).then_inc(yT_sb, 1)

            def relu_h2(g):
                for h, (t0, t1) in enumerate(halves):
                    act.wait_ge(h2_psum, g * 2 + h + 1)
                    act.activation(h2T[0:F2, t0:t1, :].rearrange("p t n -> p (t n)"), psum[0:F2, 4 + h, 0:(t1 - t0) * T],
                                   ACT.Relu).then_inc(h2_sb, 1)

            def deviation2(g):
                act.wait_ge(tok_var, g + 1)
                act.activation(std_2[:, g * G:(g + 1) * G], mv2[:, g * G:(g + 1) * G, 1], ACT.Sqrt,
                               bias=eps2[0:T, :], scale=1.0 + EPS).then_inc(tok_std, 1)

            def copy_tokT(g):
                for t in range(G):
                    act.wait_ge(tokT_psum, g * G + t + 1)
                    act.copy(tokT[:, :, t, :], psum[:, TURN[(g * G + t) % len(TURN)], 0:KD * T].rearrange(
                        "p (k n) -> p k n", k=KD)).then_inc(tokT_sb, 1)

            def copy_logitT(g):
                for h, (t0, t1) in enumerate(halves):
                    act.wait_ge(logitT_psum, g * 2 + h + 1)
                    act.copy(logitT[:, t0:t1, :].rearrange("p t n -> p (t n)"), psum[0:NX, 4 + h, 0:(t1 - t0) * T]).then_inc(logitT_sb, 1)

            relu_y(0)
            for k in range(NG + LAG):
                if k < NG:
                    relu_h2(k)
                if k + 1 < NG:
                    relu_y(k + 1)
                if 0 <= k - 1 < NG:
                    deviation2(k - 1)
                if 0 <= k - LAG < NG:
                    copy_tokT(k - LAG)
                    copy_logitT(k - LAG)

            act.wait_ge(r_dve, 1)
            act.activation(top[:, 3, :], top[:, 3, :], ACT.Exp).then_inc(r_act, 1)

            act.wait_ge(L["experts"], 48)
            act.wait_ge(slots_ready, 1)

            def copy_w1(b, j):
                e = act.value_load(ebi[0:1, ds(b, 1)], min_val=0, max_val=NX - 1)
                if not (static(b) and b < 2):
                    act.wait_ge(up_psum, b - 1)
                act.copy(w1_now[:, j % 2, :, :].rearrange("p k h -> p (k h)"),
                         w1_sb[:, ds(e, 1), :, :].rearrange("p a k h -> p (a k h)")).then_inc(w1_copied, 1)

            copy_w1(0, 0)

            def block(b, j, i, last):
                if not (last and j == 3):
                    copy_w1(b + 1, j + 1)
                act.wait_ge(up_sb, b + 1)
                if not (static(b) and b < 2):
                    act.wait_ge(down_psum, b - 1)
                act.activation(hT[:, j % 2, :, :].rearrange("p k n -> p (k n)"),
                               up[:, j % 2, :, :].rearrange("p k n -> p (k n)"), ACT.Gelu).then_inc(gelu_sb, 1)

            all_blocks(act, middle_quads(act), block)

            for g in range(NG):
                act.wait_ge(fin_done, g + 1)
                spread(act, out_t[:, g * G:(g + 1) * G, :], res[:, g * G:(g + 1) * G, :], out_stored)
            act.wait_ge(out_stored, 32 * NG)

        @block.tensor
        def _(pe):
            pe.wait_ge(c_pool, 8)
            pe.wait_ge(c_dve, 2)
            pe.wait_ge(L["small"], 64)
            for k in range(KD):
                pe.transpose(psum[:, 7, k * F1:(k + 1) * F1], gW1_sb[:, k * P:(k + 1) * P], ident[0:F1, 0:F1])
            pe.transpose(psum[0:F1, 7, 2 * F1:2 * F1 + F2], gW2_sb[:], ident[0:F2, 0:F2])
            for k in range(KD):
                last = pe.transpose(psum[0:F2, 7, 160 + k * P:160 + (k + 1) * P], gW3_sb[:, k, :], ident[:])
            last = pe.transpose(psum[:, 7, 416:416 + NX * KH], b1_rows[:], ident[0:NX * KH, 0:NX * KH])
            last.then_inc(c_pe, 1)
            pe.wait_ge(e_dve, 3)
            pe.matmul(psum[:, 6, 0:1], ones[0:T, :], inv[:, 2:3], start=True, stop=True)
            pe.matmul(psum[0:T, 6, P:P + T], key_f[:, 0:1].broadcast_to([T, T]), ident[0:T, 0:T],
                      start=True, stop=True).then_inc(e_pe, 1)

            pe.wait_ge(c_act, 4)
            for g in range(NG):
                for t in range(G):
                    pe.wait_ge(xn_ready, g * G + t + 1)
                    for k in range(KD):
                        last = pe.transpose(psum[:, t, k * T:(k + 1) * T], xn[:, g % 2, t, k * P:(k + 1) * P], ident[0:T, 0:T])
                    last.then_inc(xnT_psum, 1)
                if g == 1:
                    pe.wait_ge(e_dve, 4)
                for t in range(G):
                    pe.wait_ge(xnT_sb, g * G + t + 1)
                    for k in range(KD):
                        last = pe.matmul(psum[0:T, 5 + g % 2, t * F1:(t + 1) * F1], xnT[:, t, k, :], gW1T[:, k, :],
                                         start=(k == 0), stop=(k == KD - 1))
                last.then_inc(z_psum, 1)
                if g >= 1:
                    pe.wait_ge(zhi, g)
                if g == 0:
                    pe.wait_ge(e_dve, 5)
                    pe.matmul(psum[0:NG, 7, 0:T], start_f[:, 0:NG], ident[0:T, 0:T], start=True, stop=True)
                    pe.matmul(psum[0:NG, 7, T:T + 1], start_f[0:1, 1:NG + 1], ident[0:1, 0:1],
                              start=True, stop=True).then_inc(e_pe, 1)
                if g == 1:
                    pe.wait_ge(e_dve, 6)
                    pe.matmul(psum[0:1, 7, P:P + NG], largest_size[:], ident[0:NG, 0:NG],
                              start=True, stop=True).then_inc(e_pe, 1)
            pe.wait_ge(zhi, NG)
            pe.wait_ge(c_more, 7)
            for b in range(4):
                pe.matmul(psum[:, b, :], ones16[0:1, :], zeros16[:], start=True, stop=True).then_inc(applied, 1)
            for s_ in (applied, at_psum, win_psum):
                pe.matmul(psum[:, 5, :], ones16[0:1, :], zeros16[:], start=True, stop=True).then_inc(s_, 1)
            pe.wait_ge(rounds_ready, 1)
            pe.wait_ge(zsplit, NG)
            n_rounds = pe.value_load(rounds_i[0:1, 0:1], min_val=1, max_val=MAX_ROUNDS)
            with pe.Fori(0, n_rounds) as r:
                pe.wait_ge(key_rel, r + 1)
                pe.wait_ge(got_key, (r + 1) * 16 * NG)
                for a in range(2):
                    for g in range(NG):
                        last = pe.transpose(psum[:, 4 + 2 * a + g // 4, (g % 4) * T:(g % 4 + 1) * T], gath[:, g, :, a],
                                            ident[0:T, 0:T])
                        if g >= 3:
                            last.then_inc(keyT_psum, 1)
                pe.wait_ge(keyT_sb, (r + 1) * 4)

                def window(kt, par, c, early):
                    if c == 0:
                        pe.wait_ge(onehots, (r * NT + kt + 1) * 4)
                    if not early:
                        pe.wait_ge(win_sb, r * NT * NC + kt * NC + c - 1)
                    for q in range(c * WB, min((c + 1) * WB, NQ)):
                        last = pe.matmul(psum[:, 4 + (par + c) % 2, (q % WB) * WC:(q % WB + 1) * WC],
                                         oh_lo[:, par, :, q], oh_col[:, par, :, q], start=True, stop=True)
                    last.then_inc(win_psum, 1)

                def turn(kt, par, g, early):
                    if g == 0:
                        pe.wait_ge(win_sb, r * NT * NC + (kt + 1) * NC)
                    if not (early and g < 2):
                        pe.wait_ge(*at_count(r, kt if g >= 2 else kt - 1, (g - 2) % G))
                    bank = psum[0:T, 6 + (par + g) % 2, :].bitcast(BF16)
                    for h in range(G):
                        last = pe.transpose(bank[:, h * P:(h + 1) * P], cts[:, par, g * G + h, :], ident16[:])
                    last.then_inc(at_psum, 1)

                def apply(kt, g):
                    pe.wait_ge(*at_count(r, kt, g))
                    for h in range(G):
                        c = (g * G + h) * F1
                        for i in range(3):
                            last = pe.matmul(acc[:, c:c + F1], at[:, g, h * P:(h + 1) * P],
                                             z3[:, ds(kt, 1), i, :].rearrange("p a f -> p (a f)"),
                                             start=False, stop=True, skip_group_check=True)
                    last.then_inc(applied, 1)

                for c in range(NC):
                    window(0, 0, c, c < 2)

                def tile(kt, par):
                    for c in range(NC):
                        if 1 <= c <= G:
                            turn(kt - 1, 1 - par, c - 1, False)
                        window(kt, par, c, False)
                        if c >= 3:
                            apply(kt - 1, c - 3)
                    apply(kt - 1, G - 1)

                tiles_in_pairs(pe, tile)
                for g in range(G + 1):
                    if g < G:
                        turn(NT - 1, 0, g, False)
                    if g >= 1:
                        apply(NT - 1, g - 1)

            pe.wait_ge(L["few"], 32)

            def turn_y(g):
                pe.wait_ge(y_ready, g + 1)
                if g >= 1:
                    pe.wait_ge(h2_sb, 2 * g)
                for h, (t0, t1) in enumerate(halves):
                    for t in range(t0, t1):
                        last = pe.transpose(psum[0:F1, 4 + h, (t - t0) * T:(t - t0 + 1) * T], y1[:, g * G + t, :], ident[0:T, 0:T])
                    last.then_inc(yT_psum, 1)

            def second_layer(g):
                for h, (t0, t1) in enumerate(halves):
                    pe.wait_ge(yT_sb, g * 2 + h + 1)
                    pe.matmul(psum[0:F2, 4 + h, 0:(t1 - t0) * T], gW2T[:], y1T[:, t0:t1, :].rearrange("p t n -> p (t n)"),
                              start=True, stop=True).then_inc(h2_psum, 1)

            def third_layer(g):
                for i in range(len(H3)):
                    if g >= 1:
                        pe.wait_ge(h3_used, (g - 1) * len(H3) + i + 1)
                    for t in range(2 * i, min(2 * i + 2, G)):
                        pe.wait_ge(h2_sb, g * 2 + (1 if t < 3 else 2))
                        c = (t % 2) * D
                        last = pe.matmul(psum[0:T, H3[i], c:c + D], h2T[:, t, :], gW3T[:], start=True, stop=True)
                    last.then_inc(h3_psum, 1)

            def router_group(g):
                pe.wait_ge(*tok_ready(g))
                for t in range(G):
                    i = g * G + t
                    if i >= len(TURN):
                        pe.wait_ge(tokT_sb, i + 1 - len(TURN))
                    for k in range(KD):
                        last = pe.transpose(psum[:, TURN[i % len(TURN)], k * T:(k + 1) * T], tok[:, i, k * P:(k + 1) * P], ident[0:T, 0:T])
                    last.then_inc(tokT_psum, 1)
                if g >= 1:
                    turn_logits(g - 1)
                for h, (t0, t1) in enumerate(halves):
                    pe.wait_ge(tokT_sb, g * G + t1)
                    for k in range(KD):
                        last = pe.matmul(psum[0:NX, 4 + h, 0:(t1 - t0) * T], wr_sb[:, k, :],
                                         tokT[:, k, t0:t1, :].rearrange("p t n -> p (t n)"), start=(k == 0), stop=(k == KD - 1))
                    last.then_inc(logitT_psum, 1)

            def turn_logits(g):
                pe.wait_ge(logitT_sb, 2 * (g + 1))
                for t in range(G):
                    c = P + (g * G + t) * NX
                    last = pe.transpose(psum[0:T, 3, c:c + NX], logitT[:, t, :], ident[0:NX, 0:NX])
                last.then_inc(logit_psum, 1)

            turn_y(0)
            for k in range(NG + LAG):
                if k < NG:
                    second_layer(k)
                if k + 1 < NG:
                    turn_y(k + 1)
                if k == 0:
                    pe.wait_ge(y_ready, NG)
                if k < NG:
                    third_layer(k)
                if 0 <= k - LAG < NG:
                    router_group(k - LAG)
            turn_logits(NG - 1)

            pe.wait_ge(r_dve, 2)
            selv = sel[:].rearrange("p t e -> p (t e)")
            pe.matmul(psum[0:T, 4, 0:NT * NX], later[0:T, 0:T], selv, start=True, stop=True)
            pe.matmul(psum[:, 5, 0:NT * NX], ones16[0:T, :], selv, start=True, stop=True).then_inc(r_pe, 1)
            pe.matmul(psum[:, 6, 0:2 * NB], ones16[0:1, :], zeros16[:, 0:2 * NB], start=True, stop=True)
            for k in range(2):
                pe.wait_ge(pair_oh, k + 1)
                for t in range(NT):
                    last = pe.matmul(psum[:, 6, 0:2 * NB], oh_lane[:, k, :, t], oh_val[:, k, :, :, t].rearrange("p v b -> p (v b)"),
                                     start=False, stop=True, skip_group_check=True)
                last.then_inc(pair_mm, 1)

            pe.wait_ge(L["experts"], 48)
            pe.wait_ge(slots_ready, 1)

            def turn_x(b, j, i):
                pe.wait_ge(xg_in[j], 16 * (i + 1))
                if not (static(b) and b < 2):
                    pe.wait_ge(xgT_sb, b - 1)
                for k in range(KD):
                    last = pe.transpose(psum[:, 6 + j % 2, k * P:(k + 1) * P], xg[:, j, k * P:(k + 1) * P], ident[:])
                last.then_inc(xgT_psum, 1)

            def up_mm(b, j):
                pe.wait_ge(w1_copied, b + 1)
                pe.wait_ge(xgT_sb, b + 1)
                if not (static(b) and b < 2):
                    pe.wait_ge(up_sb, b - 1)
                for c in range(KH):
                    for k in range(KD):
                        last = pe.matmul(psum[:, j % 2, c * P:(c + 1) * P],
                                         w1_now[:, j % 2, k, c * P:(c + 1) * P],
                                         xgT[:, j % 2, k, :], start=(k == 0), stop=(k == KD - 1))
                last.then_inc(up_psum, 1)

            def down_mm(b, j):
                e = pe.value_load(ebi[0:1, ds(b, 1)], min_val=0, max_val=NX - 1)
                pe.wait_ge(gelu_sb, b + 1)
                if not (static(b) and b < 2):
                    pe.wait_ge(down_sb, b - 1)
                for k in range(KH):
                    last = pe.matmul(psum[:, 4 + j % 2, 0:D], hT[:, j % 2, k, :], w2_sb[:, ds(e, 1), k, :].rearrange("p a h -> p (a h)"),
                                     start=(k == 0), stop=(k == KH - 1))
                last.then_inc(down_psum, 1)

            turn_x(0, 0, 0)

            def expert_step(b, j, i, last):
                if not (last and j == 3):
                    turn_x(b + 1, (j + 1) % 4, i if j < 3 else i + 1)
                up_mm(b, j)
                if not (static(b) and b < 1):
                    down_mm(b - 1, (j - 1) % 4)

            middle = middle_quads(pe)
            all_blocks(pe, middle, expert_step)
            down_mm(4 * (middle + 2) + 3, 3)

        @block.vector
        def _(dve):
            done, settle, start, st = chain(dve, link_dve)

            def floor_of(out, in_, add, scale):
                done(dve.tensor_scalar(out, in_, add, scale, ALU.add, ALU.mult))
                settle()
                done(dve.tensor_scalar(out, out, 0.5, MAGIC, ALU.subtract, ALU.add))
                settle()
                done(dve.tensor_scalar(out, out, MAGIC, None, ALU.subtract))
                settle()

            dve.wait_ge(c_pool, 8)
            dve.tensor_scalar(ident[:], iota[:], part[:], None, ALU.is_equal).then_inc(c_dve, 1)
            dve.tensor_scalar(ident16[:], iota[:], part[:], None, ALU.is_equal).then_inc(c_dve, 1)
            dve.tensor_scalar(later[:], iota[:], part[:], None, ALU.is_gt).then_inc(c_dve, 1)
            done(dve.memset(inv[:], 0.0))
            dve.memset(cnt[:], 0.0).then_inc(at_dve, 1)

            dve.wait_ge(L["edges"], 32)
            dve.wait_ge(L["nextrow"], 16)
            done(dve.tensor_copy(edge_f[:, 1, :], edge_i[:, 1, :]))
            done(dve.tensor_copy(edge_f[:, 0, :], edge_i[:, 0, :]))
            done(dve.tensor_copy(next_f[0:T - 1, :], next_i[0:T - 1, :]))
            settle()
            floor_of(hi_f[:], edge_f[:, 1, :], 0.5, 1.0 / T)
            dve.scalar_tensor_tensor(key_f[:], edge_f[:, 0, :], float(NT), hi_f[:], ALU.mult, ALU.add).then_inc(e_dve, 1)
            done(dve.tensor_tensor(junk[0:T, 0:EC - 1], edge_f[:, 0, 0:EC - 1], edge_f[:, 0, 1:EC], ALU.is_gt))
            done(dve.scalar_tensor_tensor(kl_f[:, :, 1], hi_f[:], -float(T), edge_f[:, 1, :], ALU.mult, ALU.add))
            done(dve.tensor_tensor(inv[0:T - 1, 1:2], edge_f[0:T - 1, 0, EC - 1:EC], next_f[0:T - 1, :], ALU.is_gt))
            settle()
            done(dve.tensor_reduce(inv[:, 0:1], junk[0:T, 0:EC - 1], AX.X, ALU.add))
            dve.wait_ge(e_dve, 1)
            dve.tensor_copy(kl_f[:, :, 0], key_f[:]).then_inc(e_dve, 1)
            settle()
            dve.tensor_tensor(inv[:, 2:3], inv[:, 0:1], inv[:, 1:2], ALU.add).then_inc(e_dve, 1)

            def moments(g):
                dve.wait_ge(x_in[g], 32)
                for t in range(g * G, (g + 1) * G):
                    done(dve.bn_stats(stats[:, t, :], res[:, t, :]))
                settle()
                for t in range(g * G, (g + 1) * G):
                    last = dve.bn_aggr(mv[:, t, :], stats[:, t, :])
                last.then_inc(var_ready, 1)

            def normalise(g):
                dve.wait_ge(std_ready, g + 1)
                if g >= 2:
                    dve.wait_ge(xnT_psum, (g - 1) * G)
                    dve.wait_ge(res_ready, g - 1)
                done(dve.reciprocal(rstd[:, g * G:(g + 1) * G], std[:, g * G:(g + 1) * G]))
                settle()
                for i, t in enumerate(range(g * G, (g + 1) * G)):
                    dve.tensor_scalar(xn[:, g % 2, i, :], res[:, t, :], mv[:, t, 0:1], rstd[:, t:t + 1],
                                      ALU.subtract, ALU.mult).then_inc(xn_ready, 1)

            dve.wait_ge(e_pe, 1)
            done(dve.tensor_scalar(flag[:, 0:1], psum[:, 6, 0:1], 1.0, None, ALU.min))
            settle()
            done(dve.tensor_scalar(flag[:, 1:2], flag[:, 0:1], -1.0, 1.0, ALU.mult, ALU.add))
            for g in range(NG):
                done(dve.tensor_scalar(rows[:, g, 0:T], psum[0:T, 6, P:P + T], thr[:, g:g + 1], None,
                                       ALU.is_lt, ALU.add, accum_out=cnt[:, 0, g:g + 1]))
            settle()
            done(dve.tensor_scalar(cnt[:, 1, :], cnt[:, 0, :], -1.0, 0.0, ALU.add, ALU.max))
            settle()
            dve.tensor_copy(row_i[:], cnt[:, 1, :]).then_inc(e_dve, 1)
            moments(0)
            moments(1)
            normalise(0)
            moments(2)
            dve.wait_ge(row_got, 16 * NG)
            for g in range(NG):
                done(dve.tensor_scalar(junk[:], rows[:, g, :], thr[:, g:g + 1], None,
                                       ALU.is_lt, ALU.add, accum_out=cnt[:, 2, g:g + 1]))
                settle()
            done(dve.scalar_tensor_tensor(cnt[:, 3, :], cnt[:, 1, :], float(EC), cnt[:, 2, :], ALU.mult, ALU.add))
            settle()
            dve.tensor_scalar(start_f[:, 0:NG], cnt[:, 3, :], flag[0:T, 1:2], None, ALU.mult).then_inc(e_dve, 1)
            dve.wait_ge(e_dve, 5)
            dve.tensor_copy(start_i[:], start_f[:, 0:NG]).then_inc(idx_ready, 1)
            normalise(1)
            dve.wait_ge(e_pe, 2)
            done(dve.tensor_copy(start_row[:], psum[0:NG, 7, 0:T + 1]))
            settle()
            done(dve.tensor_tensor(size_row[:], start_row[:, 1:T + 1], start_row[:, 0:T], ALU.subtract))
            settle()
            dve.tensor_reduce(largest_size[:], size_row[:], AX.X, ALU.max).then_inc(e_dve, 1)

            def rest_of_hi(g):
                grp = slice(g * G, (g + 1) * G)
                dve.wait_ge(zhi, g + 1)
                dve.tensor_tensor(zres[:, grp, :], z[:, grp, :], z3[:, grp, 0, :], ALU.subtract).then_inc(zrest, 1)

            def rest_of_mid(g):
                grp = slice(g * G, (g + 1) * G)
                dve.wait_ge(zmid, g + 1)
                dve.tensor_tensor(z3[:, grp, 2, :], zres[:, grp, :], z3[:, grp, 1, :], ALU.subtract).then_inc(zsplit, 1)

            moments(3)
            normalise(2)
            rest_of_hi(0)
            dve.wait_ge(e_pe, 3)
            done(dve.tensor_reduce(rounds_f[:, 0:1], psum[0:1, 7, P:P + NG], AX.X, ALU.max))
            settle()
            done(dve.tensor_scalar(rounds_f[:, 1:2], rounds_f[:, 0:1], flag[0:1, 1:2], None, ALU.mult))
            settle()
            done(dve.scalar_tensor_tensor(rounds_f[:, 0:1], flag[0:1, 0:1], float(E), rounds_f[:, 1:2], ALU.mult, ALU.add))
            settle()
            floor_of(rounds_f[:, 2:3], rounds_f[:, 0:1], CH - 0.5, 1.0 / CH)
            done(dve.tensor_scalar(rounds_f[:, 1:2], rounds_f[:, 2:3], 1.0, None, ALU.max))
            settle()
            dve.tensor_copy(rounds_i[:], rounds_f[:, 1:2]).then_inc(rounds_ready, 1)
            moments(4)
            normalise(3)
            rest_of_hi(1)
            rest_of_mid(0)
            normalise(4)
            for g in range(2, NG):
                rest_of_hi(g)
                rest_of_mid(g - 1)
            rest_of_mid(NG - 1)
            dve.wait_ge(c_more, 7)
            dve.wait_ge(rounds_ready, 1)
            n_rounds = dve.value_load(rounds_i[0:1, 0:1], min_val=1, max_val=MAX_ROUNDS)

            done, settle, start, st = chain(dve, link_round)
            with dve.Fori(0, n_rounds) as r:
                start(r)
                dve.wait_ge(got_key, (r + 1) * 16 * NG)
                dve.tensor_tensor(gath[:, :, :, 0], gath[:, :, :, 0], thr[:].unsqueeze(2).broadcast_to([T, NG, CH]),
                                  ALU.subtract).then_inc(key_rel, 1)
                done(dve.tensor_scalar(start_f[:, 0:NG], start_f[:, 0:NG], float(CH), float(E), ALU.add, ALU.min))
                settle()
                dve.tensor_copy(start_i[:], start_f[:, 0:NG]).then_inc(idx_ready, 1)
                for a in range(2):
                    for i, (w0, w1) in enumerate(((0, 4 * T), (4 * T, NW))):
                        dve.wait_ge(keyT_psum, r * 4 + 2 * a + i + 1)
                        dve.tensor_copy(keyT[:, a, w0:w1], psum[:, 4 + 2 * a + i, 0:w1 - w0]).then_inc(keyT_sb, 1)
                dve.wait_ge(keyT_sb, (r + 1) * 4)

                def onehot(kt, par, i):
                    to, a = (oh_lo, 1) if i < 2 else (oh_col, 0)
                    n0, n1 = ((0, P // 2), (P // 2, P), (0, P // 2), (P // 2, WC))[i]
                    dve.tensor_tensor(to[:, par, n0:n1, :], count_up[:, n0:n1, :],
                                      keyT[:, a, ds(kt * NQ, NQ)].unsqueeze(1).broadcast_to([P, n1 - n0, NQ]),
                                      ALU.is_equal).then_inc(onehots, 1)

                def copy_at(kt, par, g):
                    dve.wait_ge(at_psum, 1 + r * NT * G + kt * G + g + 1)
                    dve.wait_ge(applied, SET + r * NT * G + (kt - 1) * G + g + 1)
                    dve.tensor_copy(at[:, g, :], psum[0:T, 6 + (par + g) % 2, :].bitcast(BF16)[:, 0:G * P]).then_inc(at_dve, 1)

                for kt in range(2):
                    for i in range(4):
                        onehot(kt, kt, i)

                def tile(kt, par):
                    dve.wait_ge(win_psum, 1 + r * NT * NC + kt * NC)
                    for i in range(4):
                        onehot(kt + 1, 1 - par, i)
                        for g in ((0,), (2,), (), (4,))[i]:
                            copy_at(kt - 1, 1 - par, g)

                with dve.Fori(0, (NT - 1) // 2 - 1) as i:
                    tile(2 * i + 1, 1)
                    tile(2 * i + 2, 0)
                tile(NT - 2, 1)
                for kt, par in ((NT - 2, 1), (NT - 1, 0)):
                    for g in AT_DVE:
                        copy_at(kt, par, g)
                dve.wait_ge(win_psum, 1 + (r + 1) * NT * NC)
                dve.wait_ge(applied, SET + (r + 1) * NT * G)
                assert st["n"] == 1, st["n"]

            dve.wait_ge(got_key, (n_rounds + 1) * 16 * NG)
            done, settle, start, st = chain(dve, link_late)
            dve.wait_ge(L["few"], 32)
            dve.wait_ge(res_ready, NG)

            def y_group(g):
                dve.scalar_tensor_tensor(y1[:, g * G:(g + 1) * G, :].rearrange("p t f -> p (t f)"),
                                         z[:, g * G:(g + 1) * G, :].rearrange("p t f -> p (t f)"), w_sb[0:T, :],
                                         acc[0:T, g * G * F1:(g + 1) * G * F1], ALU.mult, ALU.add).then_inc(y_ready, 1)

            def residual_group(g):
                for i in range(len(H3)):
                    dve.wait_ge(h3_psum, g * len(H3) + i + 1)
                    for t in range(2 * i, min(2 * i + 2, G)):
                        c = (t % 2) * D
                        last = dve.scalar_tensor_tensor(res[:, g * G + t, :], psum[0:T, H3[i], c:c + D], 0.0,
                                                        res[:, g * G + t, :], ALU.max, ALU.add)
                    last.then_inc(h3_used, 1)
                dve.wait_ge(h3_used, (g + 1) * len(H3))

            def moments2(g):
                for t in range(g * G, (g + 1) * G):
                    done(dve.bn_stats(stats2[:, t, :], res[:, t, :]))
                settle()
                for t in range(g * G, (g + 1) * G):
                    last = dve.bn_aggr(mv2[:, t, :], stats2[:, t, :])
                last.then_inc(tok_var, 1)

            def normalise2(g):
                dve.wait_ge(tok_std, g + 1)
                done(dve.reciprocal(rstd2[:, g * G:(g + 1) * G], std_2[:, g * G:(g + 1) * G]))
                settle()
                for t in range(g * G, (g + 1) * G):
                    last = dve.tensor_scalar(tok[:, t, :], res[:, t, :], mv2[:, t, 0:1], rstd2[:, t:t + 1],
                                             ALU.subtract, ALU.mult)
                last.then_inc(tok_norm, 1)

            def affine(g):
                t_ = tok[:, g * G:(g + 1) * G, :]
                dve.wait_ge(L["bcast"], 48)
                dve.wait_ge(tok_norm, g + 1)
                done(dve.tensor_tensor(t_, t_, gam[:].unsqueeze(1).broadcast_to([T, G, D]), ALU.mult))
                settle()
                dve.tensor_tensor(t_, t_, bet[:].unsqueeze(1).broadcast_to([T, G, D]), ALU.add).then_inc(tok_dve, 1)

            for g in range(NG):
                y_group(g)
            for k in range(NG + 1):
                if k < NG:
                    residual_group(k)
                    moments2(k)
                if k >= 1:
                    normalise2(k - 1)
                    if k - 1 >= AFFINE_POOL:
                        affine(k - 1)
            dve.wait_ge(logit_psum, NG)
            dve.tensor_tensor(logit[:], psum[0:T, 3, P:P + NT * NX].rearrange("p (t e) -> p t e", e=NX),
                              br_sb[:].unsqueeze(1).broadcast_to([T, NT, NX]), ALU.add).then_inc(logit_sb, 1)
            dve.wait_ge(logit_sb, 1)

            def over_experts(v):
                return v.unsqueeze(2).broadcast_to([T, NT, NX])

            def largest(k, v, m, a):
                done(dve.tensor_reduce(m, v, AX.X, ALU.max))
                settle()
                done(dve.tensor_tensor(rt[0][:], v, over_experts(m), ALU.is_equal))
                settle()
                done(dve.tensor_tensor(rt[1][:], rt[0][:], ex_m8[:], ALU.mult))
                settle()
                done(dve.tensor_reduce(a, rt[1][:], AX.X, ALU.min))
                settle()
                done(dve.tensor_tensor(mask[:, k, :, :], ex_m8[:], over_experts(a), ALU.is_equal))
                settle()

            largest(0, logit[:], top[:, 0, :], top[:, 1, :])
            done(dve.scalar_tensor_tensor(rt[2][:].rearrange("p t e -> p (t e)"), mask[:, 0, :, :].rearrange("p t e -> p (t e)"),
                                          -BIG, logit[:].rearrange("p t e -> p (t e)"), ALU.mult, ALU.add))
            settle()
            largest(1, rt[2][:], top[:, 2, :], top[:, 1, :])
            dve.tensor_tensor(top[:, 3, :], top[:, 2, :], top[:, 0, :], ALU.subtract).then_inc(r_dve, 1)
            dve.tensor_tensor(sel[:], mask[:, 0, :, :], mask[:, 1, :, :], ALU.add).then_inc(r_dve, 1)
            dve.wait_ge(r_act, 1)
            done(dve.tensor_scalar(top[:, 0, :], top[:, 3, :], 1.0, None, ALU.add))
            settle()
            done(dve.reciprocal(wgt[:, :, 0], top[:, 0, :]))
            settle()
            done(dve.tensor_tensor(wgt[:, :, 1], wgt[:, :, 0], top[:, 3, :], ALU.mult))
            dve.wait_ge(r_pe, 1)
            total = psum[:, 5, 0:NT * NX].rearrange("p (t e) -> p t e", e=NX)
            for e in range(NX):
                done(dve.tensor_tensor_scan(tot[:, e, :], ones[:, 0:NT], total[:, :, e], 0.0, ALU.mult, ALU.add))
            settle()
            floor_of(blk[:, 0, :], tot[:, :, NT - 1], P - 0.5, 1.0 / P)
            done(dve.tensor_tensor_scan(blk[:, 1, :], ones[:, 0:NX], blk[:, 0, :], 0.0, ALU.mult, ALU.add))
            settle()
            done(dve.tensor_tensor(blk[:, 2, :], blk[:, 1, :], blk[:, 0, :], ALU.subtract))
            settle()
            done(dve.tensor_scalar(blk[:, 3, :], blk[:, 2, :], float(P), None, ALU.mult))
            done(dve.tensor_tensor(rt[3][:], psum[0:T, 4, 0:NT * NX].rearrange("p (t e) -> p t e", e=NX),
                                   tot[0:T, :, :].rearrange("p e t -> p t e"), ALU.add))
            settle()
            done(dve.tensor_tensor(rt[2][:], rt[3][:], total[0:T], ALU.subtract))
            settle()
            done(dve.tensor_tensor(rt[3][:], rt[2][:], blk[0:T, 3, :].unsqueeze(1).broadcast_to([T, NT, NX]), ALU.add))
            settle()
            for k in range(2):
                done(dve.tensor_tensor(rt[k][:], mask[:, k, :, :], rt[3][:], ALU.mult))
                settle()
                done(dve.tensor_reduce(pos[:, k, :], rt[k][:], AX.X, ALU.add))
                done(dve.tensor_scalar(pair_no[:, k:k + 1], part[0:T, :], 2.0, float(k), ALU.mult, ALU.add))
            settle()
            floor_of(pblk[:], pos[:], 0.5, 1.0 / P)
            done(dve.tensor_copy(pblk16[:], pblk[:]))
            done(dve.tensor_copy(tile16[:], tile1[:]))
            for k in range(2):
                done(dve.tensor_scalar(pairno16[:, k, :], ones[0:T, 0:NT], pair_no[:, k:k + 1], None, ALU.mult))
            done(dve.scalar_tensor_tensor(plane16[:].rearrange("p k t -> p (k t)"), pblk[:].rearrange("p k t -> p (k t)"),
                                          -float(P), pos[:].rearrange("p k t -> p (k t)"), ALU.mult, ALU.add))
            settle()
            for k in range(2):
                def over(v, n):
                    return v.unsqueeze(1).broadcast_to([T, n, NT])

                done(dve.tensor_tensor(oh_lane[:, k, :, :], count_up[0:T, :, :], over(plane16[:, k, :], P), ALU.is_equal))
                done(dve.tensor_tensor(oh_blk[:, k, :, :], count_up[0:T, 0:NB, :], over(pblk16[:, k, :], NB), ALU.is_equal))
                settle()
                done(dve.tensor_tensor(oh_val[:, k, 0, :, :], oh_blk[:, k, :, :], over(tile16[:], NB), ALU.mult))
                dve.tensor_tensor(oh_val[:, k, 1, :, :], oh_blk[:, k, :, :], over(pairno16[:, k, :], NB),
                                  ALU.mult).then_inc(pair_oh, 1)
            done(dve.tensor_tensor(ebt[:], iota[0:1, 0:NB].unsqueeze(2).broadcast_to([1, NB, NX]),
                                   blk[0:1, 1, :].unsqueeze(1).broadcast_to([1, NB, NX]), ALU.is_ge))
            settle()
            done(dve.tensor_reduce(ebf[:], ebt[:], AX.X, ALU.add))
            floor_of(quads_f[:], blk[0:1, 1, NX - 1:NX], 3.5, 0.25)
            done(dve.tensor_scalar(quads_i[:], quads_f[:], -3.0, None, ALU.add))
            settle()
            done(dve.tensor_scalar(ebi[:], ebf[:], float(NX - 1), None, ALU.min))
            settle()
            dve.wait_ge(pair_mm, 2)
            done(dve.tensor_copy(slot[:, 0, :], psum[:, 6, 0:NB]))
            done(dve.tensor_copy(slot[:, 1, :], psum[:, 6, NB:2 * NB]))
            settle()
            floor_of(slot[:, 2, :], slot[:, 1, :], 0.5, 0.5)
            done(dve.scalar_tensor_tensor(slot[:, 3, :], slot[:, 0, :], float(T), slot[:, 2, :], ALU.mult, ALU.add))
            done(dve.scalar_tensor_tensor(slot[:, 4, :], slot[:, 0, :], float(2 * T), slot[:, 1, :], ALU.mult, ALU.add))
            settle()
            done(dve.tensor_scalar(gidx[:], slot[:, 3, :], -float(T), 0.0, ALU.add, ALU.max))
            done(dve.tensor_scalar(slot[:, 5, :], slot[:, 0, :], 0.0, None, ALU.is_equal))
            done(dve.tensor_scalar(spare_row[:], part[:], float(2 * N + 2 * T), None, ALU.add))
            settle()
            done(dve.tensor_scalar(slot[:, 2, :], iota[:, 0:NB], float(P), spare_row[:], ALU.mult, ALU.add))
            settle()
            done(dve.tensor_tensor(slot[:, 3, :], slot[:, 5, :], slot[:, 2, :], ALU.mult))
            settle()
            done(dve.scalar_tensor_tensor(sidx[:], slot[:, 4, :], -float(2 * T), slot[:, 3, :], ALU.add, ALU.add))
            settle()
            dve.engine_nop().then_inc(slots_ready, 1)

            dve.wait_ge(L["experts"], 48)

            def copy_x(b, j):
                dve.wait_ge(xgT_psum, b + 1)
                if not (static(b) and b < 2):
                    dve.wait_ge(up_psum, b - 1)
                dve.tensor_copy(xgT[:, j % 2, :, :].rearrange("p k n -> p (k n)"), psum[:, 6 + j % 2, 0:D]).then_inc(xgT_sb, 1)

            def add_b1(b, j):
                e = dve.value_load(ebi[0:1, ds(b, 1)], min_val=0, max_val=NX - 1)
                dve.wait_ge(up_psum, b + 1)
                if not (static(b) and b < 2):
                    dve.wait_ge(gelu_sb, b - 1)
                dve.tensor_tensor(up[:, j % 2, :, :], psum[:, j % 2, :].rearrange("p (c n) -> p c n", n=P),
                                  b1T[:, ds(e, 1), :].rearrange("p a c -> p (a c)").unsqueeze(2).broadcast_to([P, KH, P]),
                                  ALU.add).then_inc(up_sb, 1)

            def add_b2(b, j, i):
                e = dve.value_load(ebi[0:1, ds(b, 1)], min_val=0, max_val=NX - 1)
                dve.wait_ge(down_psum, b + 1)
                if not (static(b) and b < 4):
                    dve.wait_ge(scattered[j], 16 * i)
                dve.tensor_tensor(yb[:, j, :], psum[:, 4 + j % 2, 0:D], b2_sb[:, ds(e, 1), :].rearrange("p a h -> p (a h)"),
                                  ALU.add).then_inc(down_sb, 1)

            def expert_step(b, j, i, last):
                if not (last and j == 3):
                    copy_x(b + 1, (j + 1) % 4)
                add_b1(b, j)
                if not (static(b) and b < 1):
                    add_b2(b - 1, (j - 1) % 4, i if j >= 1 else i - 1)

            copy_x(0, 0)
            middle = middle_quads(dve)
            all_blocks(dve, middle, expert_step)
            add_b2(4 * (middle + 2) + 3, 3, middle + 2)

            for g in range(NG):
                dve.wait_ge(fin_in[g], 32)
                for k in range(2):
                    for i in range(G):
                        t = g * G + i
                        last = dve.scalar_tensor_tensor(res[:, t, :], fin(g)[:, i, k * D:(k + 1) * D], wgt[:, t, k:k + 1],
                                                        res[:, t, :], ALU.mult, ALU.add)
                    last.then_inc((fin_half, fin_done)[k], 1)
                    if k == 0:
                        dve.wait_ge(fin_half, g + 1)


_INS = ['x', 'src', 'dst', 'L0_gnn_w', 'L0_gnn_W1', 'L0_gnn_W2', 'L0_gnn_W3', 'L0_ffn_gamma', 'L0_ffn_beta',
        'L0_ffn_Wr', 'L0_ffn_br', 'L0_ffn_W1', 'L0_ffn_b1', 'L0_ffn_W2', 'L0_ffn_b2']
_OUTS = [((N, D), 'float32')]


def kernel(**inputs):
    import numpy as _np
    import concourse.bacc as _bacc
    from concourse import mybir as _mybir
    from concourse.bass_utils import run_bass_kernel_spmd as _run

    nc = _bacc.Bacc("TRN2", target_bir_lowering=False, num_devices=1)
    arrays, args = {}, []
    for name in _INS:
        a = _np.ascontiguousarray(inputs[name])
        arrays[f"in_{name}_dram"] = a
        args.append(nc.dram_tensor(f"in_{name}_dram", a.shape, _mybir.dt.from_np(a.dtype), kind="ExternalInput").ap())
    for i, (shape, dtype) in enumerate(_OUTS):
        dt = _mybir.dt.from_np(_np.dtype(dtype))
        args.append(nc.dram_tensor(f"out_{i}_dram", shape, dt, kind="ExternalOutput").ap())
    build(nc, *args)
    r = _run(nc, [arrays], core_ids=[0])
    return r.results[0]["out_0_dram"]
```
